# Optimizing a Trainium2 kernel written in Bass

```python
import numpy as np
import jax
import jax.numpy as jnp

def _softmax(x, axis=-1):
    return jax.nn.softmax(x, axis=axis)

def _gelu(x):
    return jax.nn.gelu(x, approximate=True)

def _silu(x):
    return jax.nn.silu(x)

def _sigmoid(x):
    return jax.nn.sigmoid(x)

def _layernorm(x, axis=-1, eps=1e-05):
    m = jnp.mean(x, axis=axis, keepdims=True)
    v = jnp.var(x, axis=axis, keepdims=True)
    return (x - m) / jnp.sqrt(v + eps)

def _scatter_add(tgt, idx, src, axis=0):
    return tgt.at[idx].add(src)

def _segment_sum(src, seg, n):
    return jax.ops.segment_sum(src, seg, n)
kernel_name = 'mk_seq_preln_d1_jaxref_r4_5041c6'

def setup_inputs(seed: int=0):
    np.random.seed(seed)
    _w = jnp.asarray

    def _L0_attn_setup():
        import jax, jax.numpy as jnp
        import numpy as np

        def _rotate_every_two(x):
            x1 = x[..., ::2]
            x2 = x[..., 1::2]
            return jnp.stack((-x2, x1), axis=-1).reshape(x.shape)
        key = jax.random.key(seed)
        ks = jax.random.split(key, 6)
        B, S, D = (2, 512, 256)
        w = lambda k, shape: jax.random.normal(k, shape, dtype=jnp.float32) * 0.02
        return {'x': jax.random.normal(ks[0], (B, S, D), dtype=jnp.float32), 'Wq': w(ks[1], (D, D)), 'bq': jnp.zeros((D,), jnp.float32), 'Wk': w(ks[2], (D, D)), 'bk': jnp.zeros((D,), jnp.float32), 'Wv': w(ks[3], (D, 2 * D)), 'bv': jnp.zeros((2 * D,), jnp.float32), 'Wg': w(ks[4], (D, 2 * D)), 'bg': jnp.zeros((2 * D,), jnp.float32), 'Wo': w(ks[5], (2 * D, D)), 'bo': jnp.zeros((D,), jnp.float32)}
    _L0_attn_in = _L0_attn_setup()

    def _L0_ffn_setup():
        import jax, jax.numpy as jnp
        import numpy as np
        DIM = 256
        E = 16
        TOPK = 2
        G = 4
        TOPK_G = 2
        INTER = 128
        N_SHARED = 2
        ROUTE_SCALE = 1.0

        def _gate(xf, gate_w, gate_b):
            scores = xf @ gate_w.T
            scores = jax.nn.softmax(scores.astype(jnp.float32), axis=-1)
            orig = scores
            scores = scores + gate_b
            T = xf.shape[0]
            sg = scores.reshape(T, G, E // G)
            group_scores = jax.lax.top_k(sg, 2)[0].sum(-1)
            _, gidx = jax.lax.top_k(group_scores, TOPK_G)
            keep = jax.nn.one_hot(gidx, G).sum(axis=1) > 0
            sg = jnp.where(keep[:, :, None], sg, -jnp.inf)
            scores = sg.reshape(T, E)
            _, idx = jax.lax.top_k(scores, TOPK)
            weights = jnp.take_along_axis(orig, idx, axis=1)
            weights = (weights * ROUTE_SCALE).astype(xf.dtype)
            return (weights, idx)
        key = jax.random.key(seed)
        ks = jax.random.split(key, 16)
        s = lambda fan_in: 1.0 / np.sqrt(fan_in)
        inp = {'x': jax.random.normal(ks[0], (4, 256, DIM), dtype=jnp.float32), 'gate_w': jax.random.normal(ks[1], (E, DIM), dtype=jnp.float32) * s(DIM), 'gate_b': jnp.zeros((E,), dtype=jnp.float32), 'We1': jax.random.normal(ks[2], (E, DIM, INTER), dtype=jnp.float32) * s(DIM), 'be1': jnp.zeros((E, INTER), dtype=jnp.float32), 'We2': jax.random.normal(ks[3], (E, INTER, DIM), dtype=jnp.float32) * s(INTER), 'be2': jnp.zeros((E, DIM), dtype=jnp.float32), 'We3': jax.random.normal(ks[4], (E, DIM, INTER), dtype=jnp.float32) * s(DIM), 'be3': jnp.zeros((E, INTER), dtype=jnp.float32), 'ws1': jax.random.normal(ks[5], (DIM, N_SHARED * INTER), dtype=jnp.float32) * s(DIM), 'bs1': jnp.zeros((N_SHARED * INTER,), dtype=jnp.float32), 'ws2': jax.random.normal(ks[6], (N_SHARED * INTER, DIM), dtype=jnp.float32) * s(N_SHARED * INTER), 'bs2': jnp.zeros((DIM,), dtype=jnp.float32), 'ws3': jax.random.normal(ks[7], (DIM, N_SHARED * INTER), dtype=jnp.float32) * s(DIM), 'bs3': jnp.zeros((N_SHARED * INTER,), dtype=jnp.float32)}
        return inp
    _L0_ffn_in = _L0_ffn_setup()
    _d = {'L0_attn_x': _L0_attn_in['x'], 'L0_attn_Wq': _L0_attn_in['Wq'], 'L0_attn_bq': _L0_attn_in['bq'], 'L0_attn_Wk': _L0_attn_in['Wk'], 'L0_attn_bk': _L0_attn_in['bk'], 'L0_attn_Wv': _L0_attn_in['Wv'], 'L0_attn_bv': _L0_attn_in['bv'], 'L0_attn_Wg': _L0_attn_in['Wg'], 'L0_attn_bg': _L0_attn_in['bg'], 'L0_attn_Wo': _L0_attn_in['Wo'], 'L0_attn_bo': _L0_attn_in['bo'], 'L0_ffn_gate_w': _L0_ffn_in['gate_w'], 'L0_ffn_gate_b': _L0_ffn_in['gate_b'], 'L0_ffn_We1': _L0_ffn_in['We1'], 'L0_ffn_be1': _L0_ffn_in['be1'], 'L0_ffn_We2': _L0_ffn_in['We2'], 'L0_ffn_be2': _L0_ffn_in['be2'], 'L0_ffn_We3': _L0_ffn_in['We3'], 'L0_ffn_be3': _L0_ffn_in['be3'], 'L0_ffn_ws1': _L0_ffn_in['ws1'], 'L0_ffn_bs1': _L0_ffn_in['bs1'], 'L0_ffn_ws2': _L0_ffn_in['ws2'], 'L0_ffn_bs2': _L0_ffn_in['bs2'], 'L0_ffn_ws3': _L0_ffn_in['ws3'], 'L0_ffn_bs3': _L0_ffn_in['bs3']}
    _x0 = _d['L0_attn_x']
    _d['L0_attn_x'] = jax.random.normal(jax.random.fold_in(jax.random.key(seed), 1), (8, 1024, 256), dtype=_x0.dtype)
    del _x0
    return _d

def reference(L0_attn_x, L0_attn_Wq, L0_attn_bq, L0_attn_Wk, L0_attn_bk, L0_attn_Wv, L0_attn_bv, L0_attn_Wg, L0_attn_bg, L0_attn_Wo, L0_attn_bo, L0_ffn_gate_w, L0_ffn_gate_b, L0_ffn_We1, L0_ffn_be1, L0_ffn_We2, L0_ffn_be2, L0_ffn_We3, L0_ffn_be3, L0_ffn_ws1, L0_ffn_bs1, L0_ffn_ws2, L0_ffn_bs2, L0_ffn_ws3, L0_ffn_bs3):

    def _L0_attn_ref(x, Wq, bq, Wk, bk, Wv, bv, Wg, bg, Wo, bo):
        import jax, jax.numpy as jnp
        import numpy as np

        def _rotate_every_two(x):
            x1 = x[..., ::2]
            x2 = x[..., 1::2]
            return jnp.stack((-x2, x1), axis=-1).reshape(x.shape)
        B, S, D = x.shape
        H = 16
        key_dim = D // H
        head_dim = 2 * D // H
        scaling = key_dim ** (-0.5)
        angle = 1.0 / 10000.0 ** jnp.linspace(0.0, 1.0, key_dim // 2)
        angle = jnp.repeat(angle, 2).astype(jnp.float32)
        decay = jnp.log(1.0 - 2.0 ** (-5.0 - jnp.arange(H, dtype=jnp.float32)))
        idx = jnp.arange(S, dtype=jnp.float32)
        sin = jnp.sin(idx[:, None] * angle[None, :])
        cos = jnp.cos(idx[:, None] * angle[None, :])
        diff = idx[:, None] - idx[None, :]
        mask = jnp.where(diff >= 0, jnp.exp(decay[:, None, None] * diff), 0.0)
        mask = mask / jnp.sqrt(mask.sum(-1, keepdims=True))
        q = (x @ Wq + bq).reshape(B, S, H, key_dim).transpose(0, 2, 1, 3)
        k = ((x @ Wk + bk) * scaling).reshape(B, S, H, key_dim).transpose(0, 2, 1, 3)
        v = x @ Wv + bv
        g = x @ Wg + bg
        qr = q * cos + _rotate_every_two(q) * sin
        kr = k * cos + _rotate_every_two(k) * sin
        vr = v.reshape(B, S, H, head_dim).transpose(0, 2, 1, 3)
        qk = jnp.einsum('bhsd,bhtd->bhst', qr, kr) * mask
        denom = jnp.clip(jnp.abs(jax.lax.stop_gradient(qk).sum(-1, keepdims=True)), 1.0, None)
        qk = qk / denom
        out = jnp.einsum('bhst,bhtd->bhsd', qk, vr).transpose(0, 2, 1, 3)
        mu = out.mean(-1, keepdims=True)
        var = ((out - mu) ** 2).mean(-1, keepdims=True)
        out = (out - mu) / jnp.sqrt(var + 1e-05)
        out = out.reshape(B, S, H * head_dim)
        out = jax.nn.silu(g) * out
        return out @ Wo + bo

    def _L0_ffn_ref(x, gate_w, gate_b, We1, be1, We2, be2, We3, be3, ws1, bs1, ws2, bs2, ws3, bs3):
        import jax, jax.numpy as jnp
        import numpy as np
        DIM = 256
        E = 16
        TOPK = 2
        G = 4
        TOPK_G = 2
        INTER = 128
        N_SHARED = 2
        ROUTE_SCALE = 1.0

        def _gate(xf, gate_w, gate_b):
            scores = xf @ gate_w.T
            scores = jax.nn.softmax(scores.astype(jnp.float32), axis=-1)
            orig = scores
            scores = scores + gate_b
            T = xf.shape[0]
            sg = scores.reshape(T, G, E // G)
            group_scores = jax.lax.top_k(sg, 2)[0].sum(-1)
            _, gidx = jax.lax.top_k(group_scores, TOPK_G)
            keep = jax.nn.one_hot(gidx, G).sum(axis=1) > 0
            sg = jnp.where(keep[:, :, None], sg, -jnp.inf)
            scores = sg.reshape(T, E)
            _, idx = jax.lax.top_k(scores, TOPK)
            weights = jnp.take_along_axis(orig, idx, axis=1)
            weights = (weights * ROUTE_SCALE).astype(xf.dtype)
            return (weights, idx)
        shape = x.shape
        xf = x.reshape(-1, DIM)
        weights, idx = _gate(xf, gate_w, gate_b)
        combine = (jax.nn.one_hot(idx, E, dtype=xf.dtype) * weights[..., None]).sum(1)
        h1 = jnp.einsum('td,edi->tei', xf, We1) + be1
        h3 = jnp.einsum('td,edi->tei', xf, We3) + be3
        h = jax.nn.silu(h1) * h3
        yo = jnp.einsum('tei,eid->ted', h, We2) + be2
        y = jnp.einsum('te,ted->td', combine, yo)
        z = jax.nn.silu(xf @ ws1 + bs1) * (xf @ ws3 + bs3) @ ws2 + bs2
        return (y + z).reshape(shape)
    x = L0_attn_x
    x = x + _L0_attn_ref(_layernorm(x, axis=-1), L0_attn_Wq, L0_attn_bq, L0_attn_Wk, L0_attn_bk, L0_attn_Wv, L0_attn_bv, L0_attn_Wg, L0_attn_bg, L0_attn_Wo, L0_attn_bo)
    x = x + _L0_ffn_ref(_layernorm(x, axis=-1), L0_ffn_gate_w, L0_ffn_gate_b, L0_ffn_We1, L0_ffn_be1, L0_ffn_We2, L0_ffn_be2, L0_ffn_We3, L0_ffn_be3, L0_ffn_ws1, L0_ffn_bs1, L0_ffn_ws2, L0_ffn_bs2, L0_ffn_ws3, L0_ffn_bs3)
    return x

_drawn_inputs = setup_inputs


def setup_inputs(seed=0):
    import zlib

    import numpy as np

    out = dict(_drawn_inputs(seed))
    spreads = {'L0_attn_bq': (0.0, 0.1),
     'L0_attn_bk': (0.0, 0.1),
     'L0_attn_bv': (0.0, 0.1),
     'L0_attn_bg': (0.0, 0.1),
     'L0_attn_bo': (0.0, 0.1),
     'L0_ffn_gate_b': (0.0, 0.1),
     'L0_ffn_be1': (0.0, 0.577),
     'L0_ffn_be2': (0.0, 0.359),
     'L0_ffn_be3': (0.0, 0.579),
     'L0_ffn_bs1': (0.0, 0.1),
     'L0_ffn_bs2': (0.0, 0.1),
     'L0_ffn_bs3': (0.0, 0.1)}
    factors = {}
    for name, (base, spread) in spreads.items():
        noise = np.random.default_rng([zlib.crc32(name.encode()), seed]).standard_normal(out[name].shape)
        drawn = base * np.exp(spread * noise) if base else spread * noise
        out[name] = jnp.asarray(drawn.astype(out[name].dtype))
    for name, factor in factors.items():
        out[name] = (out[name] * factor).astype(out[name].dtype)
    return out
```

```python
from contextlib import ExitStack

import numpy as np

import concourse.bass as bass
from concourse import mybir

F32 = mybir.dt.float32
BF16 = mybir.dt.bfloat16
I32 = mybir.dt.int32
ALU = mybir.AluOpType
ACT = mybir.ActivationFunctionType
AX = mybir.AxisListType.X

B, S, D = 8, 1024, 256
H, KD, VD = 16, 16, 32
HH = H // 2
VW = VD + 1
E, TOPK, G, TOPK_G, INTER = 16, 2, 4, 2, 128
P = 128
NCH = B * S // P
REG = B * S
NT = B * S * TOPK // P + E
SLOTS = E * REG + E * P
LAST_ROW = SLOTS - P
EPS = 1e-5
BIG = 3.0e38

C_ID, C_CAUSAL, C_BLOCK = 0, 128, 256
C_EVEN = C_BLOCK + HH * VW
C_ODD = C_EVEN + 1
C_IOM = C_ODD + 1
C_LT = C_IOM + E
C_REG = C_LT + G * G
C_PRE = C_REG + E
C_TILE = C_PRE + 128
C_N = C_TILE + NT


def constants():
    f = np.float32
    angle = (f(1.0) / f(10000.0) ** np.linspace(0.0, 1.0, KD // 2, dtype=f)).astype(f)
    angle = np.repeat(angle, 2)
    pos = np.arange(S, dtype=f)
    turn = (pos[:, None] * angle[None, :]).astype(f).astype(np.float64)
    decay = np.log((1.0 - 2.0 ** (-5.0 - np.arange(H))).astype(f)).astype(f).astype(np.float64)
    grow = np.exp(decay[None, :] * (pos.astype(np.float64)[:, None] - S / 2))
    sign = np.where(np.arange(KD) % 2 == 0, -1.0, 1.0)
    parts = []
    for scale in (grow, KD ** -0.5 / grow):
        parts.append(((np.cos(turn))[:, None, :] * scale[:, :, None]).reshape(S, D))
    for scale in (grow, KD ** -0.5 / grow):
        parts.append(((np.sin(turn) * sign)[:, None, :] * scale[:, :, None]).reshape(S, D))
    rotary = np.concatenate(parts, 1).astype(f)
    total = np.cumsum(np.exp(decay[None, :] * np.arange(S)[:, None]), 0)
    rownorm = (1.0 / np.sqrt(total)).astype(f)

    c = np.zeros((P, C_N), f)
    i = np.arange(P)
    c[:, C_ID:C_ID + P] = np.eye(P)
    c[:, C_CAUSAL:C_CAUSAL + P] = i[None, :] >= i[:, None]
    c[:, C_BLOCK:C_BLOCK + HH * VW] = (i[:, None] // KD) == (np.arange(HH * VW)[None, :] // VW)
    c[:, C_EVEN] = (i // KD) % 2 == 0
    c[:, C_ODD] = (i // KD) % 2 == 1
    c[:, C_IOM:C_IOM + E] = np.arange(E) - E
    c[:, C_LT:C_LT + G * G] = (np.arange(G)[None, :] < np.arange(G)[:, None]).reshape(-1)
    c[:, C_REG:C_REG + E] = np.arange(E) * REG
    c[:, C_PRE:C_PRE + P] = i[:, None] < i[None, :]
    c[:, C_TILE:C_TILE + NT] = np.arange(NT)
    return rotary, rownorm, c


def some(n):
    return not isinstance(n, int) or n > 0


def build(nc, x, Wq, bq, Wk, bk, Wv, bv, Wg, bg, Wo, bo, gate_w, gate_b, We1, be1, We2, be2, We3, be3,
          ws1, bs1, ws2, bs2, ws3, bs3, rotary, rownorm, const, out):
    xn2_rows = nc.dram_tensor("xn2_rows", [B * S, D], F32, kind="Internal").ap()
    slot_token = nc.dram_tensor("slot_token", [SLOTS, 1], I32, kind="Internal").ap()
    y_rows = nc.dram_tensor("y_rows", [NT * P, D], F32, kind="Internal").ap()
    bias_parts = nc.dram_tensor("bias_parts", [3, E + 1, 512], BF16, kind="Internal").ap()

    with ExitStack() as ctx:
        def sb(name, shape, dt=F32, scope=ctx):
            return scope.enter_context(nc.sbuf_tensor(name, shape, dt))

        bank = [ctx.enter_context(nc.psum_tensor(f"bank{i}", [P, 512], F32)) for i in range(4)]
        s_bank = [ctx.enter_context(nc.psum_tensor(f"s_bank{i}", [P, 512], F32)) for i in range(2)]
        o_bank = ctx.enter_context(nc.psum_tensor("o_bank", [P, 2, 512], F32))

        cst = sb("cst", [P, C_N])
        stream = sb("stream", [P, NCH, D])
        w13 = sb("w13", [P, 2, E, 2 * INTER])
        ones_bf = sb("ones_bf", [P, P], BF16)
        base = sb("base", [P, E])
        all_slots = sb("all_slots", [P, NCH // 2, 2, 2])
        all_w = sb("all_w", [P, NCH // 2, 2, 2])
        n_tiles = sb("n_tiles", [P, 4, E])
        tile_row = sb("tile_row", [1, NT], I32)
        tile_exp = sb("tile_exp", [1, NT], I32)

        with ExitStack() as first:
            def sa(name, shape, dt=F32):
                return sb(name, shape, dt, first)

            wqk = sa("wqk", [P, 2, 512])
            wv = sa("wv", [P, 2, 512])
            wg = sa("wg", [P, 2, 512])
            wo = sa("wo", [P, 4, D])
            ws13 = sa("ws13", [P, 2, 512])
            ws2_sb = sa("ws2_sb", [P, 2, D])
            gw = sa("gw", [P, 2, E])
            bqk_bc = sa("bqk_bc", [P, 512])
            bv_bc = sa("bv_bc", [P, 512])
            gb_bc = sa("gb_bc", [P, E])
            bg_col = sa("bg_col", [P, 4])
            bs_col = sa("bs_col", [P, 4])
            bias_o = sa("bias_o", [3, 512], BF16)
            before_bf = sa("before_bf", [P, P], BF16)
            tab = sa("tab", [P, 2, 2, 512])
            rs_tab = sa("rs_tab", [P, S // P, H])
            vmean = sa("vmean", [P, 3, H])
            state = sa("state", [P, B, 2, HH * VW])
            xn = sa("xn", [P, D])
            xnT = sa("xnT", [P, 2, P])
            qk = sa("qk", [P, 512])
            qk_cos = sa("qk_cos", [P, 512])
            qk_rot = sa("qk_rot", [P, 512])
            qkT = sa("qkT", [P, 4, P])
            q_split = sa("q_split", [P, 2, 2, P])
            val = sa("val", [P, H, VW])
            gate_silu = sa("gate_silu", [P, 2, 4, P])
            probs = sa("probs", [P, 4, 2, 2, P])
            squares = sa("squares", [P, H * VD])
            normed = sa("normed", [P, H * VD])
            gated = sa("gated", [P, 4, P])
            kv_new = sa("kv_new", [P, 2, HH * VW])
            stats = sa("stats", [P, 2, 6])
            mean_var = sa("mean_var", [P, 2, 2])
            var_eps = sa("var_eps", [P, 2])
            rstd = sa("rstd", [P, 2])
            half_neg = sa("half_neg", [P, H])
            gn = sa("gn", [P, 9, H])
            gn_pow = sa("gn_pow", [P, H])
            xn2 = sa("xn2", [P, 2, D])
            xn2T = sa("xn2T", [P, 2, P])
            sh_silu = sa("sh_silu", [P, 2, P])
            sh_hT = sa("sh_hT", [P, 2, P])
            lg = sa("lg", [P, 2, E])
            r8 = sa("r8", [P, 12, 2, G])
            r16 = sa("r16", [P, 12, 2, G])
            r32 = sa("r32", [P, 12, 2, E])
            r_cmp = sa("r_cmp", [P, 2, 2, G, G])
            r1 = sa("r1", [P, 12, 2])
            pick1 = sa("pick1", [P, 2, E])
            pick2 = sa("pick2", [P, 2, E])
            picks_bf = sa("picks_bf", [P, 2, E], BF16)
            slot_f = sa("slot_f", [P, 2, 2])
            slot_i = sa("slot_i", [P, 2, 2], I32)
            token_i = sa("token_i", [P, 2], I32)
            tile_e = sa("tile_e", [1, 3, NT])
            n_tiles_i = sa("n_tiles_i", [P, 2, E], I32)

        with ExitStack() as second:
            def sc(name, shape, dt=F32):
                return sb(name, shape, dt, second)

            w2 = sc("w2", [P, E, D])
            bias_e = sc("bias_e", [3, E, 512], BF16)
            tile_id = [sc(f"tile_id{u}", [P, 1], I32) for u in range(4)]
            tile_x = [sc(f"tile_x{u}", [P, D]) for u in range(4)]
            tile_xT = [sc(f"tile_xT{u}", [P, 2, P]) for u in range(2)]
            tile_silu = [sc(f"tile_silu{u}", [P, INTER]) for u in range(2)]
            tile_h = [sc(f"tile_h{u}", [P, INTER]) for u in range(2)]
            tile_hT = [sc(f"tile_hT{u}", [P, P]) for u in range(2)]
            tile_y = [sc(f"tile_y{u}", [P, D]) for u in range(2)]
            idx = [sc(f"idx{u}", [P, 2, 2], I32) for u in range(2)]
            slot_shift = sc("slot_shift", [P, 2 * NCH])
            slot_sum = sc("slot_sum", [P, 2 * NCH])
            picked = [sc(f"picked{u}", [P, 2, D]) for u in range(4)]

        ident = cst[:, C_ID:C_ID + P]
        causal = cst[:, C_CAUSAL:C_CAUSAL + P]
        block = cst[:, C_BLOCK:C_BLOCK + HH * VW]
        iom = cst[:, C_IOM:C_IOM + E]
        group_lt = cst[:, C_LT:C_LT + G * G].rearrange("p (g k) -> p g k", g=G)

        names = """const_in rot_in x_in w_in b_in expert_in brow_in part_out bias_in zero_in
            setup_step parts_ready setup_dve zeros_ready setup_pool
            xnT_ready xnT_taken qk_ready qk_taken v_ready v_taken gT_ready gT_taken qkT_ready qkT_taken qsplit_ready
            s_ready s_taken o_ready o_sums_taken o_squared kv_ready kv_taken state_ready
            nT_ready nT_taken wo_ready wo_taken xn2T_ready xn2T_taken h13_ready h1_taken h3_taken y_ready y_taken
            cos_ready rot_step rot_ready ln1_step ve1_ready rstd1_ready xn_ready gn_step gn_ve_ready gn_pow_ready
            normed_ready ln2_step ve2_ready rstd2_ready xn2_ready
            route_step shift_ready exp_ready picks_ready slot_step slots_ready scattered
            tile_step tiles_ready second_in
            t_x_ready t_x_taken t_h_ready t_h_silu t_h_taken t_ht_ready t_ht_taken t_y_ready t_y_taken
            idx_ready sum_step sum_done out_done""".split()
        q = {n: ctx.enter_context(nc.semaphore(n)) for n in names}

        def each(name, n):
            return [ctx.enter_context(nc.semaphore(f"{name}{u}")) for u in range(n)]

        xn2_stored = each("xn2_stored", 2)
        id_in, row_in, y_out, picked_in = each("id_in", 4), each("row_in", 4), each("y_out", 2), each("picked_in", 4)

        blk = ctx.enter_context(nc.Block())
        W_DMAS, B_DMAS = 10, 8
        tile_cmp = state[0:1, :, :, :].rearrange("p b a n -> p (b a n)")[:, 0:NT * E].rearrange("p (t e) -> p t e", e=E)
        brows = squares[0:E + 1, :]
        bres = normed[0:E + 1, :]
        bpart = gate_silu[0:E + 1, :, :, :].rearrange("p a m n -> p (a m n)").bitcast(BF16)[:, 0:3 * 512]\
            .rearrange("p (k n) -> p k n", k=3)
        zeros_i = probs[:, :, :, :, :].rearrange("p g h e s -> p (g h e s)").bitcast(I32)[:, 0:SLOTS // P]

        def alone(eng, count):
            if not isinstance(count, int):
                eng.to_reg(count)
            eng.wait_ge(q["const_in"], 16)
            return count

        @blk.sync
        def _(sp):
            sp.dma_start(cst[:, :], const).then_inc(q["const_in"], 16)
            by_pos = x.rearrange("b (c p) d -> c p b d", p=P)
            sp.dma_start(stream[:, 0:B, :], by_pos[0]).then_inc(q["x_in"], 16)
            for dst, src in ((brows[0:E, 0:INTER], be1), (brows[0:E, INTER:D], be3), (brows[0:E, D:512], be2),
                             (brows[E:E + 1, 0:D], bo.rearrange("(a n) -> a n", a=1)),
                             (brows[E:E + 1, D:512], bs2.rearrange("(a n) -> a n", a=1))):
                sp.dma_start(dst, src).then_inc(q["brow_in"], 16)
            kp = "(k p) n -> p k n"
            for dst, src in (
                (wqk[:, :, 0:D], Wq), (wqk[:, :, D:512], Wk), (wv[:, :, :], Wv), (wg[:, :, :], Wg),
                (wo[:, :, :], Wo), (ws13[:, :, 0:D], ws1), (ws13[:, :, D:512], ws3), (ws2_sb[:, :, :], ws2),
            ):
                sp.dma_start(dst, src.rearrange(kp, p=P)).then_inc(q["w_in"], 16)
            for k in range(2):
                sp.dma_start(gw[:, k, :], gate_w[:, k * P:(k + 1) * P].rearrange("e p -> p e"),
                             allow_slow_non_contiguous=True).then_inc(q["w_in"], 16)
            for dst, src in ((bg_col[:, :], bg), (bs_col[:, 0:2], bs1), (bs_col[:, 2:4], bs3)):
                sp.dma_start(dst, src.rearrange("(m p) -> p m", p=P),
                             allow_slow_non_contiguous=True).then_inc(q["b_in"], 16)
            for dst, src in ((bqk_bc[:, 0:D], bq), (bqk_bc[:, D:512], bk), (bv_bc[:, :], bv), (gb_bc[:, :], gate_b)):
                sp.dma_start(dst, src.partition_broadcast(P)).then_inc(q["b_in"], 16)
            sp.dma_start(rs_tab[:, :, :], rownorm.rearrange("(c p) h -> p c h", p=P)).then_inc(q["b_in"], 16)
            rot = rotary.rearrange("(c p) (a n) -> c p a n", p=P, a=2)
            for c in range(2):
                sp.dma_start(tab[:, c, :, :], rot[c]).then_inc(q["rot_in"], 16)
                sp.wait_ge(q["rot_in"], 16 * (c + 1))
            sp.wait_ge(q["parts_ready"], 1)
            for k in range(3):
                sp.dma_start(bias_parts[k], bpart[:, k, :]).then_inc(q["part_out"], 16)
            sp.wait_ge(q["part_out"], 48)
            sp.dma_start(bias_o[:, :], bias_parts[:, E, :]).then_inc(q["bias_in"], 16)
            sp.wait_ge(q["zeros_ready"], 1)
            sp.dma_start(slot_token.rearrange("(p n) a -> p (n a)", p=P), zeros_i).then_inc(q["zero_in"], 16)
            sp.wait_ge(q["x_in"], 16)
            for c in range(1, S // P):
                sp.dma_start(stream[:, c * B:(c + 1) * B, :], by_pos[c]).then_inc(q["x_in"], 16)
                sp.wait_ge(q["x_in"], 16 * (c + 1))
            for k in range(2):
                sp.dma_start(w13[:, k, :, 0:INTER], We1.rearrange("e (k p) i -> k p e i", p=P)[k]).then_inc(q["expert_in"], 16)
                sp.dma_start(w13[:, k, :, INTER:D], We3.rearrange("e (k p) i -> k p e i", p=P)[k]).then_inc(q["expert_in"], 16)

            def store(t, par):
                sp.wait_ge(q["xn2_ready"], alone(sp, t + 1))
                sp.dma_start(xn2_rows[bass.ds(t * P, P), :], xn2[:, par, :]).then_inc(xn2_stored[par], 16)

            for t in range(B):
                store(t, t % 2)
            with sp.Fori(0, S // P // 2 - 1) as j:
                for par in range(2):
                    sp.wait_ge(q["rot_ready"], alone(sp, (2 * j + par + 1) * B))
                    sp.dma_start(tab[:, par, :, :], rot[bass.ds(2 * j + par + 2, 1)].rearrange("c p a n -> (c p) a n"))\
                        .then_inc(q["rot_in"], 16)
                    for t in range(B):
                        store((2 * j + par + 1) * B + t, t % 2)
            for t in range(NCH - B, NCH):
                store(t, t % 2)

            sp.wait_ge(q["tiles_ready"], 1)
            sp.dma_start(bias_e[:, :, :], bias_parts[:, 0:E, :]).then_inc(q["second_in"], 16)
            sp.dma_start(w2[:, :, :], We2.rearrange("e i d -> i e d")).then_inc(q["second_in"], 16)
            for u in range(4):
                row = sp.value_load(tile_row[0:1, u:u + 1], min_val=0, max_val=LAST_ROW)
                sp.dma_start(tile_id[u][:, :], slot_token[bass.ds(row, P), :]).then_inc(id_in[u], 16)
            with sp.Fori(1, NT // 4) as j:
                for u in range(4):
                    row = sp.value_load(tile_row[0:1, bass.ds(4 * j + u, 1)], min_val=0, max_val=LAST_ROW)
                    sp.wait_ge(row_in[u], alone(sp, 16 * j))
                    sp.dma_start(tile_id[u][:, :], slot_token[bass.ds(row, P), :]).then_inc(id_in[u], 16)
            out_pos = out.rearrange("b (c p) d -> c p b d", p=P)
            for c in range(S // P):
                sp.wait_ge(q["sum_done"], (c + 1) * B)
                sp.dma_start(out_pos[c], stream[:, c * B:(c + 1) * B, :]).then_inc(q["out_done"], 16)
            sp.wait_ge(q["out_done"], 16 * (S // P))

        @blk.tensor
        def _(pe):
            def norm_transpose():
                for k in range(2):
                    tr = pe.transpose(bank[3][:, k * P:(k + 1) * P], xn[:, k * P:(k + 1) * P], ident)
                tr.then_inc(q["xnT_ready"], 1)

            def route_counts(pair):
                pe.wait_ge(q["picks_ready"], pair + 1)
                pe.matmul(bank[2][:, 272:304], before_bf[:, :], picks_bf[:, :, :], start=True, stop=False)
                pe.matmul(bank[2][:, 288:304], ones_bf[:, :], picks_bf[:, 0, :], start=False, stop=True)
                pe.matmul(bank[2][:, 304:320], ones_bf[:, :], picks_bf[:, 0, :], start=True, stop=False)
                return pe.matmul(bank[2][:, 304:320], ones_bf[:, :], picks_bf[:, 1, :], start=False, stop=True)

            def slot(i, par, pair=None, head=True, tail=True):
                t = i - 1
                if head:
                    if some(i):
                        pe.wait_ge(q["kv_taken"], 2 * i - 1)
                    pe.wait_ge(q["xnT_taken"], i + 1)
                    for k in range(2):
                        mm = pe.matmul(bank[0][:, :], xnT[:, k, :], wqk[:, k, :], start=(k == 0), stop=(k == 1))
                    mm.then_inc(q["qk_ready"], 1)
                if tail:
                    if some(t):
                        pe.wait_ge(q["y_taken"], t)
                    pe.wait_ge(q["normed_ready"], t + 1)
                    for m in range(4):
                        tr = pe.transpose(bank[2][:, m * P:(m + 1) * P], normed[:, m * P:(m + 1) * P], ident)
                    tr.then_inc(q["nT_ready"], 1)
                if head:
                    if some(i):
                        pe.wait_ge(q["kv_taken"], 2 * i)
                    for k in range(2):
                        mm = pe.matmul(bank[1][:, :], xnT[:, k, :], wv[:, k, :], start=(k == 0), stop=(k == 1))
                    mm.then_inc(q["v_ready"], 1)
                    for m in range(4):
                        for k in range(2):
                            mm = pe.matmul(bank[3][:, m * P:(m + 1) * P], wg[:, k, m * P:(m + 1) * P], xnT[:, k, :],
                                           start=(k == 0), stop=(k == 1))
                    mm.then_inc(q["gT_ready"], 1)
                if tail:
                    if head:
                        pe.wait_ge(q["qk_taken"], i + 1)
                    else:
                        pe.wait_ge(q["kv_taken"], 2 * i - 1)
                    pe.wait_ge(q["nT_taken"], t + 1)
                    for k in range(4):
                        pe.matmul(bank[0][:, 0:D], gated[:, k, :], wo[:, k, :], start=(k == 0), stop=False)
                    pe.matmul(bank[0][:, 0:D], ones_bf[0:3, :], bias_o[:, 0:D], start=False, stop=True)\
                        .then_inc(q["wo_ready"], 1)
                if head:
                    pe.wait_ge(q["v_taken"], i + 1)
                    pe.wait_ge(q["rot_ready"], i + 1)
                    for m in range(4):
                        tr = pe.transpose(bank[1][:, m * P:(m + 1) * P], qk_rot[:, m * P:(m + 1) * P], ident)
                    tr.then_inc(q["qkT_ready"], 1)
                    pe.wait_ge(q["qsplit_ready"], i + 1)
                    for g in range(4):
                        if some(4 * i + g - 1):
                            pe.wait_ge(q["s_taken"], 4 * i + g - 1)
                        for half in range(2):
                            mm = pe.matmul(s_bank[g % 2][:, half * 256:(half + 1) * 256],
                                           qkT[32 * g:32 * g + 32, 2 + half, :],
                                           q_split[32 * g:32 * g + 32, half, :, :], start=True, stop=True)
                        mm.then_inc(q["s_ready"], 1)
                if tail:
                    pe.wait_ge(q["xn2_ready"], t + 1)
                    for k in range(2):
                        tr = pe.transpose(bank[2][:, k * P:(k + 1) * P], xn2[:, 1 - par, k * P:(k + 1) * P], ident)
                    tr.then_inc(q["xn2T_ready"], 1)
                if head:
                    pe.wait_ge(q["state_ready"], i + 1)
                    for half in range(2):
                        pe.matmul(o_bank[:, half, 0:HH * VW], qkT[:, half, :], state_of(i)[:, half, :],
                                  start=True, stop=False)
                        if half == 0:
                            pe.wait_ge(q["s_taken"], 4 * i + 4)
                        for h in range(HH):
                            mm = pe.matmul(o_bank[:, half, h * VW:(h + 1) * VW], probs[:, h // 2, half, h % 2, :],
                                           val[:, half * HH + h, :], start=False, stop=(h == HH - 1))
                    mm.then_inc(q["o_ready"], 1)
                if tail:
                    if head:
                        pe.wait_ge(q["gT_taken"], i + 1)
                    else:
                        pe.wait_ge(q["h3_taken"], t)
                    pe.wait_ge(q["xn2T_taken"], t + 1)
                    for m in range(4):
                        for k in range(2):
                            mm = pe.matmul(bank[3][:, m * P:(m + 1) * P], ws13[:, k, m * P:(m + 1) * P], xn2T[:, k, :],
                                           start=(k == 0), stop=(k == 1))
                    mm.then_inc(q["h13_ready"], 1)
                if head:
                    if tail:
                        pe.wait_ge(q["wo_taken"], t + 1)
                    else:
                        pe.wait_ge(q["qk_taken"], i + 1)
                    for half in range(2):
                        if half == 1:
                            pe.wait_ge(q["qkT_taken"], i + 1)
                        pe.matmul(bank[half][:, 0:HH * VW], qk_rot[:, D + half * P:D + (half + 1) * P],
                                  val[:, half * HH:(half + 1) * HH, :], start=True, stop=True)\
                            .then_inc(q["kv_ready"], 1)
                if tail:
                    for k in range(2):
                        pe.matmul(bank[2][:, D:D + E], xn2T[:, k, :], gw[:, k, :], start=(k == 0), stop=(k == 1))
                    pe.wait_ge(q["h3_taken"], t + 1)
                    for k in range(2):
                        pe.matmul(bank[2][:, 0:D], sh_hT[:, k, :], ws2_sb[:, k, :], start=(k == 0), stop=False)
                    mm = pe.matmul(bank[2][:, 0:D], ones_bf[0:3, :], bias_o[:, D:512], start=False, stop=True)
                    if pair is not None:
                        mm = route_counts(pair)
                    mm.then_inc(q["y_ready"], 1)
                if head and not (isinstance(i, int) and i == NCH - 1):
                    if not tail:
                        pe.wait_ge(q["gT_taken"], i + 1)
                    pe.wait_ge(q["xn_ready"], i + 2)
                    norm_transpose()

            def state_of(i):
                if isinstance(i, int):
                    return state[:, i % B, :, :]
                return state[:, bass.ds(i % B, 1), :, :].rearrange("p b h n -> p (b h) n")

            pe.wait_ge(q["const_in"], 16)
            pe.wait_ge(q["xn_ready"], 1)
            norm_transpose()
            pe.wait_ge(q["w_in"], 16 * W_DMAS)
            pe.wait_ge(q["setup_dve"], 1)
            slot(0, 0, tail=False)
            pe.wait_ge(q["bias_in"], 16)
            slot(1, 1)
            slot(2, 0)
            with pe.Fori(1, NCH // 2 - 1) as j:
                slot(2 * j + 1, 1)
                slot(2 * j + 2, 0, pair=j - 1)
            slot(NCH - 1, 1)
            slot(NCH, 0, pair=NCH // 2 - 2, head=False)
            pe.wait_ge(q["y_taken"], NCH)
            route_counts(NCH // 2 - 1).then_inc(q["y_ready"], 1)

            def expert_of(t):
                at = slice(t, t + 1) if isinstance(t, int) else bass.ds(t, 1)
                return pe.value_load(tile_exp[0:1, at], min_val=0, max_val=E - 1)

            def step(t, u, turn, stages=(0, 1, 2, 3)):
                par = u % 2
                if 0 in stages:
                    pe.wait_ge(row_in[u], 16 * turn + 16)
                    if some(t - 1):
                        pe.wait_ge(q["t_x_taken"], t - 1)
                    for k in range(2):
                        tr = pe.transpose(bank[par][:, k * P:(k + 1) * P], tile_x[u][:, k * P:(k + 1) * P], ident)
                    tr.then_inc(q["t_x_ready"], 1)
                if 1 in stages:
                    e = expert_of(t - 1)
                    pe.wait_ge(q["t_x_taken"], t)
                    if some(t - 2):
                        pe.wait_ge(q["t_h_taken"], t - 2)
                    for k in range(2):
                        pe.matmul(bank[2 + 1 - par][:, 0:D], tile_xT[1 - par][:, k, :],
                                  w13[:, k, bass.ds(e, 1), :].rearrange("p e n -> p (e n)"), start=(k == 0), stop=False)
                    pe.matmul(bank[2 + 1 - par][:, 0:D], ones_bf[0:3, :],
                              bias_e[:, bass.ds(e, 1), 0:D].rearrange("p e n -> p (e n)"),
                              start=False, stop=True).then_inc(q["t_h_ready"], 1)
                if 2 in stages:
                    pe.wait_ge(q["t_h_taken"], t - 1)
                    if some(t - 3):
                        pe.wait_ge(q["t_ht_taken"], t - 3)
                    pe.transpose(s_bank[par][:, 0:P], tile_h[par][:, :], ident).then_inc(q["t_ht_ready"], 1)
                if 3 in stages:
                    e = expert_of(t - 3)
                    pe.wait_ge(q["t_ht_taken"], t - 2)
                    if some(t - 4):
                        pe.wait_ge(q["t_y_taken"], t - 4)
                    pe.matmul(o_bank[:, 1 - par, 0:D], tile_hT[1 - par][:, :],
                              w2[:, bass.ds(e, 1), :].rearrange("p e n -> p (e n)"), start=True, stop=False)
                    pe.matmul(o_bank[:, 1 - par, 0:D], ones_bf[0:3, :],
                              bias_e[:, bass.ds(e, 1), D:512].rearrange("p e n -> p (e n)"),
                              start=False, stop=True).then_inc(q["t_y_ready"], 1)

            pe.wait_ge(q["expert_in"], 64)
            pe.wait_ge(q["tiles_ready"], 1)
            pe.wait_ge(q["second_in"], 32)
            for t in range(4):
                step(t, t, 0, stages=range(t + 1))
            with pe.Fori(1, NT // 4) as j:
                for u in range(4):
                    step(4 * j + u, u, j)
            for t in range(NT, NT + 3):
                step(t, t % 4, t // 4, stages=range(t - NT + 1, 4))

        @blk.scalar
        def _(act):
            def norm_taken(i):
                act.wait_ge(q["xnT_ready"], i + 1)
                act.activation(xnT[:, :, :], bank[3][:, 0:D].rearrange("p (k n) -> p k n", k=2), ACT.Copy)\
                    .then_inc(q["xnT_taken"], 1)

            def slot(i, par, exp_of=None, head=True, tail=True):
                t = i - 1
                if head:
                    act.wait_ge(q["gT_ready"], i + 1)
                    if some(i - 1):
                        act.wait_ge(q["nT_taken"], i - 1)
                    for m in range(4):
                        a = act.activation(gate_silu[:, par, m, :], bank[3][:, m * P:(m + 1) * P], ACT.Silu,
                                           bias=bg_col[:, m:m + 1])
                    a.then_inc(q["gT_taken"], 1)
                    act.wait_ge(q["qkT_ready"], i + 1)
                    if some(i):
                        act.wait_ge(q["kv_ready"], 2 * i)
                    act.activation(qkT[:, :, :], bank[1][:, :].rearrange("p (k n) -> p k n", k=4), ACT.Copy)\
                        .then_inc(q["qkT_taken"], 1)
                if tail:
                    act.wait_ge(q["xn2T_ready"], t + 1)
                    if some(t):
                        act.wait_ge(q["y_ready"], t)
                    act.activation(xn2T[:, :, :], bank[2][:, 0:D].rearrange("p (k n) -> p k n", k=2), ACT.Copy)\
                        .then_inc(q["xn2T_taken"], 1)
                if head:
                    act.wait_ge(q["o_sums_taken"], i + 1)
                    if some(i):
                        act.wait_ge(q["normed_ready"], i)
                    act.activation(squares[:, :].rearrange("p (a h d) -> p a h d", a=2, h=HH),
                                   o_bank[:, :, 0:HH * VW].rearrange("p a (h w) -> p a h w", w=VW)[:, :, :, 0:VD],
                                   ACT.Square).then_inc(q["o_squared"], 1)
                if tail:
                    act.wait_ge(q["h13_ready"], t + 1)
                    if some(t):
                        act.wait_ge(q["h3_taken"], t)
                    for m in range(2):
                        a = act.activation(sh_silu[:, m, :], bank[3][:, m * P:(m + 1) * P], ACT.Silu,
                                           bias=bs_col[:, m:m + 1])
                    a.then_inc(q["h1_taken"], 1)
                if head and not (isinstance(i, int) and i == NCH - 1):
                    norm_taken(i + 1)
                if exp_of is not None:
                    act.wait_ge(q["shift_ready"], exp_of + 1)
                    act.activation(r32[:, 1, :, :], r32[:, 0, :, :], ACT.Exp).then_inc(q["exp_ready"], 1)

            act.wait_ge(q["b_in"], 16 * B_DMAS)
            norm_taken(0)
            act.wait_ge(q["part_out"], 48)
            slot(0, 0, tail=False)
            slot(1, 1)
            slot(2, 0, exp_of=0)
            with act.Fori(1, NCH // 2 - 1) as j:
                slot(2 * j + 1, 1)
                slot(2 * j + 2, 0, exp_of=j)
            slot(NCH - 1, 1)
            slot(NCH, 0, exp_of=NCH // 2 - 1, head=False)

            def step(t, u, turn, stages=(0, 1, 3)):
                par = u % 2
                if 0 in stages:
                    act.wait_ge(q["t_x_ready"], t + 1)
                    if some(t - 1):
                        act.wait_ge(q["t_h_ready"], t - 1)
                    act.activation(tile_xT[par][:, :, :], bank[par][:, 0:D].rearrange("p (k n) -> p k n", k=2),
                                   ACT.Copy).then_inc(q["t_x_taken"], 1)
                if 1 in stages:
                    act.wait_ge(q["t_h_ready"], t)
                    if some(t - 2):
                        act.wait_ge(q["t_h_taken"], t - 2)
                    act.activation(tile_silu[1 - par][:, :], bank[2 + 1 - par][:, 0:INTER], ACT.Silu)\
                        .then_inc(q["t_h_silu"], 1)
                if 3 in stages:
                    act.wait_ge(q["t_y_ready"], t - 2)
                    if some(t - 4):
                        act.wait_ge(y_out[1 - par], 16 * stores_before(u, turn))
                    act.activation(tile_y[1 - par][:, :], o_bank[:, 1 - par, 0:D], ACT.Copy).then_inc(q["t_y_taken"], 1)
                    act.wait_ge(q["t_y_taken"], t - 2)
                    act.dma_start(y_rows[bass.ds((t - 3) * P, P), :], tile_y[1 - par][:, :]).then_inc(y_out[1 - par], 16)

            def stores_before(u, turn):
                return 2 * turn + (u - 3) // 2

            act.wait_ge(q["tiles_ready"], 1)
            for t in range(4):
                step(t, t, 0, stages=[s for s in (0, 1, 3) if s <= t])
            with act.Fori(1, NT // 4) as j:
                for u in range(4):
                    step(4 * j + u, u, j)
            for t in range(NT, NT + 3):
                step(t, t % 4, t // 4, stages=[s for s in (1, 3) if s > t - NT])

        @blk.vector
        def _(dve):
            dve.wait_ge(q["brow_in"], 80)
            n = [0]

            def then(ins):
                n[0] += 1
                ins.then_inc(q["setup_step"], 1)
                dve.wait_ge(q["setup_step"], n[0])

            then(dve.tensor_copy(bpart[:, 0, :], brows))
            then(dve.tensor_tensor(bres, brows, bpart[:, 0, :], ALU.subtract))
            then(dve.tensor_copy(bpart[:, 1, :], bres))
            then(dve.tensor_tensor(brows, bres, bpart[:, 1, :], ALU.subtract))
            dve.tensor_copy(bpart[:, 2, :], brows).then_inc(q["parts_ready"], 1)
            dve.memset(zeros_i, 0).then_inc(q["zeros_ready"], 1)

            def norm_stats(src, w, step_sem, ready, i):
                dve.bn_stats(stats[:, w, :], src).then_inc(step_sem, 1)
                dve.wait_ge(step_sem, alone(dve, 2 * i + 1))
                dve.bn_aggr(mean_var[:, w, :], stats[:, w, :]).then_inc(step_sem, 1)
                dve.wait_ge(step_sem, 2 * i + 2)
                dve.tensor_scalar(var_eps[:, w:w + 1], mean_var[:, w, 1:2], EPS, None, ALU.add).then_inc(ready, 1)

            def row(i):
                return stream[:, i, :] if isinstance(i, int) else \
                    stream[:, bass.ds(i, 1), :].rearrange("p c d -> p (c d)")

            def norm1(i):
                dve.wait_ge(q["rstd1_ready"], i + 1)
                if some(i):
                    dve.wait_ge(q["xnT_ready"], i)
                dve.tensor_scalar(xn[:, :], row(i), mean_var[:, 0, 0:1], rstd[:, 0:1], ALU.subtract, ALU.mult)\
                    .then_inc(q["xn_ready"], 1)

            dve.memset(half_neg[:, :], -0.5).then_inc(q["setup_step"], 1)
            dve.wait_ge(q["x_in"], 16)
            dve.wait_ge(q["setup_step"], 5)
            norm_stats(row(0), 0, q["ln1_step"], q["ve1_ready"], 0)
            norm1(0)
            n[0] = 5
            dve.wait_ge(q["const_in"], 16)
            dve.wait_ge(q["w_in"], 16 * W_DMAS)
            dve.wait_ge(q["b_in"], 16 * B_DMAS)
            for k, v in ((0, wv[:, 0, :]), (1, wv[:, 1, :]), (2, bv_bc[:, :])):
                v3 = v.rearrange("p (h d) -> p h d", h=H)
                then(dve.tensor_reduce(vmean[:, k, :], v3, AX, ALU.add))
                then(dve.tensor_scalar(vmean[:, k, :], vmean[:, k, :], 1.0 / VD, None, ALU.mult))
                then(dve.tensor_tensor(v3, v3, vmean[:, k, :].unsqueeze(2).broadcast_to([P, H, VD]), ALU.subtract))
            dve.memset(val[:, :, VD:VW], 1.0)
            dve.memset(ones_bf[:, :], 1.0)
            dve.tensor_copy(before_bf[:, :], cst[:, C_PRE:C_PRE + P])
            dve.tensor_copy(base[:, :], cst[:, C_REG:C_REG + E]).then_inc(q["setup_dve"], 1)

            even, odd = cst[:, C_EVEN:C_EVEN + 1], cst[:, C_ODD:C_ODD + 1]
            bank3v = bank[3][:, :].rearrange("p (m n) -> p m n", m=4)

            def tab_of(i, a):
                if isinstance(i, int):
                    return tab[:, (i // B) % 2, a, :]
                return tab[:, bass.ds((i // B) % 2, 1), a, :].rearrange("p c n -> p (c n)")

            def rs_of(i):
                if isinstance(i, int):
                    return rs_tab[:, i // B, :]
                return rs_tab[:, bass.ds(i // B, 1), :].rearrange("p c h -> p (c h)")

            GN_STEPS, R_STEPS, SLOT_STEPS = 8, 31, 7

            def slot(i, par, pair=None, route=None, count=None, head=True, tail=True):
                t = i - 1
                if head:
                    dve.wait_ge(q["qk_ready"], i + 1)
                    dve.tensor_tensor(qk[:, :], bank[0][:, :], bqk_bc[:, :], ALU.add).then_inc(q["qk_taken"], 1)
                    dve.wait_ge(q["rot_in"], 16 * (i // B) + 16)
                    if some(i):
                        dve.wait_ge(q["kv_ready"], 2 * i)
                    dve.wait_ge(q["qk_taken"], i + 1)
                    for a in range(2):
                        dve.tensor_tensor(qk_rot[:, a::2], qk[:, 1 - a::2], tab_of(i, 1)[:, a::2], ALU.mult)\
                            .then_inc(q["rot_step"], 1)
                    if not (isinstance(i, int) and i == NCH - 1):
                        dve.wait_ge(q["x_in"], alone(dve, 16 * ((i + 1) // B) + 16))
                        norm_stats(row(i + 1), 0, q["ln1_step"], q["ve1_ready"], i + 1)
                    dve.wait_ge(q["rot_step"], 2 * i + 2)
                    dve.wait_ge(q["cos_ready"], i + 1)
                    dve.tensor_tensor(qk_rot[:, :], qk_rot[:, :], qk_cos[:, :], ALU.add).then_inc(q["rot_ready"], 1)
                    dve.wait_ge(q["v_ready"], i + 1)
                    dve.tensor_tensor(val[:, :, 0:VD], bank[1][:, :].rearrange("p (h d) -> p h d", h=H),
                                      bv_bc[:, :].rearrange("p (h d) -> p h d", h=H), ALU.add).then_inc(q["v_taken"], 1)
                    if not (isinstance(i, int) and i == NCH - 1):
                        norm1(i + 1)
                if tail:
                    dve.wait_ge(q["nT_ready"], t + 1)
                    dve.wait_ge(q["gT_taken"], t + 1)
                    dve.tensor_tensor(gated[:, :, :], bank[2][:, :].rearrange("p (m n) -> p m n", m=4),
                                      gate_silu[:, 1 - par, :, :], ALU.mult).then_inc(q["nT_taken"], 1)
                    dve.wait_ge(q["wo_ready"], t + 1)
                    dve.tensor_tensor(row(t), bank[0][:, 0:D], row(t), ALU.add).then_inc(q["wo_taken"], 1)
                    dve.wait_ge(q["wo_taken"], alone(dve, t + 1))
                    norm_stats(row(t), 1, q["ln2_step"], q["ve2_ready"], t)
                if head:
                    dve.wait_ge(q["qkT_taken"], i + 1)
                    dve.tensor_scalar(q_split[:, :, 0, :], qkT[:, 0:2, :], even, None, ALU.mult)
                    dve.tensor_scalar(q_split[:, :, 1, :], qkT[:, 0:2, :], odd, None, ALU.mult)\
                        .then_inc(q["qsplit_ready"], 1)
                if tail:
                    dve.wait_ge(q["rstd2_ready"], t + 1)
                    if some(pair):
                        dve.wait_ge(xn2_stored[1 - par], 16 * pair)
                    dve.tensor_scalar(xn2[:, 1 - par, :], row(t), mean_var[:, 1, 0:1], rstd[:, 1:2],
                                      ALU.subtract, ALU.mult).then_inc(q["xn2_ready"], 1)
                if head:
                    for g in range(4):
                        dve.wait_ge(q["s_ready"], 4 * i + g + 1)
                        dve.tensor_tensor(probs[:, g, :, :, :].rearrange("p h e s -> p (h e) s"),
                                          s_bank[g % 2][:, :].rearrange("p (h s) -> p h s", h=4),
                                          causal.unsqueeze(1).broadcast_to([P, 4, P]), ALU.mult)\
                            .then_inc(q["s_taken"], 1)
                    m = [0]

                    def gn_next(ins):
                        m[0] += 1
                        ins.then_inc(q["gn_step"], 1)
                        dve.wait_ge(q["gn_step"], GN_STEPS * i + m[0])

                    two = "p (a h) -> p a h"
                    dve.wait_ge(q["o_ready"], i + 1)
                    dve.tensor_tensor(gn[:, 0, :].rearrange(two, a=2),
                                      o_bank[:, :, 0:HH * VW].rearrange("p a (h w) -> p a h w", w=VW)[:, :, :, VD],
                                      rs_of(i).rearrange(two, a=2), ALU.mult).then_inc(q["o_sums_taken"], 1)
                    dve.wait_ge(q["o_sums_taken"], i + 1)
                    gn_next(dve.scalar_tensor_tensor(gn[:, 1, :], gn[:, 0, :], -1.0, gn[:, 0, :], ALU.mult, ALU.max))
                    gn_next(dve.tensor_scalar(gn[:, 2, :], gn[:, 1, :], 1.0, None, ALU.max))
                    gn_next(dve.reciprocal(gn[:, 3, :], gn[:, 2, :]))
                    gn_next(dve.tensor_tensor(gn[:, 4, :], gn[:, 3, :], rs_of(i), ALU.mult))
                    gn_next(dve.tensor_tensor(gn[:, 5, :], gn[:, 4, :], gn[:, 4, :], ALU.mult))
                    dve.wait_ge(q["o_squared"], i + 1)
                    gn_next(dve.tensor_reduce(gn[:, 6, :], squares[:, :].rearrange("p (h d) -> p h d", h=H), AX, ALU.add))
                    gn_next(dve.tensor_tensor(gn[:, 7, :], gn[:, 6, :], gn[:, 5, :], ALU.mult))
                    dve.tensor_scalar(gn[:, 8, :], gn[:, 7, :], 1.0 / VD, EPS, ALU.mult, ALU.add)\
                        .then_inc(q["gn_ve_ready"], 1)
                if tail:
                    dve.wait_ge(q["h1_taken"], t + 1)
                    for k in range(2):
                        h = dve.scalar_tensor_tensor(sh_hT[:, k, :], bank3v[:, 2 + k, :], bs_col[:, 2 + k:3 + k],
                                                     sh_silu[:, k, :], ALU.add, ALU.mult)
                    h.then_inc(q["h3_taken"], 1)
                if head:
                    dve.wait_ge(q["state_ready"], i + B)
                    for half in range(2):
                        dve.wait_ge(q["kv_ready"], 2 * i + half + 1)
                        dve.tensor_tensor(kv_new[:, half, :], bank[half][:, 0:HH * VW], block, ALU.mult)\
                            .then_inc(q["kv_taken"], 1)
                if tail:
                    dve.wait_ge(q["y_ready"], t + 1)
                    dve.tensor_copy(lg[:, 1 - par, :], bank[2][:, D:D + E])
                    y = dve.tensor_tensor(row(t), bank[2][:, 0:D], row(t), ALU.add)
                    if count is None:
                        y.then_inc(q["y_taken"], 1)
                    else:
                        counts(count)
                if head:
                    dve.wait_ge(q["gn_pow_ready"], i + 1)
                    gn_next(dve.tensor_tensor(gn[:, 0, :], gn[:, 4, :], gn_pow[:, :], ALU.mult))
                    assert m[0] == GN_STEPS
                    dve.tensor_tensor(normed[:, :].rearrange("p (a h d) -> p a h d", a=2, h=HH),
                                      o_bank[:, :, 0:HH * VW].rearrange("p a (h w) -> p a h w", w=VW)[:, :, :, 0:VD],
                                      gn[:, 0, :].rearrange(two, a=2).unsqueeze(3).broadcast_to([P, 2, HH, VD]),
                                      ALU.mult).then_inc(q["normed_ready"], 1)
                if route is not None:
                    pick_experts(route)

            def wide(v):
                return v.unsqueeze(2).broadcast_to([P, 2, E])

            def pick_experts(p):
                m = [0]

                def nxt(ins):
                    m[0] += 1
                    ins.then_inc(q["route_step"], 1)
                    dve.wait_ge(q["route_step"], R_STEPS * p + m[0])

                by_e = cst[:, C_IOM:C_IOM + E].unsqueeze(1).broadcast_to([P, 2, E])
                in_groups = "p c (g e) -> p (c g) e"
                nxt(dve.tensor_reduce(r1[:, 0, :], lg[:, :, :], AX, ALU.max))
                dve.tensor_tensor(r32[:, 0, :, :], lg[:, :, :], wide(r1[:, 0, :]), ALU.subtract)\
                    .then_inc(q["shift_ready"], 1)
                dve.wait_ge(q["exp_ready"], p + 1)
                nxt(dve.tensor_reduce(r1[:, 1, :], r32[:, 1, :, :], AX, ALU.add))
                nxt(dve.reciprocal(r1[:, 2, :], r1[:, 1, :]))
                nxt(dve.tensor_tensor(r32[:, 2, :, :], r32[:, 1, :, :], wide(r1[:, 2, :]), ALU.mult))
                score = r32[:, 3, :, :]
                nxt(dve.tensor_tensor(score, r32[:, 2, :, :], gb_bc[:, :].unsqueeze(1).broadcast_to([P, 2, E]), ALU.add))
                sg = score.rearrange(in_groups, g=G)
                hi = r16[:, 0:2, :, :].rearrange("p a c g -> p (a c g)").rearrange("p (n e) -> p n e", e=2)
                lo = r16[:, 2:4, :, :].rearrange("p a c g -> p (a c g)").rearrange("p (n e) -> p n e", e=2)
                dve.tensor_tensor(hi, sg[:, :, 0::2], sg[:, :, 1::2], ALU.max)
                nxt(dve.tensor_tensor(lo, sg[:, :, 0::2], sg[:, :, 1::2], ALU.min))
                flat8 = lambda k: r8[:, k, :, :].rearrange("p c g -> p (c g)")
                dve.tensor_tensor(flat8(0), hi[:, :, 0], hi[:, :, 1], ALU.max)
                dve.tensor_tensor(flat8(1), hi[:, :, 0], hi[:, :, 1], ALU.min)
                nxt(dve.tensor_tensor(flat8(2), lo[:, :, 0], lo[:, :, 1], ALU.max))
                nxt(dve.tensor_tensor(flat8(3), flat8(1), flat8(2), ALU.max))
                nxt(dve.tensor_tensor(flat8(4), flat8(0), flat8(3), ALU.add))
                mine = r8[:, 4, :, :].unsqueeze(3).broadcast_to([P, 2, G, G])
                other = r8[:, 4, :, :].unsqueeze(2).broadcast_to([P, 2, G, G])
                dve.tensor_tensor(r_cmp[:, 0, :, :, :], other, mine, ALU.is_gt)
                nxt(dve.tensor_tensor(r_cmp[:, 1, :, :, :], other, mine, ALU.is_equal))
                nxt(dve.tensor_tensor(r_cmp[:, 1, :, :, :], r_cmp[:, 1, :, :, :],
                                      group_lt.unsqueeze(1).broadcast_to([P, 2, G, G]), ALU.mult))
                nxt(dve.tensor_tensor(r_cmp[:, 0, :, :, :], r_cmp[:, 0, :, :, :], r_cmp[:, 1, :, :, :], ALU.add))
                nxt(dve.tensor_reduce(r8[:, 5, :, :], r_cmp[:, 0, :, :, :], AX, ALU.add))
                nxt(dve.tensor_scalar(r8[:, 6, :, :], r8[:, 5, :, :], float(TOPK_G), None, ALU.is_lt))
                nxt(dve.tensor_scalar(r8[:, 7, :, :], r8[:, 6, :, :], -1.0, BIG, ALU.add, ALU.mult))
                per_e = lambda k: r8[:, k, :, :].rearrange("p c g -> p (c g)").unsqueeze(2)\
                    .broadcast_to([P, 2 * G, E // G])
                left = r32[:, 4, :, :]
                nxt(dve.tensor_tensor(left.rearrange(in_groups, g=G), sg, per_e(6), ALU.mult))
                nxt(dve.tensor_tensor(left.rearrange(in_groups, g=G), left.rearrange(in_groups, g=G), per_e(7), ALU.add))
                for pick, v in ((pick1, left), (pick2, r32[:, 5, :, :])):
                    nxt(dve.tensor_reduce(r1[:, 3, :], v, AX, ALU.max))
                    nxt(dve.tensor_tensor(r32[:, 6, :, :], v, wide(r1[:, 3, :]), ALU.is_equal))
                    nxt(dve.tensor_tensor(r32[:, 7, :, :], r32[:, 6, :, :], by_e, ALU.mult))
                    nxt(dve.tensor_reduce(r1[:, 4, :], r32[:, 7, :, :], AX, ALU.min))
                    nxt(dve.tensor_tensor(pick[:, :, :], by_e, wide(r1[:, 4, :]), ALU.is_equal))
                    if pick is pick1:
                        nxt(dve.scalar_tensor_tensor(r32[:, 5, :, :], pick1[:, :, :], -BIG, left, ALU.mult, ALU.add))
                dve.tensor_tensor(picks_bf[:, :, :], pick1[:, :, :], pick2[:, :, :], ALU.add).then_inc(q["picks_ready"], 1)
                dve.tensor_tensor(r32[:, 8, :, :], r32[:, 2, :, :], pick1[:, :, :], ALU.mult)
                nxt(dve.tensor_tensor(r32[:, 9, :, :], r32[:, 2, :, :], pick2[:, :, :], ALU.mult))
                w_at = all_w[:, p, :, :] if isinstance(p, int) else \
                    all_w[:, bass.ds(p, 1), :, :].rearrange("p n k c -> p (n k) c")
                for k in range(2):
                    nxt(dve.tensor_reduce(w_at[:, k, :], r32[:, 8 + k, :, :], AX, ALU.add))
                assert m[0] == R_STEPS, m[0]

            def counts(p):
                m = [0]

                def nxt(ins):
                    m[0] += 1
                    ins.then_inc(q["slot_step"], 1)
                    dve.wait_ge(q["slot_step"], SLOT_STEPS * p + m[0])

                nxt(dve.tensor_tensor(r32[:, 10, :, :], bank[2][:, 272:304].rearrange("p (c e) -> p c e", c=2),
                                      base[:, :].unsqueeze(1).broadcast_to([P, 2, E]), ALU.add))
                dve.tensor_tensor(base[:, :], bank[2][:, 304:320], base[:, :], ALU.add).then_inc(q["y_taken"], 1)
                nxt(dve.tensor_tensor(r32[:, 11, :, :], r32[:, 10, :, :], pick1[:, :, :], ALU.mult))
                nxt(dve.tensor_reduce(slot_f[:, 0, :], r32[:, 11, :, :], AX, ALU.add))
                nxt(dve.tensor_tensor(r32[:, 11, :, :], r32[:, 10, :, :], pick2[:, :, :], ALU.mult))
                nxt(dve.tensor_reduce(slot_f[:, 1, :], r32[:, 11, :, :], AX, ALU.add))
                if some(p):
                    dve.wait_ge(q["scattered"], 64 * p)
                nxt(dve.tensor_copy(slot_i[:, :, :], slot_f[:, :, :]))
                at = all_slots[:, p, :, :] if isinstance(p, int) else \
                    all_slots[:, bass.ds(p, 1), :, :].rearrange("p n k c -> p (n k) c")
                nxt(dve.tensor_scalar(token_i[:, :], token_i[:, :], 2.0 * P, None, ALU.add))
                dve.tensor_copy(at, slot_f[:, :, :]).then_inc(q["slots_ready"], 1)

            dve.wait_ge(q["setup_step"], n[0])
            dve.wait_ge(q["setup_pool"], 1)
            dve.wait_ge(q["part_out"], 48)
            dve.wait_ge(q["zero_in"], 16)
            slot(0, 0, tail=False)
            slot(1, 1, pair=0)
            slot(2, 0, pair=0, route=0)
            with dve.Fori(1, NCH // 2 - 1) as j:
                slot(2 * j + 1, 1, pair=j)
                slot(2 * j + 2, 0, pair=j, route=j, count=j - 1)
            slot(NCH - 1, 1, pair=NCH // 2 - 1)
            slot(NCH, 0, pair=NCH // 2 - 1, route=NCH // 2 - 1, count=NCH // 2 - 2, head=False)
            dve.wait_ge(q["y_ready"], NCH + 1)
            counts(NCH // 2 - 1)

            n[0] = 0

            def tile_next(ins):
                n[0] += 1
                ins.then_inc(q["tile_step"], 1)
                dve.wait_ge(q["tile_step"], n[0])

            nt = n_tiles
            dve.wait_ge(q["y_taken"], NCH + 1)
            tile_next(dve.tensor_tensor(nt[:, 0, :], base[:, :], cst[:, C_REG:C_REG + E], ALU.subtract))
            tile_next(dve.tensor_scalar(nt[:, 0, :], nt[:, 0, :], float(P - 1), None, ALU.add))
            tile_next(dve.tensor_copy(n_tiles_i[:, 0, :], nt[:, 0, :]))
            tile_next(dve.tensor_scalar(n_tiles_i[:, 1, :], n_tiles_i[:, 0, :], 7, None, ALU.arith_shift_right))
            tile_next(dve.tensor_copy(nt[:, 1, :], n_tiles_i[:, 1, :]))
            tile_next(dve.memset(nt[:, 3, :], 1.0))
            tile_next(dve.tensor_tensor_scan(nt[:, 2, :], nt[:, 3, :], nt[:, 1, :], 0.0, ALU.mult, ALU.add))
            tiles = cst[0:1, C_TILE:C_TILE + NT]
            per_tile = lambda v: v.unsqueeze(1).broadcast_to([1, NT, E])
            tile_next(dve.tensor_tensor(tile_cmp, tiles.unsqueeze(2).broadcast_to([1, NT, E]),
                                        per_tile(nt[0:1, 2, :]), ALU.is_ge))
            tile_next(dve.tensor_reduce(tile_e[:, 0, :], tile_cmp, AX, ALU.add))
            tile_next(dve.tensor_tensor(tile_cmp, tile_cmp, per_tile(nt[0:1, 1, :]), ALU.mult))
            tile_next(dve.tensor_reduce(tile_e[:, 1, :], tile_cmp, AX, ALU.add))
            tile_next(dve.tensor_tensor(tile_e[:, 2, :], tiles, tile_e[:, 1, :], ALU.subtract))
            tile_next(dve.tensor_scalar(tile_e[:, 2, :], tile_e[:, 2, :], float(P), None, ALU.mult))
            tile_next(dve.scalar_tensor_tensor(tile_e[:, 2, :], tile_e[:, 0, :], float(REG), tile_e[:, 2, :],
                                               ALU.mult, ALU.add))
            tile_next(dve.tensor_copy(tile_row[:, :], tile_e[:, 2, :]))
            dve.wait_ge(q["scattered"], 64 * (NCH // 2))
            for par in range(2):
                dve.wait_ge(xn2_stored[par], 16 * (NCH // 2))
            dve.tensor_scalar(tile_exp[:, :], tile_e[:, 0, :], float(E - 1), None, ALU.min).then_inc(q["tiles_ready"], 1)

            tile_next(dve.tensor_scalar(nt[:, 3, :], nt[:, 1, :], float(P), -float(REG), ALU.mult, ALU.add))
            slots = all_slots[:, :, :, :].rearrange("p n k c -> p (n k c)")
            for e in range(1, E):
                tile_next(dve.tensor_scalar(slot_shift[:, :], slots, float(e * REG), nt[:, 3, e - 1:e],
                                            ALU.is_ge, ALU.mult))
                tile_next(dve.tensor_tensor(slot_sum[:, :], slot_shift[:, :], slots if e == 1 else slot_sum[:, :],
                                            ALU.add))
            tile_next(dve.tensor_copy(slots, slot_sum[:, :]))

            def step(t, u, turn, stages=(1, 2)):
                par = u % 2
                if 1 in stages:
                    dve.wait_ge(q["t_h_silu"], t)
                    if some(t - 2):
                        dve.wait_ge(q["t_ht_ready"], t - 2)
                    dve.tensor_tensor(tile_h[1 - par][:, :], bank[2 + 1 - par][:, INTER:D], tile_silu[1 - par][:, :],
                                      ALU.mult).then_inc(q["t_h_taken"], 1)
                if 2 in stages:
                    dve.wait_ge(q["t_ht_ready"], t - 1)
                    if some(t - 3):
                        dve.wait_ge(q["t_y_ready"], t - 3)
                    dve.tensor_copy(tile_hT[par][:, :], s_bank[par][:, 0:P]).then_inc(q["t_ht_taken"], 1)

            for t in range(4):
                step(t, t, 0, stages=[s for s in (1, 2) if s <= t])
            with dve.Fori(1, NT // 4) as j:
                for u in range(4):
                    step(4 * j + u, u, j)
            for t in range(NT, NT + 2):
                step(t, t % 4, t // 4, stages=[s for s in (1, 2) if s > t - NT])

            def add_pair(p, two):
                for c in range(2):
                    u = 2 * two + c
                    for k in range(2):
                        w = all_w[:, p, k, c:c + 1] if isinstance(p, int) else \
                            all_w[:, bass.ds(p, 1), k, c:c + 1].rearrange("p n c -> p (n c)")
                        if k == 0:
                            dve.wait_ge(picked_in[u], 32 * (p // 2) + 32 if isinstance(p, int) else 32 * turn_of(p, two))
                        o = dve.scalar_tensor_tensor(row(2 * p + c), picked[u][:, k, :], w, row(2 * p + c),
                                                     ALU.mult, ALU.add)
                        if k == 0:
                            o.then_inc(q["sum_step"], 1)
                            dve.wait_ge(q["sum_step"], 2 * p + c + 1)
                        else:
                            o.then_inc(q["sum_done"], 1)

            def turn_of(p, two):
                return (p - two) // 2 + 1

            def indices(p, two):
                at = all_slots[:, p, :, :] if isinstance(p, int) else \
                    all_slots[:, bass.ds(p, 1), :, :].rearrange("p n k c -> p (n k) c")
                dve.tensor_copy(idx[two][:, :, :], at).then_inc(q["idx_ready"], 1)

            indices(0, 0)
            indices(1, 1)
            with dve.Fori(0, NCH // 4 - 1) as j:
                for two in range(2):
                    add_pair(2 * j + two, two)
                    indices(2 * j + two + 2, two)
            for two in range(2):
                add_pair(NCH // 2 - 2 + two, two)

        @blk.gpsimd
        def _(pool):
            pool.iota(token_i[:, :], pattern=[[P, 2]], base=-2 * P, channel_multiplier=1).then_inc(q["setup_pool"], 1)
            pool.memset(state[:, :, :, :], 0.0).then_inc(q["state_ready"], B)
            pool.wait_ge(q["state_ready"], B)

            def rstd_of(w, ready):
                pool.tensor_tensor(rstd[:, w:w + 1], var_eps[:, w:w + 1], half_neg[:, 0:1], ALU.pow).then_inc(ready, 1)

            def tab_of(i, a):
                if isinstance(i, int):
                    return tab[:, (i // B) % 2, a, :]
                return tab[:, bass.ds((i // B) % 2, 1), a, :].rearrange("p c n -> p (c n)")

            def slot(i, par, count=None, head=True, tail=True):
                t = i - 1
                if head:
                    pool.wait_ge(q["rot_in"], 16 * (i // B) + 16)
                    if some(i):
                        pool.wait_ge(q["rot_ready"], i)
                    pool.wait_ge(q["qk_taken"], i + 1)
                    pool.tensor_tensor(qk_cos[:, :], qk[:, :], tab_of(i, 0), ALU.mult).then_inc(q["cos_ready"], 1)
                    if not (isinstance(i, int) and i == NCH - 1):
                        pool.wait_ge(q["ve1_ready"], i + 2)
                        rstd_of(0, q["rstd1_ready"])
                if tail:
                    pool.wait_ge(q["ve2_ready"], t + 1)
                    rstd_of(1, q["rstd2_ready"])
                if head:
                    pool.wait_ge(q["gn_ve_ready"], i + 1)
                    pool.tensor_tensor(gn_pow[:, :], gn[:, 8, :], half_neg[:, :], ALU.pow).then_inc(q["gn_pow_ready"], 1)
                    pool.wait_ge(q["kv_taken"], 2 * i + 2)
                    st = state[:, i % B, :, :].rearrange("p a n -> p (a n)") if isinstance(i, int) else \
                        state[:, bass.ds(i % B, 1), :, :].rearrange("p b a n -> p (b a n)")
                    pool.tensor_tensor(st, st, kv_new[:, :, :].rearrange("p a n -> p (a n)"), ALU.add)\
                        .then_inc(q["state_ready"], 1)
                if count is not None:
                    scatter(count)

            def scatter(p):
                pool.wait_ge(q["slots_ready"], alone(pool, p + 1))
                for k in range(2):
                    for c in range(2):
                        pool.indirect_dma_start(
                            out=slot_token, out_offset=bass.IndirectOffsetOnAxis(ap=slot_i[:, k, c:c + 1], axis=0),
                            in_=token_i[:, c:c + 1], in_offset=None).then_inc(q["scattered"], 16)

            pool.wait_ge(q["ve1_ready"], 1)
            rstd_of(0, q["rstd1_ready"])
            slot(0, 0, tail=False)
            slot(1, 1)
            slot(2, 0)
            pool.wait_ge(q["zero_in"], 16)
            with pool.Fori(1, NCH // 2 - 1) as j:
                slot(2 * j + 1, 1)
                slot(2 * j + 2, 0, count=j - 1)
            slot(NCH - 1, 1)
            slot(NCH, 0, count=NCH // 2 - 2, head=False)
            scatter(NCH // 2 - 1)

            def gather(t, u, turn):
                pool.wait_ge(id_in[u], alone(pool, 16 * turn + 16))
                if some(t - 3):
                    pool.wait_ge(q["t_x_ready"], alone(pool, t - 3))
                pool.indirect_dma_start(
                    out=tile_x[u][:, :], out_offset=None, in_=xn2_rows,
                    in_offset=bass.IndirectOffsetOnAxis(ap=tile_id[u][:, 0:1], axis=0)).then_inc(row_in[u], 16)

            pool.wait_ge(q["tiles_ready"], 1)
            for t in range(4):
                gather(t, t, 0)
            with pool.Fori(1, NT // 4) as j:
                for u in range(4):
                    gather(4 * j + u, u, j)

            for par in range(2):
                pool.wait_ge(y_out[par], 16 * (NT // 2))

            def gather_pair(p, two, turn):
                pool.wait_ge(q["idx_ready"], alone(pool, p + 1))
                for c in range(2):
                    if some(turn):
                        pool.wait_ge(q["sum_done"], alone(pool, 4 * turn + 2 * two + c - 3))
                    for k in range(2):
                        pool.indirect_dma_start(
                            out=picked[2 * two + c][:, k, :], out_offset=None, in_=y_rows,
                            in_offset=bass.IndirectOffsetOnAxis(ap=idx[two][:, k, c:c + 1], axis=0))\
                            .then_inc(picked_in[2 * two + c], 16)

            for two in range(2):
                gather_pair(two, two, 0)
            with pool.Fori(1, NCH // 4) as j:
                for two in range(2):
                    gather_pair(2 * j + two, two, j)


_INS = ["L0_attn_x", "L0_attn_Wq", "L0_attn_bq", "L0_attn_Wk", "L0_attn_bk", "L0_attn_Wv", "L0_attn_bv", "L0_attn_Wg",
        "L0_attn_bg", "L0_attn_Wo", "L0_attn_bo", "L0_ffn_gate_w", "L0_ffn_gate_b", "L0_ffn_We1", "L0_ffn_be1",
        "L0_ffn_We2", "L0_ffn_be2", "L0_ffn_We3", "L0_ffn_be3", "L0_ffn_ws1", "L0_ffn_bs1", "L0_ffn_ws2",
        "L0_ffn_bs2", "L0_ffn_ws3", "L0_ffn_bs3"]


def kernel(**inputs):
    import numpy as _np
    import concourse.bacc as _bacc
    from concourse import mybir as _mybir
    from concourse.bass_utils import run_bass_kernel_spmd as _run

    nc = _bacc.Bacc("TRN2", target_bir_lowering=False, num_devices=1)
    arrays, args = {}, []

    def give(name, a):
        arrays[name] = a
        args.append(nc.dram_tensor(name, a.shape, _mybir.dt.from_np(a.dtype), kind="ExternalInput").ap())

    for name in _INS:
        give(f"in_{name}_dram", _np.ascontiguousarray(inputs[name]))
    for name, a in zip(("rotary", "rownorm", "const"), constants()):
        give(f"table_{name}_dram", a)
    out = nc.dram_tensor("out_0_dram", (B, S, D), F32, kind="ExternalOutput").ap()
    build(nc, *args, out)
    r = _run(nc, [arrays], core_ids=[0])
    return r.results[0]["out_0_dram"]
```

```python
from contextlib import ExitStack

import numpy as np

import concourse.bass as bass
from concourse import mybir

F32 = mybir.dt.float32
BF16 = mybir.dt.bfloat16
I32 = mybir.dt.int32
ALU = mybir.AluOpType
ACT = mybir.ActivationFunctionType
AX = mybir.AxisListType.X

B, S, D = 8, 1024, 256
H, KD, VD = 16, 16, 32
HH = H // 2
VW = VD + 1
E, TOPK, G, TOPK_G, INTER = 16, 2, 4, 2, 128
P = 128
NCH = B * S // P
REG = B * S
NT = B * S * TOPK // P + E
SLOTS = E * REG + E * P
LAST_ROW = SLOTS - P
EPS = 1e-5
BIG = 3.0e38

C_ID, C_CAUSAL, C_BLOCK = 0, 128, 256
C_HEAD = C_BLOCK + HH * VW
C_IOM = C_HEAD + HH
C_LT = C_IOM + E
C_REG = C_LT + G * G
C_PRE = C_REG + E
C_TILE = C_PRE + 128
C_N = C_TILE + NT


def constants():
    f = np.float32
    angle = (f(1.0) / f(10000.0) ** np.linspace(0.0, 1.0, KD // 2, dtype=f)).astype(f)
    angle = np.repeat(angle, 2)
    pos = np.arange(S, dtype=f)
    turn = (pos[:, None] * angle[None, :]).astype(f).astype(np.float64)
    decay = np.log((1.0 - 2.0 ** (-5.0 - np.arange(H))).astype(f)).astype(f).astype(np.float64)
    grow = np.exp(decay[None, :] * (pos.astype(np.float64)[:, None] - S / 2))
    sign = np.where(np.arange(KD) % 2 == 0, -1.0, 1.0)
    parts = []
    for scale in (grow, KD ** -0.5 / grow):
        parts.append(((np.cos(turn))[:, None, :] * scale[:, :, None]).reshape(S, D))
    for scale in (grow, KD ** -0.5 / grow):
        parts.append(((np.sin(turn) * sign)[:, None, :] * scale[:, :, None]).reshape(S, D))
    rotary = np.concatenate(parts, 1).astype(f)
    floor = (EPS * np.cumsum(np.exp(decay[None, :] * np.arange(S)[:, None]), 0)).astype(f)

    c = np.zeros((P, C_N), f)
    i = np.arange(P)
    c[:, C_ID:C_ID + P] = np.eye(P)
    c[:, C_CAUSAL:C_CAUSAL + P] = i[None, :] >= i[:, None]
    c[:, C_BLOCK:C_BLOCK + HH * VW] = (i[:, None] // KD) == (np.arange(HH * VW)[None, :] // VW)
    c[:, C_HEAD:C_HEAD + HH] = (i[:, None] // KD) == np.arange(HH)[None, :]
    c[:, C_IOM:C_IOM + E] = np.arange(E) - E
    c[:, C_LT:C_LT + G * G] = (np.arange(G)[None, :] < np.arange(G)[:, None]).reshape(-1)
    c[:, C_REG:C_REG + E] = np.arange(E) * REG
    c[:, C_PRE:C_PRE + P] = i[:, None] < i[None, :]
    c[:, C_TILE:C_TILE + NT] = np.arange(NT)
    return rotary, floor, c


def some(n):
    return not isinstance(n, int) or n > 0


def build(nc, x, Wq, bq, Wk, bk, Wv, bv, Wg, bg, Wo, bo, gate_w, gate_b, We1, be1, We2, be2, We3, be3,
          ws1, bs1, ws2, bs2, ws3, bs3, rotary, floor, const, out):
    xn2_rows = nc.dram_tensor("xn2_rows", [B * S, D], F32, kind="Internal").ap()
    slot_token = nc.dram_tensor("slot_token", [SLOTS, 1], I32, kind="Internal").ap()
    y_rows = nc.dram_tensor("y_rows", [NT * P, D], F32, kind="Internal").ap()
    bias_parts = nc.dram_tensor("bias_parts", [3, E + 1, 512], BF16, kind="Internal").ap()

    with ExitStack() as ctx:
        def sb(name, shape, dt=F32, scope=ctx):
            return scope.enter_context(nc.sbuf_tensor(name, shape, dt))

        bank = [ctx.enter_context(nc.psum_tensor(f"bank{i}", [P, 512], F32)) for i in range(4)]
        s_bank = [ctx.enter_context(nc.psum_tensor(f"s_bank{i}", [P, 512], F32)) for i in range(2)]
        o_bank = ctx.enter_context(nc.psum_tensor("o_bank", [P, 2, 512], F32))

        cst = sb("cst", [P, C_N])
        stream = sb("stream", [P, NCH, D])
        w13 = sb("w13", [P, 2, E, 2 * INTER])
        ones_bf = sb("ones_bf", [P, P], BF16)
        base = sb("base", [P, E])
        all_slots = sb("all_slots", [P, NCH // B, 2, B])
        all_w = sb("all_w", [P, NCH // B, 2, B])
        n_tiles = sb("n_tiles", [P, 4, E])
        tile_row = sb("tile_row", [1, NT], I32)
        tile_exp = sb("tile_exp", [1, NT], I32)

        with ExitStack() as first:
            def sa(name, shape, dt=F32):
                return sb(name, shape, dt, first)

            wqk = sa("wqk", [P, 2, 512])
            wv = sa("wv", [P, 2, 512])
            wg = sa("wg", [P, 2, 512])
            wo = sa("wo", [P, 4, D])
            ws13 = sa("ws13", [P, 2, 512])
            ws2_sb = sa("ws2_sb", [P, 2, D])
            gw = sa("gw", [P, 2, E])
            bias_qkv = sa("bias_qkv", [3, 2, 512], BF16)
            gb_bc = sa("gb_bc", [P, E])
            bg_col = sa("bg_col", [P, 4])
            bs_col = sa("bs_col", [P, 4])
            bias_o = sa("bias_o", [3, 512], BF16)
            before_bf = sa("before_bf", [P, P], BF16)
            tab = sa("tab", [P, 2, 2, 512])
            floor_tab = sa("floor_tab", [P, S // P, H])
            vmean = sa("vmean", [P, 2, H])
            vmean_b = sa("vmean_b", [3, H])
            state = sa("state", [P, B, 2, HH * VW])
            xn = sa("xn", [P, D])
            xnT = sa("xnT", [P, 2, P])
            qk = sa("qk", [P, 512])
            qk_cos = sa("qk_cos", [P, 512])
            qk_rot = sa("qk_rot", [P, 512])
            qkT = sa("qkT", [P, 4, P])
            q_split = sa("q_split", [P, 2, HH, P])
            val = sa("val", [P, H, VW])
            gate_silu = sa("gate_silu", [P, 2, 4, P])
            probs = sa("probs", [P, 4, 2, 2, P])
            squares = sa("squares", [P, 2, HH * VW])
            normed = sa("normed", [P, H * VD])
            gated = sa("gated", [P, 4, P])
            kv_new = sa("kv_new", [P, 2, HH * VW])
            stats = sa("stats", [P, 2, 6])
            mean_var = sa("mean_var", [P, 2, 2])
            var_eps = sa("var_eps", [P, 2])
            rstd = sa("rstd", [P, 2])
            half_neg = sa("half_neg", [P, H])
            gn = sa("gn", [P, 3, H])
            gn_pow = sa("gn_pow", [P, H])
            xn2 = sa("xn2", [P, 2, D])
            xn2T = sa("xn2T", [P, 2, P])
            sh_silu = sa("sh_silu", [P, 2, P])
            sh_hT = sa("sh_hT", [P, 2, P])
            lg = sa("lg", [P, B, E])
            r8 = sa("r8", [P, 8, B, G])
            r16 = sa("r16", [P, 4, B, G])
            r32 = sa("r32", [P, 6, B, E])
            r_cmp = sa("r_cmp", [P, 2, B, G, G])
            r1 = sa("r1", [P, 5, B])
            pick1 = sa("pick1", [P, B, E])
            pick2 = sa("pick2", [P, B, E])
            picks_bf = sa("picks_bf", [P, B, E], BF16)
            slot_f = sa("slot_f", [P, 2, B])
            slot_i = sa("slot_i", [P, 2, B], I32)
            token_i = sa("token_i", [P, B], I32)
            tile_e = sa("tile_e", [1, 3, NT])
            n_tiles_i = sa("n_tiles_i", [P, 2, E], I32)

        with ExitStack() as second:
            def sc(name, shape, dt=F32):
                return sb(name, shape, dt, second)

            w2 = sc("w2", [P, E, D])
            bias_e = sc("bias_e", [3, E, 512], BF16)
            tile_id = [sc(f"tile_id{u}", [P, 1], I32) for u in range(4)]
            tile_x = [sc(f"tile_x{u}", [P, D]) for u in range(4)]
            tile_xT = [sc(f"tile_xT{u}", [P, 2, P]) for u in range(2)]
            tile_silu = [sc(f"tile_silu{u}", [P, INTER]) for u in range(2)]
            tile_h = [sc(f"tile_h{u}", [P, INTER]) for u in range(2)]
            tile_hT = [sc(f"tile_hT{u}", [P, P]) for u in range(2)]
            tile_y = [sc(f"tile_y{u}", [P, D]) for u in range(2)]
            idx = sc("idx", [P, 2, B], I32)
            slot_shift = sc("slot_shift", [P, 2 * NCH])
            slot_sum = sc("slot_sum", [P, 2 * NCH])
            picked = [sc(f"picked{u}", [P, 2, D]) for u in range(4)]

        ident = cst[:, C_ID:C_ID + P]
        causal = cst[:, C_CAUSAL:C_CAUSAL + P]
        block = cst[:, C_BLOCK:C_BLOCK + HH * VW]
        iom = cst[:, C_IOM:C_IOM + E]
        group_lt = cst[:, C_LT:C_LT + G * G].rearrange("p (g k) -> p g k", g=G)

        names = """const_in rot_in x_in w_in b_in expert_in brow_in part_out bias_in zero_in
            setup_step parts_ready setup_dve zeros_ready setup_pool
            xnT_ready xnT_taken qk_ready qk_taken v_ready v_taken gT_ready gT_taken qkT_ready
            s_ready s_taken o_ready o_squared kv_ready kv_taken state_ready
            nT_ready nT_taken wo_ready wo_taken xn2T_ready xn2T_taken h13_ready h1_taken h3_taken y_ready y_taken
            cos_ready rot_step rot_ready ln1_step ve1_ready rstd1_ready xn_ready gn_step gn_ve_ready gn_pow_ready
            normed_ready ln2_step ve2_ready qsplit_ready qcopy_ready rstd2_ready xn2_ready
            route_step shift_ready exp_ready picks_ready slot_step slots_ready scattered
            tile_step tiles_ready second_in
            row_step t_x_ready t_x_taken t_h_ready t_h_silu t_h_taken t_ht_ready t_ht_taken t_y_ready t_y_taken
            idx_ready sum_step sum_done out_done""".split()
        q = {n: ctx.enter_context(nc.semaphore(n)) for n in names}

        def each(name, n):
            return [ctx.enter_context(nc.semaphore(f"{name}{u}")) for u in range(n)]

        xn2_stored = each("xn2_stored", 2)
        id_in, row_in, y_out, picked_in = each("id_in", 4), each("row_in", 4), each("y_out", 2), each("picked_in", 4)

        blk = ctx.enter_context(nc.Block())
        W_DMAS, B_DMAS = 10, 8
        tile_cmp = state[0:1, :, :, :].rearrange("p b a n -> p (b a n)")[:, 0:NT * E].rearrange("p (t e) -> p t e", e=E)
        brows = squares[0:E + 1, :, :].rearrange("p a n -> p (a n)")[:, 0:512]
        bres = normed[0:E + 1, :]
        bpart = gate_silu[0:E + 1, :, :, :].rearrange("p a m n -> p (a m n)").bitcast(BF16)[:, 0:3 * 512]\
            .rearrange("p (k n) -> p k n", k=3)
        bias_f = q_split[0:3, 0, :, :].rearrange("p h n -> p (h n)").rearrange("p (a n) -> p a n", a=2)
        bpart3 = gated[0:3, :, :].rearrange("p m n -> p (m n)").bitcast(BF16).rearrange("p (a n) -> p a n", a=1)
        bsum = xn2[0:3, :, :].rearrange("p a n -> p (a n)").bitcast(BF16)
        zeros_i = probs[:, :, :, :, :].rearrange("p g h e s -> p (g h e s)").bitcast(I32)[:, 0:SLOTS // P]

        def alone(eng, count):
            if not isinstance(count, int):
                eng.to_reg(count)
            eng.wait_ge(q["const_in"], 16)
            return count

        COUNTS_AT, SLOTS_AT, SCATTERS_AT = 5, 6, 7

        @blk.sync
        def _(sp):
            sp.dma_start(cst[:, :], const).then_inc(q["const_in"], 16)
            by_pos = x.rearrange("b (c p) d -> c p b d", p=P)
            sp.dma_start(stream[:, 0:B, :], by_pos[0]).then_inc(q["x_in"], 16)
            for dst, src in ((brows[0:E, 0:INTER], be1), (brows[0:E, INTER:D], be3), (brows[0:E, D:512], be2),
                             (brows[E:E + 1, 0:D], bo.rearrange("(a n) -> a n", a=1)),
                             (brows[E:E + 1, D:512], bs2.rearrange("(a n) -> a n", a=1))):
                sp.dma_start(dst, src).then_inc(q["brow_in"], 16)
            kp = "(k p) n -> p k n"
            for dst, src in (
                (wqk[:, :, 0:D], Wq), (wqk[:, :, D:512], Wk), (wv[:, :, :], Wv), (wg[:, :, :], Wg),
                (wo[:, :, :], Wo), (ws13[:, :, 0:D], ws1), (ws13[:, :, D:512], ws3), (ws2_sb[:, :, :], ws2),
            ):
                sp.dma_start(dst, src.rearrange(kp, p=P)).then_inc(q["w_in"], 16)
            for k in range(2):
                sp.dma_start(gw[:, k, :], gate_w[:, k * P:(k + 1) * P].rearrange("e p -> p e"),
                             allow_slow_non_contiguous=True).then_inc(q["w_in"], 16)
            for dst, src in ((bg_col[:, :], bg), (bs_col[:, 0:2], bs1), (bs_col[:, 2:4], bs3)):
                sp.dma_start(dst, src.rearrange("(m p) -> p m", p=P),
                             allow_slow_non_contiguous=True).then_inc(q["b_in"], 16)
            for dst, src in ((bias_f[:, 0, 0:D], bq), (bias_f[:, 0, D:512], bk), (bias_f[:, 1, :], bv)):
                sp.dma_start(dst, src.partition_broadcast(3)).then_inc(q["b_in"], 16)
            sp.dma_start(gb_bc[:, :], gate_b.partition_broadcast(P)).then_inc(q["b_in"], 16)
            sp.dma_start(floor_tab[:, :, :], floor.rearrange("(c p) h -> p c h", p=P)).then_inc(q["b_in"], 16)
            rot = rotary.rearrange("(c p) (a n) -> c p a n", p=P, a=2)
            for c in range(2):
                sp.dma_start(tab[:, c, :, :], rot[c]).then_inc(q["rot_in"], 16)
                sp.wait_ge(q["rot_in"], 16 * (c + 1))
            sp.wait_ge(q["parts_ready"], 1)
            for k in range(3):
                sp.dma_start(bias_parts[k], bpart[:, k, :]).then_inc(q["part_out"], 16)
            sp.wait_ge(q["part_out"], 48)
            sp.dma_start(bias_o[:, :], bias_parts[:, E, :]).then_inc(q["bias_in"], 16)
            sp.wait_ge(q["zeros_ready"], 1)
            sp.dma_start(slot_token.rearrange("(p n) a -> p (n a)", p=P), zeros_i).then_inc(q["zero_in"], 16)
            sp.wait_ge(q["x_in"], 16)
            for c in range(1, S // P):
                sp.dma_start(stream[:, c * B:(c + 1) * B, :], by_pos[c]).then_inc(q["x_in"], 16)
                sp.wait_ge(q["x_in"], 16 * (c + 1))
            for k in range(2):
                sp.dma_start(w13[:, k, :, 0:INTER], We1.rearrange("e (k p) i -> k p e i", p=P)[k]).then_inc(q["expert_in"], 16)
                sp.dma_start(w13[:, k, :, INTER:D], We3.rearrange("e (k p) i -> k p e i", p=P)[k]).then_inc(q["expert_in"], 16)

            def store(t, par):
                sp.wait_ge(q["xn2_ready"], alone(sp, t + 1))
                sp.dma_start(xn2_rows[bass.ds(t * P, P), :], xn2[:, par, :]).then_inc(xn2_stored[par], 16)

            for t in range(B):
                store(t, t % 2)
            with sp.Fori(0, S // P // 2 - 1) as j:
                for par in range(2):
                    sp.wait_ge(q["rot_ready"], alone(sp, (2 * j + par + 1) * B))
                    sp.dma_start(tab[:, par, :, :], rot[bass.ds(2 * j + par + 2, 1)].rearrange("c p a n -> (c p) a n"))\
                        .then_inc(q["rot_in"], 16)
                    for t in range(B):
                        store((2 * j + par + 1) * B + t, t % 2)
            for t in range(NCH - B, NCH):
                store(t, t % 2)

            sp.wait_ge(q["tiles_ready"], 1)
            sp.dma_start(bias_e[:, :, :], bias_parts[:, 0:E, :]).then_inc(q["second_in"], 16)
            sp.dma_start(w2[:, :, :], We2.rearrange("e i d -> i e d")).then_inc(q["second_in"], 16)
            for u in range(4):
                row = sp.value_load(tile_row[0:1, u:u + 1], min_val=0, max_val=LAST_ROW)
                sp.dma_start(tile_id[u][:, :], slot_token[bass.ds(row, P), :]).then_inc(id_in[u], 16)
            with sp.Fori(1, NT // 4) as j:
                for u in range(4):
                    row = sp.value_load(tile_row[0:1, bass.ds(4 * j + u, 1)], min_val=0, max_val=LAST_ROW)
                    sp.wait_ge(row_in[u], alone(sp, 16 * j))
                    sp.dma_start(tile_id[u][:, :], slot_token[bass.ds(row, P), :]).then_inc(id_in[u], 16)
            out_pos = out.rearrange("b (c p) d -> c p b d", p=P)
            for c in range(S // P):
                sp.wait_ge(q["sum_done"], (c + 1) * B)
                sp.dma_start(out_pos[c], stream[:, c * B:(c + 1) * B, :]).then_inc(q["out_done"], 16)
            sp.wait_ge(q["out_done"], 16 * (S // P))

        @blk.tensor
        def _(pe):
            def norm_transpose():
                for k in range(2):
                    tr = pe.transpose(bank[3][:, k * P:(k + 1) * P], xn[:, k * P:(k + 1) * P], ident)
                tr.then_inc(q["xnT_ready"], 1)

            def route_counts(c):
                pe.wait_ge(q["picks_ready"], c + 1)
                at = 272
                pe.matmul(bank[2][:, at:at + B * E], before_bf[:, :], picks_bf[:, :, :], start=True, stop=False)
                for b in range(1, B):
                    pe.matmul(bank[2][:, at + b * E:at + B * E], ones_bf[:, :], picks_bf[:, 0:B - b, :],
                              start=False, stop=(b == B - 1))
                for b in range(B):
                    mm = pe.matmul(bank[2][:, at + B * E:at + (B + 1) * E], ones_bf[:, :], picks_bf[:, b, :],
                                   start=(b == 0), stop=(b == B - 1))
                return mm

            def slot(i, u, counts_of=None, head=True, tail=True):
                t = i - 1
                if head:
                    if some(i):
                        pe.wait_ge(q["kv_taken"], 2 * i - 1)
                    pe.wait_ge(q["xnT_taken"], i + 1)
                    for k in range(2):
                        pe.matmul(bank[0][:, :], xnT[:, k, :], wqk[:, k, :], start=(k == 0), stop=False)
                    pe.matmul(bank[0][:, :], ones_bf[0:3, :], bias_qkv[:, 0, :], start=False, stop=True)\
                        .then_inc(q["qk_ready"], 1)
                    if some(i):
                        pe.wait_ge(q["kv_taken"], 2 * i)
                    for k in range(2):
                        pe.matmul(bank[1][:, :], xnT[:, k, :], wv[:, k, :], start=(k == 0), stop=False)
                    pe.matmul(bank[1][:, :], ones_bf[0:3, :], bias_qkv[:, 1, :], start=False, stop=True)\
                        .then_inc(q["v_ready"], 1)
                if tail:
                    if some(t):
                        pe.wait_ge(q["y_taken"], t)
                    pe.wait_ge(q["normed_ready"], t + 1)
                    for m in range(4):
                        tr = pe.transpose(bank[2][:, m * P:(m + 1) * P], normed[:, m * P:(m + 1) * P], ident)
                    tr.then_inc(q["nT_ready"], 1)
                if head:
                    for m in range(4):
                        for k in range(2):
                            mm = pe.matmul(bank[3][:, m * P:(m + 1) * P], wg[:, k, m * P:(m + 1) * P], xnT[:, k, :],
                                           start=(k == 0), stop=(k == 1))
                    mm.then_inc(q["gT_ready"], 1)
                if head:
                    pe.wait_ge(q["v_taken"], i + 1)
                    pe.wait_ge(q["rot_ready"], i + 1)
                    for m in range(4):
                        tr = pe.transpose(bank[1][:, m * P:(m + 1) * P], qk_rot[:, m * P:(m + 1) * P], ident)
                    tr.then_inc(q["qkT_ready"], 1)
                if tail:
                    if head:
                        pe.wait_ge(q["qk_taken"], i + 1)
                    else:
                        pe.wait_ge(q["kv_taken"], 2 * i - 1)
                    pe.wait_ge(q["nT_taken"], t + 1)
                    for k in range(4):
                        pe.matmul(bank[0][:, 0:D], gated[:, k, :], wo[:, k, :], start=(k == 0), stop=False)
                    pe.matmul(bank[0][:, 0:D], ones_bf[0:3, :], bias_o[:, 0:D], start=False, stop=True)\
                        .then_inc(q["wo_ready"], 1)
                if head:
                    for g in range(3):
                        scores(i, g)
                if tail:
                    pe.wait_ge(q["xn2_ready"], t + 1)
                    for k in range(2):
                        tr = pe.transpose(bank[2][:, k * P:(k + 1) * P], xn2[:, 1 - u % 2, k * P:(k + 1) * P], ident)
                    tr.then_inc(q["xn2T_ready"], 1)
                if head:
                    scores(i, 3)
                    pe.wait_ge(q["state_ready"], i + 1)
                    pe.wait_ge(q["qcopy_ready"], i + 1)
                    if tail:
                        pe.wait_ge(q["gT_taken"], i + 1)
                        pe.wait_ge(q["xn2T_taken"], t + 1)
                    for half in range(2):
                        if tail:
                            for n in range(4 * half, 4 * half + 4):
                                hidden(n, t)
                        pe.matmul(o_bank[:, half, 0:HH * VW], qkT[:, half, :], state[:, u, half, :],
                                  start=True, stop=False)
                        for h in range(HH):
                            if half == 0 and h % 2 == 0:
                                pe.wait_ge(q["s_taken"], 4 * i + 1 + h // 2)
                            mm = pe.matmul(o_bank[:, half, h * VW:(h + 1) * VW], probs[:, h // 2, half, h % 2, :],
                                           val[:, half * HH + h, :], start=False, stop=(h == HH - 1))
                    mm.then_inc(q["o_ready"], 1)
                else:
                    pe.wait_ge(q["xn2T_taken"], t + 1)
                    for n in range(8):
                        hidden(n, t)
                if head:
                    if tail:
                        pe.wait_ge(q["wo_taken"], t + 1)
                    else:
                        pe.wait_ge(q["qk_taken"], i + 1)
                    for half in range(2):
                        if half == 1:
                            pe.wait_ge(q["qcopy_ready"], i + 1)
                        pe.matmul(bank[half][:, 0:HH * VW], qk_rot[:, D + half * P:D + (half + 1) * P],
                                  val[:, half * HH:(half + 1) * HH, :], start=True, stop=True)\
                            .then_inc(q["kv_ready"], 1)
                if tail:
                    pe.wait_ge(q["h3_taken"], t + 1)
                if head and not (isinstance(i, int) and i == NCH - 1):
                    if not tail:
                        pe.wait_ge(q["gT_taken"], i + 1)
                    pe.wait_ge(q["xn_ready"], i + 2)
                    norm_transpose()
                if tail:
                    for k in range(2):
                        pe.matmul(bank[2][:, D:D + E], xn2T[:, k, :], gw[:, k, :], start=(k == 0), stop=(k == 1))
                    for k in range(2):
                        pe.matmul(bank[2][:, 0:D], sh_hT[:, k, :], ws2_sb[:, k, :], start=(k == 0), stop=False)
                    mm = pe.matmul(bank[2][:, 0:D], ones_bf[0:3, :], bias_o[:, D:512], start=False, stop=True)
                    if counts_of is not None:
                        mm = route_counts(counts_of)
                    mm.then_inc(q["y_ready"], 1)

            def scores(i, g):
                if some(4 * i + g - 1):
                    pe.wait_ge(q["s_taken"], 4 * i + g - 1)
                pe.wait_ge(q["qsplit_ready"], 4 * i + g + 1)
                for half in range(2):
                    mm = pe.matmul(s_bank[g % 2][:, half * 256:(half + 1) * 256], qkT[:, 2 + half, :],
                                   q_split[:, half, 2 * g:2 * g + 2, :], start=True, stop=True)
                mm.then_inc(q["s_ready"], 1)

            def hidden(n, t):
                m, k = n // 2, n % 2
                mm = pe.matmul(bank[3][:, m * P:(m + 1) * P], ws13[:, k, m * P:(m + 1) * P], xn2T[:, k, :],
                               start=(k == 0), stop=(k == 1))
                if n == 7:
                    mm.then_inc(q["h13_ready"], 1)

            pe.wait_ge(q["const_in"], 16)
            pe.wait_ge(q["xn_ready"], 1)
            norm_transpose()
            pe.wait_ge(q["w_in"], 16 * W_DMAS)
            pe.wait_ge(q["setup_dve"], 1)
            slot(0, 0, tail=False)
            pe.wait_ge(q["bias_in"], 16)
            for i in range(1, B + 1):
                slot(i, i % B)
            with pe.Fori(1, NCH // B - 1) as c:
                for u in range(1, B + 1):
                    slot(B * c + u, u % B, counts_of=c - 1 if u == COUNTS_AT else None)
            for u in range(1, B + 1):
                slot(NCH - B + u, u % B, counts_of=NCH // B - 2 if u == COUNTS_AT else None, head=u < B)
            pe.wait_ge(q["y_taken"], NCH)
            route_counts(NCH // B - 1).then_inc(q["y_ready"], 1)

            expert = [pe.alloc_register(f"expert{u}") for u in range(4)]

            def expert_of(u):
                return pe.snap(expert[u % 4], min_val=0, max_val=E - 1)

            def step(t, u, turn, stages=(0, 1, 2, 3)):
                par = u % 2
                if 0 in stages:
                    pe.wait_ge(row_in[u], 16 * turn + 16)
                    if some(t - 1):
                        pe.wait_ge(q["t_x_taken"], t - 1)
                    for k in range(2):
                        tr = pe.transpose(bank[par][:, k * P:(k + 1) * P], tile_x[u][:, k * P:(k + 1) * P], ident)
                    tr.then_inc(q["t_x_ready"], 1)
                if 1 in stages:
                    e = expert_of(u - 1)
                    pe.wait_ge(q["t_x_taken"], t)
                    if some(t - 2):
                        pe.wait_ge(q["t_h_taken"], t - 2)
                    for k in range(2):
                        pe.matmul(bank[2 + 1 - par][:, 0:D], tile_xT[1 - par][:, k, :],
                                  w13[:, k, bass.ds(e, 1), :].rearrange("p e n -> p (e n)"), start=(k == 0), stop=False)
                    pe.matmul(bank[2 + 1 - par][:, 0:D], ones_bf[0:3, :],
                              bias_e[:, bass.ds(e, 1), 0:D].rearrange("p e n -> p (e n)"),
                              start=False, stop=True).then_inc(q["t_h_ready"], 1)
                if 0 in stages:
                    at = slice(t, t + 1) if isinstance(t, int) else bass.ds(t, 1)
                    pe.reg_load(expert[u], tile_exp[0:1, at])
                if 2 in stages:
                    pe.wait_ge(q["t_h_taken"], t - 1)
                    if some(t - 3):
                        pe.wait_ge(q["t_ht_taken"], t - 3)
                    pe.transpose(s_bank[par][:, 0:P], tile_h[par][:, :], ident).then_inc(q["t_ht_ready"], 1)
                if 3 in stages:
                    e = expert_of(u - 3)
                    pe.wait_ge(q["t_ht_taken"], t - 2)
                    if some(t - 4):
                        pe.wait_ge(q["t_y_taken"], t - 4)
                    pe.matmul(o_bank[:, 1 - par, 0:D], tile_hT[1 - par][:, :],
                              w2[:, bass.ds(e, 1), :].rearrange("p e n -> p (e n)"), start=True, stop=False)
                    pe.matmul(o_bank[:, 1 - par, 0:D], ones_bf[0:3, :],
                              bias_e[:, bass.ds(e, 1), D:512].rearrange("p e n -> p (e n)"),
                              start=False, stop=True).then_inc(q["t_y_ready"], 1)

            pe.wait_ge(q["expert_in"], 64)
            pe.wait_ge(q["tiles_ready"], 1)
            pe.wait_ge(q["second_in"], 32)
            for t in range(4):
                step(t, t, 0, stages=range(t + 1))
            with pe.Fori(1, NT // 4) as j:
                for u in range(4):
                    step(4 * j + u, u, j)
            for t in range(NT, NT + 3):
                step(t, t % 4, t // 4, stages=range(t - NT + 1, 4))

        @blk.scalar
        def _(act):
            def norm_taken(i):
                act.wait_ge(q["xnT_ready"], i + 1)
                act.activation(xnT[:, :, :], bank[3][:, 0:D].rearrange("p (k n) -> p k n", k=2), ACT.Copy)\
                    .then_inc(q["xnT_taken"], 1)

            def slot(i, u, exp_of=None, head=True, tail=True):
                t = i - 1
                if exp_of is not None:
                    act.wait_ge(q["shift_ready"], exp_of + 1)
                    act.activation(r32[:, 1, :, :], r32[:, 0, :, :], ACT.Exp).then_inc(q["exp_ready"], 1)
                if head:
                    act.wait_ge(q["qk_ready"], i + 1)
                    if some(i):
                        act.wait_ge(q["rot_ready"], i)
                    act.activation(qk[:, :], bank[0][:, :], ACT.Copy).then_inc(q["qk_taken"], 1)
                    act.wait_ge(q["v_ready"], i + 1)
                    if some(i):
                        act.wait_ge(q["kv_ready"], 2 * i)
                    act.activation(val[:, :, 0:VD], bank[1][:, :].rearrange("p (h d) -> p h d", h=H), ACT.Copy)\
                        .then_inc(q["v_taken"], 1)
                    act.wait_ge(q["gT_ready"], i + 1)
                    if some(i - 1):
                        act.wait_ge(q["nT_taken"], i - 1)
                    for m in range(4):
                        a = act.activation(gate_silu[:, u % 2, m, :], bank[3][:, m * P:(m + 1) * P], ACT.Silu,
                                           bias=bg_col[:, m:m + 1])
                    a.then_inc(q["gT_taken"], 1)
                    act.wait_ge(q["qkT_ready"], i + 1)
                    qT = bank[1][:, 0:D].rearrange("p (k n) -> p k n", k=2)
                    act.activation(qkT[:, 2:4, :], bank[1][:, D:512].rearrange("p (k n) -> p k n", k=2), ACT.Copy)
                    for h in range(HH):
                        a = act.activation(q_split[:, :, h, :], qT, ACT.Copy, scale=cst[:, C_HEAD + h:C_HEAD + h + 1])
                        if h % 2:
                            a.then_inc(q["qsplit_ready"], 1)
                    act.activation(qkT[:, 0:2, :], qT, ACT.Copy).then_inc(q["qcopy_ready"], 1)
                if tail:
                    act.wait_ge(q["xn2T_ready"], t + 1)
                    if some(t):
                        act.wait_ge(q["y_ready"], t)
                    act.activation(xn2T[:, :, :], bank[2][:, 0:D].rearrange("p (k n) -> p k n", k=2), ACT.Copy)\
                        .then_inc(q["xn2T_taken"], 1)
                    act.wait_ge(q["h13_ready"], t + 1)
                    if some(t):
                        act.wait_ge(q["h3_taken"], t)
                    for m in range(2):
                        a = act.activation(sh_silu[:, m, :], bank[3][:, m * P:(m + 1) * P], ACT.Silu,
                                           bias=bs_col[:, m:m + 1])
                    a.then_inc(q["h1_taken"], 1)
                if head:
                    act.wait_ge(q["o_ready"], i + 1)
                    if some(i):
                        act.wait_ge(q["gn_ve_ready"], i)
                    act.activation(squares[:, :, :], o_bank[:, :, 0:HH * VW], ACT.Square).then_inc(q["o_squared"], 1)
                if head and not (isinstance(i, int) and i == NCH - 1):
                    norm_taken(i + 1)

            act.wait_ge(q["b_in"], 16 * B_DMAS)
            norm_taken(0)
            act.wait_ge(q["setup_dve"], 1)
            act.wait_ge(q["part_out"], 48)
            slot(0, 0, tail=False)
            for i in range(1, B + 1):
                slot(i, i % B)
            with act.Fori(1, NCH // B - 1) as c:
                for u in range(1, B + 1):
                    slot(B * c + u, u % B, exp_of=c - 1 if u == 2 else None)
            for u in range(1, B + 1):
                slot(NCH - B + u, u % B, exp_of=NCH // B - 2 if u == 2 else None, head=u < B)
            act.wait_ge(q["shift_ready"], NCH // B)
            act.activation(r32[:, 1, :, :], r32[:, 0, :, :], ACT.Exp).then_inc(q["exp_ready"], 1)

            def step(t, u, turn, stages=(0, 1, 3)):
                par = u % 2
                if 0 in stages:
                    act.wait_ge(q["t_x_ready"], t + 1)
                    if some(t - 1):
                        act.wait_ge(q["t_h_ready"], t - 1)
                    act.activation(tile_xT[par][:, :, :], bank[par][:, 0:D].rearrange("p (k n) -> p k n", k=2),
                                   ACT.Copy).then_inc(q["t_x_taken"], 1)
                if 1 in stages:
                    act.wait_ge(q["t_h_ready"], t)
                    if some(t - 2):
                        act.wait_ge(q["t_h_taken"], t - 2)
                    act.activation(tile_silu[1 - par][:, :], bank[2 + 1 - par][:, 0:INTER], ACT.Silu)\
                        .then_inc(q["t_h_silu"], 1)
                if 3 in stages:
                    act.wait_ge(q["t_y_ready"], t - 2)
                    if some(t - 4):
                        act.wait_ge(y_out[1 - par], 16 * stores_before(u, turn))
                    act.activation(tile_y[1 - par][:, :], o_bank[:, 1 - par, 0:D], ACT.Copy).then_inc(q["t_y_taken"], 1)
                    act.wait_ge(q["t_y_taken"], t - 2)
                    act.dma_start(y_rows[bass.ds((t - 3) * P, P), :], tile_y[1 - par][:, :]).then_inc(y_out[1 - par], 16)

            def stores_before(u, turn):
                return 2 * turn + (u - 3) // 2

            act.wait_ge(q["tiles_ready"], 1)
            for t in range(4):
                step(t, t, 0, stages=[s for s in (0, 1, 3) if s <= t])
            with act.Fori(1, NT // 4) as j:
                for u in range(4):
                    step(4 * j + u, u, j)
            for t in range(NT, NT + 3):
                step(t, t % 4, t // 4, stages=[s for s in (1, 3) if s > t - NT])

        @blk.vector
        def _(dve):
            dve.wait_ge(q["brow_in"], 80)
            n = [0]

            def then(ins):
                n[0] += 1
                ins.then_inc(q["setup_step"], 1)
                dve.wait_ge(q["setup_step"], n[0])

            then(dve.tensor_copy(bpart[:, 0, :], brows))
            then(dve.tensor_tensor(bres, brows, bpart[:, 0, :], ALU.subtract))
            then(dve.tensor_copy(bpart[:, 1, :], bres))
            then(dve.tensor_tensor(brows, bres, bpart[:, 1, :], ALU.subtract))
            dve.tensor_copy(bpart[:, 2, :], brows).then_inc(q["parts_ready"], 1)
            dve.memset(zeros_i, 0).then_inc(q["zeros_ready"], 1)

            def norm_stats(src, w, step_sem, ready, i):
                dve.bn_stats(stats[:, w, :], src).then_inc(step_sem, 1)
                dve.wait_ge(step_sem, alone(dve, 2 * i + 1))
                dve.bn_aggr(mean_var[:, w, :], stats[:, w, :]).then_inc(step_sem, 1)
                dve.wait_ge(step_sem, 2 * i + 2)
                dve.tensor_scalar(var_eps[:, w:w + 1], mean_var[:, w, 1:2], EPS, None, ALU.add).then_inc(ready, 1)

            def row(i):
                return stream[:, i, :] if isinstance(i, int) else \
                    stream[:, bass.ds(i, 1), :].rearrange("p c d -> p (c d)")

            def norm1(i):
                dve.wait_ge(q["rstd1_ready"], i + 1)
                if some(i):
                    dve.wait_ge(q["xnT_ready"], i)
                dve.tensor_scalar(xn[:, :], row(i), mean_var[:, 0, 0:1], rstd[:, 0:1], ALU.subtract, ALU.mult)\
                    .then_inc(q["xn_ready"], 1)

            dve.memset(half_neg[:, :], -0.5).then_inc(q["setup_step"], 1)
            dve.wait_ge(q["x_in"], 16)
            dve.wait_ge(q["setup_step"], 5)
            norm_stats(row(0), 0, q["ln1_step"], q["ve1_ready"], 0)
            norm1(0)
            n[0] = 5
            dve.wait_ge(q["const_in"], 16)
            dve.wait_ge(q["w_in"], 16 * W_DMAS)
            dve.wait_ge(q["b_in"], 16 * B_DMAS)
            for mean, v in ((vmean[:, 0, :], wv[:, 0, :]), (vmean[:, 1, :], wv[:, 1, :]),
                            (vmean_b[:, :], bias_f[:, 1, :])):
                v3 = v.rearrange("p (h d) -> p h d", h=H)
                then(dve.tensor_reduce(mean, v3, AX, ALU.add))
                then(dve.tensor_scalar(mean, mean, 1.0 / VD, None, ALU.mult))
                then(dve.tensor_tensor(v3, v3, mean.unsqueeze(2).broadcast_to(list(v3.shape)), ALU.subtract))
            for k in range(3):
                pick = cst[0:3, C_ID + k:C_ID + k + 1]
                then(dve.tensor_copy(bpart3[:, 0, :], bias_f[:, :, :].rearrange("p a n -> p (a n)")))
                if k == 0:
                    then(dve.tensor_scalar(bsum, bpart3[:, 0, :], pick, None, ALU.mult))
                else:
                    then(dve.scalar_tensor_tensor(bsum, bpart3[:, 0, :], pick, bsum, ALU.mult, ALU.add))
                then(dve.tensor_tensor(bias_f[:, :, :].rearrange("p a n -> p (a n)"),
                                       bias_f[:, :, :].rearrange("p a n -> p (a n)"), bpart3[:, 0, :], ALU.subtract))
            then(dve.tensor_copy(bias_qkv[:, :, :].rearrange("p a n -> p (a n)"), bsum))
            dve.memset(val[:, :, VD:VW], 1.0)
            dve.memset(ones_bf[:, :], 1.0)
            dve.tensor_copy(before_bf[:, :], cst[:, C_PRE:C_PRE + P])
            dve.tensor_copy(base[:, :], cst[:, C_REG:C_REG + E]).then_inc(q["setup_dve"], 1)

            bank3v = bank[3][:, :].rearrange("p (m n) -> p m n", m=4)

            def tab_of(i, a):
                if isinstance(i, int):
                    return tab[:, (i // B) % 2, a, :]
                return tab[:, bass.ds((i // B) % 2, 1), a, :].rearrange("p c n -> p (c n)")

            R_STEPS, SLOT_STEPS = 32, 7

            def slot(i, u, route=None, head=True, tail=True):
                t = i - 1
                last = isinstance(i, int) and i == NCH - 1
                if tail:
                    dve.wait_ge(q["gn_pow_ready"], t + 1)
                    if some(t):
                        dve.wait_ge(q["nT_ready"], t)
                    dve.tensor_tensor(normed[:, :].rearrange("p (a h d) -> p a h d", a=2, h=HH),
                                      o_bank[:, :, 0:HH * VW].rearrange("p a (h w) -> p a h w", w=VW)[:, :, :, 0:VD],
                                      gn_pow[:, :].rearrange("p (a h) -> p a h", a=2).unsqueeze(3)
                                      .broadcast_to([P, 2, HH, VD]), ALU.mult).then_inc(q["normed_ready"], 1)
                if head:
                    dve.wait_ge(q["rot_in"], 16 * (i // B) + 16)
                    if some(i):
                        dve.wait_ge(q["kv_ready"], 2 * i)
                    dve.wait_ge(q["qk_taken"], i + 1)
                    for a in range(2):
                        dve.tensor_tensor(qk_rot[:, a::2], qk[:, 1 - a::2], tab_of(i, 1)[:, a::2], ALU.mult)\
                            .then_inc(q["rot_step"], 1)
                    if not last:
                        dve.wait_ge(q["x_in"], alone(dve, 16 * ((i + 1) // B) + 16))
                        dve.bn_stats(stats[:, 0, :], row(i + 1)).then_inc(q["ln1_step"], 1)
                    dve.wait_ge(q["rot_step"], 2 * i + 2)
                    dve.wait_ge(q["cos_ready"], i + 1)
                    dve.tensor_tensor(qk_rot[:, :], qk_rot[:, :], qk_cos[:, :], ALU.add).then_inc(q["rot_ready"], 1)
                    if not last:
                        dve.wait_ge(q["ln1_step"], alone(dve, 2 * i + 3))
                        dve.bn_aggr(mean_var[:, 0, :], stats[:, 0, :]).then_inc(q["ln1_step"], 1)
                if route is not None and u == 1:
                    pick_experts(route, 0)
                if head and not last:
                    dve.wait_ge(q["ln1_step"], 2 * i + 4)
                    dve.tensor_scalar(var_eps[:, 0:1], mean_var[:, 0, 1:2], EPS, None, ALU.add)\
                        .then_inc(q["ve1_ready"], 1)
                if tail:
                    dve.wait_ge(q["nT_ready"], t + 1)
                    dve.wait_ge(q["gT_taken"], t + 1)
                    dve.tensor_tensor(gated[:, :, :], bank[2][:, :].rearrange("p (m n) -> p m n", m=4),
                                      gate_silu[:, 1 - u % 2, :, :], ALU.mult).then_inc(q["nT_taken"], 1)
                if head and not last:
                    norm1(i + 1)
                if tail:
                    dve.wait_ge(q["wo_ready"], t + 1)
                    dve.tensor_tensor(row(t), bank[0][:, 0:D], row(t), ALU.add).then_inc(q["wo_taken"], 1)
                    dve.wait_ge(q["wo_taken"], alone(dve, t + 1))
                    norm_stats(row(t), 1, q["ln2_step"], q["ve2_ready"], t)
                if head:
                    for g in range(2):
                        mask(i, g)
                if tail:
                    dve.wait_ge(q["rstd2_ready"], t + 1)
                    if some(t // 2):
                        dve.wait_ge(xn2_stored[1 - u % 2], 16 * (t // 2))
                    dve.tensor_scalar(xn2[:, 1 - u % 2, :], row(t), mean_var[:, 1, 0:1], rstd[:, 1:2],
                                      ALU.subtract, ALU.mult).then_inc(q["xn2_ready"], 1)
                if head:
                    for g in range(2, 4):
                        mask(i, g)
                if tail:
                    dve.wait_ge(q["h1_taken"], t + 1)
                    if some(t):
                        dve.wait_ge(q["y_ready"], t)
                    for k in range(2):
                        h = dve.scalar_tensor_tensor(sh_hT[:, k, :], bank3v[:, 2 + k, :], bs_col[:, 2 + k:3 + k],
                                                     sh_silu[:, k, :], ALU.add, ALU.mult)
                    h.then_inc(q["h3_taken"], 1)
                if route is not None and 2 <= u <= 5:
                    pick_experts(route, u - 1)
                if route is not None and u == SLOTS_AT:
                    slots_of(route)
                if head:
                    sq = squares[:, :, :].rearrange("p a (h w) -> p (a h) w", w=VW)
                    dve.wait_ge(q["o_squared"], i + 1)
                    dve.scalar_tensor_tensor(gn[:, 0, :], sq[:, :, VD], EPS, floor_of(i), ALU.mult, ALU.max)\
                        .then_inc(q["gn_step"], 1)
                    dve.tensor_reduce(gn[:, 1, :], sq[:, :, 0:VD], AX, ALU.add).then_inc(q["gn_step"], 1)
                    dve.wait_ge(q["gn_step"], 2 * i + 2)
                    if some(i):
                        dve.wait_ge(q["gn_pow_ready"], i)
                    dve.scalar_tensor_tensor(gn[:, 2, :], gn[:, 1, :], 1.0 / VD, gn[:, 0, :], ALU.mult, ALU.add)\
                        .then_inc(q["gn_ve_ready"], 1)
                    dve.wait_ge(q["state_ready"], i + B)
                    for half in range(2):
                        dve.wait_ge(q["kv_ready"], 2 * i + half + 1)
                        dve.tensor_tensor(kv_new[:, half, :], bank[half][:, 0:HH * VW], block, ALU.mult)\
                            .then_inc(q["kv_taken"], 1)
                if tail:
                    dve.wait_ge(q["y_ready"], t + 1)
                    if route is not None and u == 1:
                        dve.wait_ge(q["shift_ready"], route + 1)
                    dve.tensor_copy(lg[:, (u - 1) % B, :], bank[2][:, D:D + E])
                    y = dve.tensor_tensor(row(t), bank[2][:, 0:D], row(t), ALU.add)
                    if route is not None and u == COUNTS_AT:
                        take_counts(route)
                    else:
                        y.then_inc(q["y_taken"], 1)

            def floor_of(i):
                if isinstance(i, int):
                    return floor_tab[:, i // B, :]
                return floor_tab[:, bass.ds(i // B, 1), :].rearrange("p c h -> p (c h)")

            def mask(i, g):
                dve.wait_ge(q["s_ready"], 4 * i + g + 1)
                if g == 0 and some(i):
                    dve.wait_ge(q["o_ready"], i)
                dve.tensor_tensor(probs[:, g, :, :, :].rearrange("p h e s -> p (h e) s"),
                                  s_bank[g % 2][:, :].rearrange("p (h s) -> p h s", h=4),
                                  causal.unsqueeze(1).broadcast_to([P, 4, P]), ALU.mult).then_inc(q["s_taken"], 1)

            def wide(v):
                return v.unsqueeze(2).broadcast_to([P, B, E])

            def flat(v):
                return v.rearrange("p c g -> p (c g)")

            FIRST_STEP = (0, 1, 9, 17, 24)

            def pick_experts(c, part):
                m = [FIRST_STEP[part]]

                def nxt(ins):
                    m[0] += 1
                    ins.then_inc(q["route_step"], 1)
                    dve.wait_ge(q["route_step"], R_STEPS * c + m[0])

                by_e = cst[:, C_IOM:C_IOM + E].unsqueeze(1).broadcast_to([P, B, E])
                in_groups = "p c (g e) -> p (c g) e"
                soft, score, left, left2, tmp = (r32[:, k, :, :] for k in (2, 3, 4, 5, 0))
                sg, lg4 = score.rearrange(in_groups, g=G), left.rearrange(in_groups, g=G)

                def pick_best(pick, v):
                    nxt(dve.tensor_reduce(r1[:, 3, :], v, AX, ALU.max))
                    nxt(dve.tensor_tensor(tmp, v, wide(r1[:, 3, :]), ALU.is_equal))
                    nxt(dve.tensor_tensor(tmp, tmp, by_e, ALU.mult))
                    nxt(dve.tensor_reduce(r1[:, 4, :], tmp, AX, ALU.min))
                    nxt(dve.tensor_tensor(pick[:, :, :], by_e, wide(r1[:, 4, :]), ALU.is_equal))

                if part == 0:
                    dve.wait_ge(q["y_taken"], B * c + B)
                    nxt(dve.tensor_reduce(r1[:, 0, :], lg[:, :, :], AX, ALU.max))
                    dve.tensor_tensor(r32[:, 0, :, :], lg[:, :, :], wide(r1[:, 0, :]), ALU.subtract)\
                        .then_inc(q["shift_ready"], 1)
                elif part == 1:
                    dve.wait_ge(q["exp_ready"], c + 1)
                    nxt(dve.tensor_reduce(r1[:, 1, :], r32[:, 1, :, :], AX, ALU.add))
                    nxt(dve.reciprocal(r1[:, 2, :], r1[:, 1, :]))
                    nxt(dve.tensor_tensor(soft, r32[:, 1, :, :], wide(r1[:, 2, :]), ALU.mult))
                    nxt(dve.tensor_tensor(score, soft, gb_bc[:, :].unsqueeze(1).broadcast_to([P, B, E]), ALU.add))
                    high = r16[:, 0:2, :, :].rearrange("p a c g -> p (a c g)").rearrange("p (n e) -> p n e", e=2)
                    low = r16[:, 2:4, :, :].rearrange("p a c g -> p (a c g)").rearrange("p (n e) -> p n e", e=2)
                    dve.tensor_tensor(high, sg[:, :, 0::2], sg[:, :, 1::2], ALU.max)
                    nxt(dve.tensor_tensor(low, sg[:, :, 0::2], sg[:, :, 1::2], ALU.min))
                    dve.tensor_tensor(flat(r8[:, 0, :, :]), high[:, :, 0], high[:, :, 1], ALU.max)
                    dve.tensor_tensor(flat(r8[:, 1, :, :]), high[:, :, 0], high[:, :, 1], ALU.min)
                    nxt(dve.tensor_tensor(flat(r8[:, 2, :, :]), low[:, :, 0], low[:, :, 1], ALU.max))
                    nxt(dve.tensor_tensor(r8[:, 3, :, :], r8[:, 1, :, :], r8[:, 2, :, :], ALU.max))
                    nxt(dve.tensor_tensor(r8[:, 4, :, :], r8[:, 0, :, :], r8[:, 3, :, :], ALU.add))
                elif part == 2:
                    mine = r8[:, 4, :, :].unsqueeze(3).broadcast_to([P, B, G, G])
                    other = r8[:, 4, :, :].unsqueeze(2).broadcast_to([P, B, G, G])
                    higher, same = r_cmp[:, 0, :, :, :], r_cmp[:, 1, :, :, :]
                    dve.tensor_tensor(higher, other, mine, ALU.is_gt)
                    nxt(dve.tensor_tensor(same, other, mine, ALU.is_equal))
                    nxt(dve.tensor_tensor(same, same, group_lt.unsqueeze(1).broadcast_to([P, B, G, G]), ALU.mult))
                    nxt(dve.tensor_tensor(higher, higher, same, ALU.add))
                    nxt(dve.tensor_reduce(r8[:, 5, :, :], higher, AX, ALU.add))
                    nxt(dve.tensor_scalar(r8[:, 6, :, :], r8[:, 5, :, :], float(TOPK_G), None, ALU.is_lt))
                    nxt(dve.tensor_scalar(r8[:, 7, :, :], r8[:, 6, :, :], -1.0, BIG, ALU.add, ALU.mult))
                    per_e = lambda k: flat(r8[:, k, :, :]).unsqueeze(2).broadcast_to([P, B * G, E // G])
                    nxt(dve.tensor_tensor(lg4, sg, per_e(6), ALU.mult))
                    nxt(dve.tensor_tensor(lg4, lg4, per_e(7), ALU.add))
                elif part == 3:
                    pick_best(pick1, left)
                    nxt(dve.scalar_tensor_tensor(left2, pick1[:, :, :], -BIG, left, ALU.mult, ALU.add))
                    nxt(dve.tensor_tensor(left, soft, pick1[:, :, :], ALU.mult))
                else:
                    pick_best(pick2, left2)
                    dve.tensor_tensor(picks_bf[:, :, :], pick1[:, :, :], pick2[:, :, :], ALU.add)\
                        .then_inc(q["picks_ready"], 1)
                    nxt(dve.tensor_tensor(left2, soft, pick2[:, :, :], ALU.mult))
                    w_at = all_w[:, c, :, :] if isinstance(c, int) else \
                        all_w[:, bass.ds(c, 1), :, :].rearrange("p n k c -> p (n k) c")
                    nxt(dve.tensor_reduce(w_at[:, 0, :], left, AX, ALU.add))
                    nxt(dve.tensor_reduce(w_at[:, 1, :], left2, AX, ALU.add))
                want = (FIRST_STEP + (R_STEPS,))[part + 1]
                assert m[0] == want, (part, m[0])

            def slot_next(c, k, ins):
                ins.then_inc(q["slot_step"], 1)
                dve.wait_ge(q["slot_step"], SLOT_STEPS * c + k)

            def take_counts(c):
                slot_next(c, 1, dve.tensor_tensor(
                    r32[:, 0, :, :], bank[2][:, 272:272 + B * E].rearrange("p (c e) -> p c e", c=B),
                    base[:, :].unsqueeze(1).broadcast_to([P, B, E]), ALU.add))
                dve.tensor_tensor(base[:, :], bank[2][:, 272 + B * E:272 + (B + 1) * E], base[:, :], ALU.add)\
                    .then_inc(q["y_taken"], 1)

            def slots_of(c):
                for k, pick in ((0, pick1), (1, pick2)):
                    slot_next(c, 2 + 2 * k, dve.tensor_tensor(r32[:, 1, :, :], r32[:, 0, :, :], pick[:, :, :], ALU.mult))
                    slot_next(c, 3 + 2 * k, dve.tensor_reduce(slot_f[:, k, :], r32[:, 1, :, :], AX, ALU.add))
                if some(c):
                    dve.wait_ge(q["scattered"], 32 * B * c)
                slot_next(c, 6, dve.tensor_copy(slot_i[:, :, :], slot_f[:, :, :]))
                slot_next(c, 7, dve.tensor_scalar(token_i[:, :], token_i[:, :], float(B * P), None, ALU.add))
                at = all_slots[:, c, :, :] if isinstance(c, int) else \
                    all_slots[:, bass.ds(c, 1), :, :].rearrange("p n k c -> p (n k) c")
                dve.tensor_copy(at, slot_f[:, :, :]).then_inc(q["slots_ready"], 1)

            dve.wait_ge(q["setup_step"], n[0])
            dve.wait_ge(q["setup_pool"], 1)
            dve.wait_ge(q["part_out"], 48)
            dve.wait_ge(q["zero_in"], 16)
            slot(0, 0, tail=False)
            for i in range(1, B + 1):
                slot(i, i % B)
            with dve.Fori(1, NCH // B - 1) as c:
                for u in range(1, B + 1):
                    slot(B * c + u, u % B, route=c - 1)
            for u in range(1, B + 1):
                slot(NCH - B + u, u % B, route=NCH // B - 2, head=u < B)
            for part in range(5):
                pick_experts(NCH // B - 1, part)
            dve.wait_ge(q["y_ready"], NCH + 1)
            take_counts(NCH // B - 1)
            slots_of(NCH // B - 1)

            n[0] = 0

            def tile_next(ins):
                n[0] += 1
                ins.then_inc(q["tile_step"], 1)
                dve.wait_ge(q["tile_step"], n[0])

            nt = n_tiles
            dve.wait_ge(q["y_taken"], NCH + 1)
            tile_next(dve.tensor_tensor(nt[:, 0, :], base[:, :], cst[:, C_REG:C_REG + E], ALU.subtract))
            tile_next(dve.tensor_scalar(nt[:, 0, :], nt[:, 0, :], float(P - 1), None, ALU.add))
            tile_next(dve.tensor_copy(n_tiles_i[:, 0, :], nt[:, 0, :]))
            tile_next(dve.tensor_scalar(n_tiles_i[:, 1, :], n_tiles_i[:, 0, :], 7, None, ALU.arith_shift_right))
            tile_next(dve.tensor_copy(nt[:, 1, :], n_tiles_i[:, 1, :]))
            tile_next(dve.memset(nt[:, 3, :], 1.0))
            tile_next(dve.tensor_tensor_scan(nt[:, 2, :], nt[:, 3, :], nt[:, 1, :], 0.0, ALU.mult, ALU.add))
            tiles = cst[0:1, C_TILE:C_TILE + NT]
            per_tile = lambda v: v.unsqueeze(1).broadcast_to([1, NT, E])
            tile_next(dve.tensor_tensor(tile_cmp, tiles.unsqueeze(2).broadcast_to([1, NT, E]),
                                        per_tile(nt[0:1, 2, :]), ALU.is_ge))
            tile_next(dve.tensor_reduce(tile_e[:, 0, :], tile_cmp, AX, ALU.add))
            tile_next(dve.tensor_tensor(tile_cmp, tile_cmp, per_tile(nt[0:1, 1, :]), ALU.mult))
            tile_next(dve.tensor_reduce(tile_e[:, 1, :], tile_cmp, AX, ALU.add))
            tile_next(dve.tensor_tensor(tile_e[:, 2, :], tiles, tile_e[:, 1, :], ALU.subtract))
            tile_next(dve.tensor_scalar(tile_e[:, 2, :], tile_e[:, 2, :], float(P), None, ALU.mult))
            tile_next(dve.scalar_tensor_tensor(tile_e[:, 2, :], tile_e[:, 0, :], float(REG), tile_e[:, 2, :],
                                               ALU.mult, ALU.add))
            tile_next(dve.tensor_copy(tile_row[:, :], tile_e[:, 2, :]))
            dve.wait_ge(q["scattered"], 32 * NCH)
            for par in range(2):
                dve.wait_ge(xn2_stored[par], 16 * (NCH // 2))
            dve.tensor_scalar(tile_exp[:, :], tile_e[:, 0, :], float(E - 1), None, ALU.min).then_inc(q["tiles_ready"], 1)

            tile_next(dve.tensor_scalar(nt[:, 3, :], nt[:, 1, :], float(P), -float(REG), ALU.mult, ALU.add))
            slots = all_slots[:, :, :, :].rearrange("p n k c -> p (n k c)")
            dve.tensor_copy(slot_sum[:, :], slots).then_inc(q["row_step"], 1)

            def shrink(e):
                limit, less = (cst[:, C_REG + e:C_REG + e + 1], nt[:, 3, e - 1:e]) if isinstance(e, int) else \
                    (cst[:, bass.ds(C_REG + e, 1)], nt[:, 3, bass.ds(e - 1, 1)])
                dve.tensor_scalar(slot_shift[:, :], slots, limit, less, ALU.is_ge, ALU.mult).then_inc(q["row_step"], 1)
                dve.wait_ge(q["row_step"], 2 * e)
                dve.tensor_tensor(slot_sum[:, :], slot_shift[:, :], slot_sum[:, :], ALU.add).then_inc(q["row_step"], 1)

            def step(t, u, turn, stages=(1, 2)):
                par = u % 2
                if 1 in stages:
                    dve.wait_ge(q["t_h_silu"], t)
                    if some(t - 2):
                        dve.wait_ge(q["t_ht_ready"], t - 2)
                    dve.tensor_tensor(tile_h[1 - par][:, :], bank[2 + 1 - par][:, INTER:D], tile_silu[1 - par][:, :],
                                      ALU.mult).then_inc(q["t_h_taken"], 1)
                if 2 in stages:
                    dve.wait_ge(q["t_ht_ready"], t - 1)
                    if some(t - 3):
                        dve.wait_ge(q["t_y_ready"], t - 3)
                    dve.tensor_copy(tile_hT[par][:, :], s_bank[par][:, 0:P]).then_inc(q["t_ht_taken"], 1)

            for t in range(4):
                step(t, t, 0, stages=[s for s in (1, 2) if s <= t])
            with dve.Fori(1, E) as j:
                for u in range(4):
                    step(4 * j + u, u, j)
                shrink(j)
            with dve.Fori(E, NT // 4) as j:
                for u in range(4):
                    step(4 * j + u, u, j)
            for t in range(NT, NT + 2):
                step(t, t % 4, t // 4, stages=[s for s in (1, 2) if s > t - NT])

            def add_pair(c, p, j):
                for b in (2 * p, 2 * p + 1):
                    u = b % 4
                    at = row(B * c + b)
                    for k in range(2):
                        w = all_w[:, c, k, b:b + 1] if isinstance(c, int) else \
                            all_w[:, bass.ds(c, 1), k, b:b + 1].rearrange("p n c -> p (n c)")
                        if k == 0:
                            dve.wait_ge(picked_in[u], 32 * j + 32)
                        o = dve.scalar_tensor_tensor(at, picked[u][:, k, :], w, at, ALU.mult, ALU.add)
                        if k == 0:
                            o.then_inc(q["sum_step"], 1)
                            dve.wait_ge(q["sum_step"], B * c + b + 1)
                        else:
                            o.then_inc(q["sum_done"], 1)

            def indices(c):
                at = slot_sum[:, c * 2 * B:(c + 1) * 2 * B] if isinstance(c, int) else \
                    slot_sum[:, bass.ds(c * 2 * B, 2 * B)]
                dve.tensor_copy(idx[:, :, :].rearrange("p k b -> p (k b)"), at).then_inc(q["idx_ready"], 1)

            dve.wait_ge(q["row_step"], 2 * E - 1)
            indices(0)
            with dve.Fori(0, S // P - 1) as c:
                for p in range(4):
                    add_pair(c, p, 2 * c + p // 2)
                indices(c + 1)
            for p in range(4):
                add_pair(S // P - 1, p, 2 * (S // P - 1) + p // 2)

        @blk.gpsimd
        def _(pool):
            pool.iota(token_i[:, :], pattern=[[P, B]], base=-B * P, channel_multiplier=1).then_inc(q["setup_pool"], 1)
            pool.memset(state[:, :, :, :], 0.0).then_inc(q["state_ready"], B)
            pool.wait_ge(q["state_ready"], B)

            def rstd_of(w, ready):
                pool.tensor_tensor(rstd[:, w:w + 1], var_eps[:, w:w + 1], half_neg[:, 0:1], ALU.pow).then_inc(ready, 1)

            def tab_of(i, a):
                if isinstance(i, int):
                    return tab[:, (i // B) % 2, a, :]
                return tab[:, bass.ds((i // B) % 2, 1), a, :].rearrange("p c n -> p (c n)")

            def slot(i, u, scatter_of=None, head=True, tail=True):
                t = i - 1
                last = isinstance(i, int) and i == NCH - 1
                if head:
                    pool.wait_ge(q["rot_in"], 16 * (i // B) + 16)
                    if some(i):
                        pool.wait_ge(q["rot_ready"], i)
                    pool.wait_ge(q["qk_taken"], i + 1)
                    pool.tensor_tensor(qk_cos[:, :], qk[:, :], tab_of(i, 0), ALU.mult).then_inc(q["cos_ready"], 1)
                    if not last:
                        pool.wait_ge(q["ve1_ready"], i + 2)
                        rstd_of(0, q["rstd1_ready"])
                scatters = scatter_of is not None and (u - SCATTERS_AT) % B < 2
                first = 4 * ((u - SCATTERS_AT) % B)
                if scatters:
                    scatter(scatter_of, first)
                if tail:
                    pool.wait_ge(q["ve2_ready"], t + 1)
                    rstd_of(1, q["rstd2_ready"])
                if scatters:
                    for b in range(first + 1, first + 4):
                        scatter(scatter_of, b)
                if head:
                    pool.wait_ge(q["gn_ve_ready"], i + 1)
                    if some(i):
                        pool.wait_ge(q["normed_ready"], i)
                    pool.tensor_tensor(gn_pow[:, :], gn[:, 2, :], half_neg[:, :], ALU.pow)\
                        .then_inc(q["gn_pow_ready"], 1)
                    pool.wait_ge(q["kv_taken"], 2 * i + 2)
                    st = state[:, u, :, :].rearrange("p a n -> p (a n)")
                    pool.tensor_tensor(st, st, kv_new[:, :, :].rearrange("p a n -> p (a n)"), ALU.add)\
                        .then_inc(q["state_ready"], 1)

            def scatter(c, b):
                pool.wait_ge(q["slots_ready"], alone(pool, c + 1))
                for k in range(2):
                    pool.indirect_dma_start(
                        out=slot_token, out_offset=bass.IndirectOffsetOnAxis(ap=slot_i[:, k, b:b + 1], axis=0),
                        in_=token_i[:, b:b + 1], in_offset=None).then_inc(q["scattered"], 16)

            pool.wait_ge(q["ve1_ready"], 1)
            rstd_of(0, q["rstd1_ready"])
            slot(0, 0, tail=False)
            for i in range(1, B + 1):
                slot(i, i % B)
            pool.wait_ge(q["zero_in"], 16)
            with pool.Fori(1, NCH // B - 1) as c:
                for u in range(1, B + 1):
                    slot(B * c + u, u % B, scatter_of=c - 1)
            for u in range(1, B + 1):
                slot(NCH - B + u, u % B, scatter_of=NCH // B - 2, head=u < B)
            for b in range(B):
                scatter(NCH // B - 1, b)

            def gather(t, u, turn):
                pool.wait_ge(id_in[u], alone(pool, 16 * turn + 16))
                if some(t - 3):
                    pool.wait_ge(q["t_x_ready"], alone(pool, t - 3))
                pool.indirect_dma_start(
                    out=tile_x[u][:, :], out_offset=None, in_=xn2_rows,
                    in_offset=bass.IndirectOffsetOnAxis(ap=tile_id[u][:, 0:1], axis=0)).then_inc(row_in[u], 16)

            pool.wait_ge(q["tiles_ready"], 1)
            for t in range(4):
                gather(t, t, 0)
            with pool.Fori(1, NT // 4) as j:
                for u in range(4):
                    gather(4 * j + u, u, j)

            for par in range(2):
                pool.wait_ge(y_out[par], 16 * (NT // 2))

            def gather_chunk(c, b, turn):
                pool.wait_ge(q["idx_ready"], alone(pool, c + 1))
                if some(turn) or b >= 4:
                    pool.wait_ge(q["sum_done"], alone(pool, B * c + b - 3))
                for k in range(2):
                    pool.indirect_dma_start(
                        out=picked[b % 4][:, k, :], out_offset=None, in_=y_rows,
                        in_offset=bass.IndirectOffsetOnAxis(ap=idx[:, k, b:b + 1], axis=0))\
                        .then_inc(picked_in[b % 4], 16)

            for b in range(B):
                gather_chunk(0, b, b // 4)
            with pool.Fori(1, S // P) as c:
                for b in range(B):
                    gather_chunk(c, b, 1)


_INS = ["L0_attn_x", "L0_attn_Wq", "L0_attn_bq", "L0_attn_Wk", "L0_attn_bk", "L0_attn_Wv", "L0_attn_bv", "L0_attn_Wg",
        "L0_attn_bg", "L0_attn_Wo", "L0_attn_bo", "L0_ffn_gate_w", "L0_ffn_gate_b", "L0_ffn_We1", "L0_ffn_be1",
        "L0_ffn_We2", "L0_ffn_be2", "L0_ffn_We3", "L0_ffn_be3", "L0_ffn_ws1", "L0_ffn_bs1", "L0_ffn_ws2",
        "L0_ffn_bs2", "L0_ffn_ws3", "L0_ffn_bs3"]


def kernel(**inputs):
    import numpy as _np
    import concourse.bacc as _bacc
    from concourse import mybir as _mybir
    from concourse.bass_utils import run_bass_kernel_spmd as _run

    nc = _bacc.Bacc("TRN2", target_bir_lowering=False, num_devices=1)
    arrays, args = {}, []

    def give(name, a):
        arrays[name] = a
        args.append(nc.dram_tensor(name, a.shape, _mybir.dt.from_np(a.dtype), kind="ExternalInput").ap())

    for name in _INS:
        give(f"in_{name}_dram", _np.ascontiguousarray(inputs[name]))
    for name, a in zip(("rotary", "floor", "const"), constants()):
        give(f"table_{name}_dram", a)
    out = nc.dram_tensor("out_0_dram", (B, S, D), F32, kind="ExternalOutput").ap()
    build(nc, *args, out)
    r = _run(nc, [arrays], core_ids=[0])
    return r.results[0]["out_0_dram"]
```

```python
from contextlib import ExitStack

import numpy as np

import concourse.bass as bass
from concourse import mybir

F32 = mybir.dt.float32
F32R = mybir.dt.float32r
BF16 = mybir.dt.bfloat16
I32 = mybir.dt.int32
ALU = mybir.AluOpType
ACT = mybir.ActivationFunctionType
AX = mybir.AxisListType.X

B, S, D = 8, 1024, 256
H, KD, VD = 16, 16, 32
HH = H // 2
VW = VD + 1
E, TOPK, G, TOPK_G, INTER = 16, 2, 4, 2, 128
P = 128
NCH = B * S // P
REG = B * S
NT = B * S * TOPK // P + E
SLOTS = E * REG + E * P
LAST_SLOT = SLOTS - P
ROWS = B * S * TOPK
EPS = 1e-5
BIG = 3.0e38

C_ID, C_CAUSAL, C_BLOCK = 0, 128, 256
C_HEAD = C_BLOCK + HH * VW
C_IOM = C_HEAD + HH
C_LT = C_IOM + E
C_REG = C_LT + G * G
C_PRE = C_REG + E
C_TILE = C_PRE + 128
C_SPARE = C_TILE + NT
C_N = C_SPARE + 1


def constants():
    f = np.float32
    angle = (f(1.0) / f(10000.0) ** np.linspace(0.0, 1.0, KD // 2, dtype=f)).astype(f)
    angle = np.repeat(angle, 2)
    pos = np.arange(S, dtype=f)
    turn = (pos[:, None] * angle[None, :]).astype(f).astype(np.float64)
    decay = np.log((1.0 - 2.0 ** (-5.0 - np.arange(H))).astype(f)).astype(f).astype(np.float64)
    grow = np.exp(decay[None, :] * (pos.astype(np.float64)[:, None] - S / 2))
    sign = np.where(np.arange(KD) % 2 == 0, -1.0, 1.0)
    parts = []
    for scale in (grow, KD ** -0.5 / grow):
        parts.append(((np.cos(turn))[:, None, :] * scale[:, :, None]).reshape(S, D))
    for scale in (grow, KD ** -0.5 / grow):
        parts.append(((np.sin(turn) * sign)[:, None, :] * scale[:, :, None]).reshape(S, D))
    rotary = np.concatenate(parts, 1).astype(f)
    floor = (EPS * np.cumsum(np.exp(decay[None, :] * np.arange(S)[:, None]), 0)).astype(f)

    c = np.zeros((P, C_N), f)
    i = np.arange(P)
    c[:, C_ID:C_ID + P] = np.eye(P)
    c[:, C_CAUSAL:C_CAUSAL + P] = i[None, :] >= i[:, None]
    c[:, C_BLOCK:C_BLOCK + HH * VW] = (i[:, None] // KD) == (np.arange(HH * VW)[None, :] // VW)
    c[:, C_HEAD:C_HEAD + HH] = (i[:, None] // KD) == np.arange(HH)[None, :]
    c[:, C_IOM:C_IOM + E] = np.arange(E) - E
    c[:, C_LT:C_LT + G * G] = (np.arange(G)[None, :] < np.arange(G)[:, None]).reshape(-1)
    c[:, C_REG:C_REG + E] = np.arange(E) * REG
    c[:, C_PRE:C_PRE + P] = i[:, None] < i[None, :]
    c[:, C_TILE:C_TILE + NT] = np.arange(NT)
    c[:, C_SPARE] = ROWS + (i // B) * P
    return rotary, floor, c


def some(n):
    return not isinstance(n, int) or n > 0


def build(nc, x, Wq, bq, Wk, bk, Wv, bv, Wg, bg, Wo, bo, gate_w, gate_b, We1, be1, We2, be2, We3, be3,
          ws1, bs1, ws2, bs2, ws3, bs3, rotary, floor, const, out):
    xn2_rows = nc.dram_tensor("xn2_rows", [B * S, D], F32, kind="Internal").ap()
    slot_table = nc.dram_tensor("slot_table", [SLOTS, 2], I32, kind="Internal").ap()
    y_rows = nc.dram_tensor("y_rows", [ROWS + 2 * E * P, D], F32, kind="Internal").ap()
    bias_parts = nc.dram_tensor("bias_parts", [3, E + 1, 512], BF16, kind="Internal").ap()

    with ExitStack() as ctx:
        def sb(name, shape, dt=F32, scope=ctx):
            return scope.enter_context(nc.sbuf_tensor(name, shape, dt))

        bank = [ctx.enter_context(nc.psum_tensor(f"bank{i}", [P, 512], F32)) for i in range(4)]
        s_bank = [ctx.enter_context(nc.psum_tensor(f"s_bank{i}", [P, 512], F32)) for i in range(2)]
        o_bank = ctx.enter_context(nc.psum_tensor("o_bank", [P, 2, 512], F32))
        score_bank = [s_bank[0][:, :], s_bank[1][:, :], o_bank[:, 0, :], o_bank[:, 1, :]]

        cst = sb("cst", [P, C_N])
        stream = sb("stream", [P, NCH, D])
        ones_bf = sb("ones_bf", [P, P], BF16)
        base = sb("base", [P, E])
        all_w = sb("all_w", [P, NCH // B, 2, B])
        n_tiles = sb("n_tiles", [P, 4, E])
        tile_row = sb("tile_row", [1, NT], I32)
        tile_exp = sb("tile_exp", [1, NT], I32)

        with ExitStack() as first:
            def sa(name, shape, dt=F32):
                return sb(name, shape, dt, first)

            wqk = sa("wqk", [P, 2, 2, 512], F32R)
            wv = sa("wv", [P, 2, 2, 512], F32R)
            wg = sa("wg", [P, 2, 512])
            wo = sa("wo", [P, 2, 4, D], F32R)
            ws13 = sa("ws13", [P, 2, 512])
            ws2_sb = sa("ws2_sb", [P, 2, D])
            gw = sa("gw", [P, 2, E])
            bias_qkv = sa("bias_qkv", [3, 2, 512], BF16)
            bg_col = sa("bg_col", [P, 4])
            bs_col = sa("bs_col", [P, 4])
            bias_o = sa("bias_o", [3, 512], BF16)
            tab = sa("tab", [P, 2, 2, 512])
            floor_tab = sa("floor_tab", [P, S // P, H])
            vmean = sa("vmean", [P, 2, H])
            vmean_b = sa("vmean_b", [3, H])
            state = sa("state", [P, B, 2, HH * VW])
            xn = sa("xn", [P, D])
            xnT = sa("xnT", [P, 2, P])
            xnT_r = sa("xnT_r", [P, 2, 2, P], F32R)
            qk = sa("qk", [P, 512])
            qk_cos = sa("qk_cos", [P, 512])
            qk_rot = sa("qk_rot", [P, 512])
            qkT = sa("qkT", [P, 4, P])
            q_split = sa("q_split", [P, 2, HH, P])
            val = sa("val", [P, H, VW])
            gate_silu = sa("gate_silu", [P, 2, 4, P])
            probs = sa("probs", [P, 4, 2, 2, P])
            squares = sa("squares", [P, 2, HH * VW])
            normed = sa("normed", [P, H * VD])
            gated = sa("gated", [P, 4, P])
            gated_r = sa("gated_r", [P, 2, 4, P], F32R)
            kv_new = sa("kv_new", [P, 2, HH * VW])
            stats = sa("stats", [P, 2, 6])
            mean_var = sa("mean_var", [P, 2, 2])
            var_eps = sa("var_eps", [P, 2])
            rstd = sa("rstd", [P, 2])
            half_neg = sa("half_neg", [P, H])
            gn = sa("gn", [P, 3, H])
            gn_pow = sa("gn_pow", [P, H])
            xn2 = sa("xn2", [P, 2, D])
            xn2T = sa("xn2T", [P, 2, P])
            sh_silu = sa("sh_silu", [P, 2, P])
            sh_hT = sa("sh_hT", [P, 2, P])
            gb_bc = sa("gb_bc", [P, E])
            before_bf = sa("before_bf", [P, P], BF16)
            lg = sa("lg", [P, B, E])
            r8 = sa("r8", [P, 8, B, G])
            r16 = sa("r16", [P, 4, B, G])
            r32 = sa("r32", [P, 6, B, E])
            r_cmp = sa("r_cmp", [P, 2, B, G, G])
            r1 = sa("r1", [P, 5, B])
            pick1 = sa("pick1", [P, B, E])
            pick2 = sa("pick2", [P, B, E])
            picks_bf = sa("picks_bf", [P, B, E], BF16)
            slot_f = sa("slot_f", [P, 2, B])
            slot_i = sa("slot_i", [P, 2, B], I32)
            token_i = sa("token_i", [P, 2, B, 2], I32)
            tile_e = sa("tile_e", [1, 3, NT])
            scratch = sa("scratch", [P, NT * E])
            n_tiles_i = sa("n_tiles_i", [P, 2, E], I32)

        with ExitStack() as second:
            def sc(name, shape, dt=F32):
                return sb(name, shape, dt, second)

            w13 = sc("w13", [P, 2, E, 2 * INTER])
            w2 = sc("w2", [P, E, D])
            bias_e = sc("bias_e", [3, E, 512], BF16)
            tile_id = [sc(f"tile_id{u}", [P, 2], I32) for u in range(8)]
            tile_dest = [sc(f"tile_dest{u}", [P, 1], I32) for u in range(8)]
            tile_x = [sc(f"tile_x{u}", [P, D]) for u in range(4)]
            tile_xT = [sc(f"tile_xT{u}", [P, 2, P]) for u in range(2)]
            tile_silu = [sc(f"tile_silu{u}", [P, INTER]) for u in range(2)]
            tile_h = [sc(f"tile_h{u}", [P, INTER]) for u in range(2)]
            tile_hT = [sc(f"tile_hT{u}", [P, P]) for u in range(2)]
            tile_y = [sc(f"tile_y{u}", [P, D]) for u in range(4)]
            picked = [sc(f"picked{u}", [P, 2, 4, D]) for u in range(4)]

        ident = cst[:, C_ID:C_ID + P]
        causal = cst[:, C_CAUSAL:C_CAUSAL + P]
        block = cst[:, C_BLOCK:C_BLOCK + HH * VW]
        group_lt = cst[:, C_LT:C_LT + G * G].rearrange("p (g k) -> p g k", g=G)

        names = """const_in rot_in x_in w_in b_in expert_in brow_in part_out bias_in zero_in
            setup_step parts_ready setup_dve zeros_ready setup_pool
            xnT_ready xnT_taken xnT_left w_rounded gated_rounded gated_left
            qk_ready qk_taken v_ready v_taken gT_ready gT_taken qkT_ready
            s_ready s_taken o_ready o_squared kv_ready kv_taken state_ready
            nT_ready nT_taken wo_ready wo_taken xn2T_ready xn2T_taken h13_ready h1_taken h3_taken y_ready y_taken
            cos_ready rot_step rot_ready ln1_step ve1_ready rstd1_ready xn_ready gn_step gn_ve_ready gn_pow_ready
            normed_ready ln2_step ve2_ready qsplit_ready qcopy_ready rstd2_ready xn2_ready
            route_step shift_ready exp_ready picks_ready slot_step slots_ready scattered
            tile_step tiles_ready second_in
            t_x_ready t_x_taken t_h_ready t_h_silu t_h_taken t_ht_ready t_ht_taken t_y_ready t_y_taken
            dest_ready sum_step sum_done out_done""".split()
        q = {n: ctx.enter_context(nc.semaphore(n)) for n in names}

        def each(name, n):
            return [ctx.enter_context(nc.semaphore(f"{name}{u}")) for u in range(n)]

        xn2_stored = each("xn2_stored", 2)
        id_in, row_in, y_out, picked_in = each("id_in", 8), each("row_in", 4), each("y_out", 4), each("picked_in", 4)

        blk = ctx.enter_context(nc.Block())
        W_DMAS, B_DMAS = 10, 8
        tile_cmp = scratch[0:1, :].rearrange("p (t e) -> p t e", e=E)
        wqk_f = scratch[:, 0:2 * 512].rearrange("p (k n) -> p k n", k=2)
        wv_f = scratch[:, 2 * 512:4 * 512].rearrange("p (k n) -> p k n", k=2)
        wo_f = q_split[:, 1, :, :].rearrange("p h n -> p (h n)").rearrange("p (k n) -> p k n", k=4)
        brows = squares[0:E + 1, :, :].rearrange("p a n -> p (a n)")[:, 0:512]
        bres = normed[0:E + 1, :]
        bpart = gate_silu[0:E + 1, :, :, :].rearrange("p a m n -> p (a m n)").bitcast(BF16)[:, 0:3 * 512]\
            .rearrange("p (k n) -> p k n", k=3)
        bias_f = q_split[0:3, 0, :, :].rearrange("p h n -> p (h n)").rearrange("p (a n) -> p a n", a=2)
        bpart3 = gated[0:3, :, :].rearrange("p m n -> p (m n)").bitcast(BF16).rearrange("p (a n) -> p a n", a=1)
        bsum = xn2[0:3, :, :].rearrange("p a n -> p (a n)").bitcast(BF16)
        per_part = E * REG // P
        fill = probs[:, :, :, :, :].rearrange("p g h e s -> p (g h e s)").bitcast(I32)\
            .rearrange("p (n a) -> p n a", a=2)
        fill_spare = kv_new[:, :, :].rearrange("p a n -> p (a n)").bitcast(I32)[:, 0:2 * E]\
            .rearrange("p (n a) -> p n a", a=2)

        def alone(eng, count):
            if not isinstance(count, int):
                eng.to_reg(count)
            eng.wait_ge(q["const_in"], 16)
            return count

        COS_POOL = 256
        COUNTS_AT, SLOTS_AT, SCATTERS_AT = 5, 6, 7

        @blk.sync
        def _(sp):
            sp.dma_start(cst[:, :], const).then_inc(q["const_in"], 16)
            by_pos = x.rearrange("b (c p) d -> c p b d", p=P)
            sp.dma_start(stream[:, 0:B, :], by_pos[0]).then_inc(q["x_in"], 16)
            for dst, src in ((brows[0:E, 0:INTER], be1), (brows[0:E, INTER:D], be3), (brows[0:E, D:512], be2),
                             (brows[E:E + 1, 0:D], bo.rearrange("(a n) -> a n", a=1)),
                             (brows[E:E + 1, D:512], bs2.rearrange("(a n) -> a n", a=1))):
                sp.dma_start(dst, src).then_inc(q["brow_in"], 16)
            for dst, src in ((bg_col[:, :], bg), (bs_col[:, 0:2], bs1), (bs_col[:, 2:4], bs3)):
                sp.dma_start(dst, src.rearrange("(m p) -> p m", p=P),
                             allow_slow_non_contiguous=True).then_inc(q["b_in"], 16)
            for dst, src in ((bias_f[:, 0, 0:D], bq), (bias_f[:, 0, D:512], bk), (bias_f[:, 1, :], bv)):
                sp.dma_start(dst, src.partition_broadcast(3)).then_inc(q["b_in"], 16)
            sp.dma_start(gb_bc[:, :], gate_b.partition_broadcast(P)).then_inc(q["b_in"], 16)
            sp.dma_start(floor_tab[:, :, :], floor.rearrange("(c p) h -> p c h", p=P)).then_inc(q["b_in"], 16)
            kp = "(k p) n -> p k n"
            for dst, src in (
                (wqk_f[:, :, 0:D], Wq), (wqk_f[:, :, D:512], Wk), (wv_f, Wv), (wg[:, :, :], Wg),
                (wo_f, Wo), (ws13[:, :, 0:D], ws1), (ws13[:, :, D:512], ws3), (ws2_sb[:, :, :], ws2),
            ):
                sp.dma_start(dst, src.rearrange(kp, p=P)).then_inc(q["w_in"], 16)
            for k in range(2):
                sp.dma_start(gw[:, k, :], gate_w[:, k * P:(k + 1) * P].rearrange("e p -> p e"),
                             allow_slow_non_contiguous=True).then_inc(q["w_in"], 16)
            rot = rotary.rearrange("(c p) (a n) -> c p a n", p=P, a=2)
            for c in range(2):
                sp.dma_start(tab[:, c, :, :], rot[c]).then_inc(q["rot_in"], 16)
                sp.wait_ge(q["rot_in"], 16 * (c + 1))
            sp.wait_ge(q["parts_ready"], 1)
            for k in range(3):
                sp.dma_start(bias_parts[k], bpart[:, k, :]).then_inc(q["part_out"], 16)
            sp.wait_ge(q["part_out"], 48)
            sp.dma_start(bias_o[:, :], bias_parts[:, E, :]).then_inc(q["bias_in"], 16)
            sp.wait_ge(q["zeros_ready"], 1)
            sp.dma_start(slot_table[0:E * REG, :].rearrange("(p n) a -> p (n a)", p=P),
                         fill.rearrange("p n a -> p (n a)")).then_inc(q["zero_in"], 16)
            sp.dma_start(slot_table[E * REG:SLOTS, :].rearrange("(p n) a -> p (n a)", p=P),
                         fill_spare.rearrange("p n a -> p (n a)")).then_inc(q["zero_in"], 16)
            sp.wait_ge(q["x_in"], 16)
            for c in range(1, S // P):
                sp.dma_start(stream[:, c * B:(c + 1) * B, :], by_pos[c]).then_inc(q["x_in"], 16)
                sp.wait_ge(q["x_in"], 16 * (c + 1))

            def store(t, par):
                sp.wait_ge(q["xn2_ready"], alone(sp, t + 1))
                sp.dma_start(xn2_rows[bass.ds(t * P, P), :], xn2[:, par, :]).then_inc(xn2_stored[par], 16)

            for t in range(B):
                store(t, t % 2)
            with sp.Fori(0, S // P // 2 - 1) as j:
                for par in range(2):
                    sp.wait_ge(q["rot_ready"], alone(sp, (2 * j + par + 1) * B))
                    sp.dma_start(tab[:, par, :, :], rot[bass.ds(2 * j + par + 2, 1)].rearrange("c p a n -> (c p) a n"))\
                        .then_inc(q["rot_in"], 16)
                    for t in range(B):
                        store((2 * j + par + 1) * B + t, t % 2)
            for t in range(NCH - B, NCH):
                store(t, t % 2)

            sp.wait_ge(q["y_ready"], NCH)
            for k in range(2):
                sp.dma_start(w13[:, k, :, 0:INTER], We1.rearrange("e (k p) i -> k p e i", p=P)[k]).then_inc(q["expert_in"], 16)
                sp.dma_start(w13[:, k, :, INTER:D], We3.rearrange("e (k p) i -> k p e i", p=P)[k]).then_inc(q["expert_in"], 16)
            sp.dma_start(bias_e[:, :, :], bias_parts[:, 0:E, :]).then_inc(q["second_in"], 16)
            sp.dma_start(w2[:, :, :], We2.rearrange("e i d -> i e d")).then_inc(q["second_in"], 16)
            sp.wait_ge(q["tiles_ready"], 1)
            for u in range(8):
                row = sp.value_load(tile_row[0:1, u:u + 1], min_val=0, max_val=LAST_SLOT)
                sp.dma_start(tile_id[u][:, :], slot_table[bass.ds(row, P), :]).then_inc(id_in[u], 16)
            with sp.Fori(1, NT // 8) as j:
                for u in range(8):
                    row = sp.value_load(tile_row[0:1, bass.ds(8 * j + u, 1)], min_val=0, max_val=LAST_SLOT)
                    sp.wait_ge(row_in[u % 4], alone(sp, 16 * (2 * j - 1 + u // 4)))
                    sp.wait_ge(q["dest_ready"], alone(sp, 8 * j - 7 + u))
                    sp.dma_start(tile_id[u][:, :], slot_table[bass.ds(row, P), :]).then_inc(id_in[u], 16)
            for u in range(4):
                sp.wait_ge(y_out[u], 16 * (NT // 4))

            def load(g, u):
                for k in range(2):
                    sp.dma_start(picked[u][:, k, :, :],
                                 y_rows[bass.ds(g * 4 * P + k * B * S, 4 * P), :].rearrange("(b p) d -> p b d", p=P))\
                        .then_inc(picked_in[u], 16)

            for u in range(4):
                load(u, u)
            with sp.Fori(1, NCH // 16) as j:
                for u in range(4):
                    sp.wait_ge(q["sum_done"], alone(sp, 16 * j - 12 + 4 * u))
                    load(4 * j + u, u)

        @blk.tensor
        def _(pe):
            def norm_transpose():
                for k in range(2):
                    tr = pe.transpose(bank[3][:, k * P:(k + 1) * P], xn[:, k * P:(k + 1) * P], ident)
                tr.then_inc(q["xnT_ready"], 1)

            def split_product(out, lhs, rhs, left, count):
                first = True
                for a, b in ((0, 0), (0, 1), (1, 0)):
                    if a == 1:
                        pe.wait_ge(left, count)
                    for k in range(lhs.shape[2]):
                        pe.matmul(out, lhs[:, a, k, :], rhs[:, b, k, :], start=first, stop=False)
                        first = False

            def route_counts(c):
                pe.wait_ge(q["picks_ready"], c + 1)
                at = 272
                pe.matmul(bank[2][:, at:at + B * E], before_bf[:, :], picks_bf[:, :, :], start=True, stop=False)
                for b in range(1, B):
                    pe.matmul(bank[2][:, at + b * E:at + B * E], ones_bf[:, :], picks_bf[:, 0:B - b, :],
                              start=False, stop=(b == B - 1))
                for b in range(B):
                    mm = pe.matmul(bank[2][:, at + B * E:at + (B + 1) * E], ones_bf[:, :], picks_bf[:, b, :],
                                   start=(b == 0), stop=(b == B - 1))
                return mm

            def slot(i, u, counts_of=None, head=True, tail=True):
                t = i - 1
                if head:
                    if some(i):
                        pe.wait_ge(q["kv_taken"], 2 * i - 1)
                    pe.wait_ge(q["xnT_taken"], i + 1)
                    split_product(bank[0][:, :], xnT_r, wqk, q["xnT_left"], i + 1)
                    pe.matmul(bank[0][:, :], ones_bf[0:3, :], bias_qkv[:, 0, :], start=False, stop=True)\
                        .then_inc(q["qk_ready"], 1)
                    if some(i):
                        pe.wait_ge(q["kv_taken"], 2 * i)
                    split_product(bank[1][:, :], xnT_r, wv, q["xnT_left"], i + 1)
                    pe.matmul(bank[1][:, :], ones_bf[0:3, :], bias_qkv[:, 1, :], start=False, stop=True)\
                        .then_inc(q["v_ready"], 1)
                if head:
                    for m in range(3):
                        for k in range(2):
                            mm = pe.matmul(bank[3][:, m * P:(m + 1) * P], wg[:, k, m * P:(m + 1) * P], xnT[:, k, :],
                                           start=(k == 0), stop=(k == 1))
                    pe.wait_ge(q["v_taken"], i + 1)
                    pe.wait_ge(q["rot_ready"], i + 1)
                    for m in range(4):
                        tr = pe.transpose(bank[1][:, m * P:(m + 1) * P], qk_rot[:, m * P:(m + 1) * P], ident)
                    tr.then_inc(q["qkT_ready"], 1)
                    for k in range(2):
                        mm = pe.matmul(bank[3][:, 3 * P:4 * P], wg[:, k, 3 * P:4 * P], xnT[:, k, :],
                                       start=(k == 0), stop=(k == 1))
                    mm.then_inc(q["gT_ready"], 1)
                if tail:
                    if some(t):
                        pe.wait_ge(q["y_taken"], t)
                    pe.wait_ge(q["normed_ready"], t + 1)
                    for m in range(4):
                        tr = pe.transpose(bank[2][:, m * P:(m + 1) * P], normed[:, m * P:(m + 1) * P], ident)
                    tr.then_inc(q["nT_ready"], 1)
                if head:
                    for g in range(4):
                        scores(i, g)
                if tail:
                    if head:
                        pe.wait_ge(q["qk_taken"], i + 1)
                    else:
                        pe.wait_ge(q["kv_taken"], 2 * i - 1)
                    pe.wait_ge(q["gated_rounded"], t + 1)
                    split_product(bank[0][:, 0:D], gated_r, wo, q["gated_left"], t + 1)
                    pe.matmul(bank[0][:, 0:D], ones_bf[0:3, :], bias_o[:, 0:D], start=False, stop=True)\
                        .then_inc(q["wo_ready"], 1)
                if head:
                    pe.wait_ge(q["state_ready"], i + 1)
                    pe.wait_ge(q["qcopy_ready"], i + 1)
                    for half in range(2):
                        pe.wait_ge(q["s_taken"], 4 * i + 3 + half)
                        pe.matmul(o_bank[:, half, 0:HH * VW], qkT[:, half, :], state[:, u, half, :],
                                  start=True, stop=False)
                    from_chunk(0)
                    from_chunk(1, range(0, 2))
                if tail:
                    pe.wait_ge(q["xn2_ready"], t + 1)
                    for k in range(2):
                        tr = pe.transpose(bank[2][:, k * P:(k + 1) * P], xn2[:, 1 - u % 2, k * P:(k + 1) * P], ident)
                    tr.then_inc(q["xn2T_ready"], 1)
                    if head:
                        from_chunk(1, range(2, 5))
                        pe.wait_ge(q["gT_taken"], i + 1)
                    pe.wait_ge(q["xn2T_taken"], t + 1)
                    for m in range(4):
                        for k in range(2):
                            mm = pe.matmul(bank[3][:, m * P:(m + 1) * P], ws13[:, k, m * P:(m + 1) * P], xn2T[:, k, :],
                                           start=(k == 0), stop=(k == 1))
                    mm.then_inc(q["h13_ready"], 1)
                if head:
                    from_chunk(1, range(5 if tail else 2, HH)).then_inc(q["o_ready"], 1)
                if head:
                    if tail:
                        pe.wait_ge(q["wo_taken"], t + 1)
                    else:
                        pe.wait_ge(q["qk_taken"], i + 1)
                    for half in range(2):
                        if half == 1:
                            pe.wait_ge(q["qcopy_ready"], i + 1)
                        pe.matmul(bank[half][:, 0:HH * VW], qk_rot[:, D + half * P:D + (half + 1) * P],
                                  val[:, half * HH:(half + 1) * HH, :], start=True, stop=True)\
                            .then_inc(q["kv_ready"], 1)
                if tail:
                    pe.wait_ge(q["h3_taken"], t + 1)
                if head and not (isinstance(i, int) and i == NCH - 1):
                    if not tail:
                        pe.wait_ge(q["gT_taken"], i + 1)
                    pe.wait_ge(q["xn_ready"], i + 2)
                    norm_transpose()
                if tail:
                    for k in range(2):
                        pe.matmul(bank[2][:, D:D + E], xn2T[:, k, :], gw[:, k, :], start=(k == 0), stop=(k == 1))
                    for k in range(2):
                        pe.matmul(bank[2][:, 0:D], sh_hT[:, k, :], ws2_sb[:, k, :], start=(k == 0), stop=False)
                    mm = pe.matmul(bank[2][:, 0:D], ones_bf[0:3, :], bias_o[:, D:512], start=False, stop=True)
                    if counts_of is not None:
                        mm = route_counts(counts_of)
                    mm.then_inc(q["y_ready"], 1)

            def scores(i, g):
                if g < 2 and some(i):
                    pe.wait_ge(q["s_taken"], 4 * i - 2 + g)
                elif some(i):
                    pe.wait_ge(q["normed_ready"], i)
                pe.wait_ge(q["qsplit_ready"], 4 * i + g + 1)
                for half in range(2):
                    mm = pe.matmul(score_bank[g][:, half * 256:(half + 1) * 256], qkT[:, 2 + half, :],
                                   q_split[:, half, 2 * g:2 * g + 2, :], start=True, stop=True)
                mm.then_inc(q["s_ready"], 1)

            def from_chunk(half, heads=range(HH)):
                for h in heads:
                    mm = pe.matmul(o_bank[:, half, h * VW:(h + 1) * VW], probs[:, h // 2, half, h % 2, :],
                                   val[:, half * HH + h, :], start=False, stop=(h == HH - 1))
                return mm

            pe.wait_ge(q["const_in"], 16)
            pe.wait_ge(q["xn_ready"], 1)
            norm_transpose()
            pe.wait_ge(q["w_in"], 16 * W_DMAS)
            pe.wait_ge(q["setup_dve"], 1)
            slot(0, 0, tail=False)
            pe.wait_ge(q["bias_in"], 16)
            for i in range(1, B + 1):
                slot(i, i % B)
            with pe.Fori(1, NCH // B - 1) as c:
                for u in range(1, B + 1):
                    slot(B * c + u, u % B, counts_of=c - 1 if u == COUNTS_AT else None)
            for u in range(1, B + 1):
                slot(NCH - B + u, u % B, counts_of=NCH // B - 2 if u == COUNTS_AT else None, head=u < B)
            pe.wait_ge(q["y_taken"], NCH)
            route_counts(NCH // B - 1).then_inc(q["y_ready"], 1)

            expert = [pe.alloc_register(f"expert{u}") for u in range(4)]

            def expert_of(u):
                return pe.snap(expert[u % 4], min_val=0, max_val=E - 1)

            def step(t, u, turn, stages=(0, 1, 2, 3)):
                par = u % 2
                if 0 in stages:
                    pe.wait_ge(row_in[u], 16 * turn + 16)
                    if some(t - 1):
                        pe.wait_ge(q["t_x_taken"], t - 1)
                    for k in range(2):
                        tr = pe.transpose(bank[par][:, k * P:(k + 1) * P], tile_x[u][:, k * P:(k + 1) * P], ident)
                    tr.then_inc(q["t_x_ready"], 1)
                if 1 in stages:
                    e = expert_of(u - 1)
                    pe.wait_ge(q["t_x_taken"], t)
                    if some(t - 2):
                        pe.wait_ge(q["t_h_taken"], t - 2)
                    for k in range(2):
                        pe.matmul(bank[2 + 1 - par][:, 0:D], tile_xT[1 - par][:, k, :],
                                  w13[:, k, bass.ds(e, 1), :].rearrange("p e n -> p (e n)"), start=(k == 0), stop=False)
                    pe.matmul(bank[2 + 1 - par][:, 0:D], ones_bf[0:3, :],
                              bias_e[:, bass.ds(e, 1), 0:D].rearrange("p e n -> p (e n)"),
                              start=False, stop=True).then_inc(q["t_h_ready"], 1)
                if 0 in stages:
                    at = slice(t, t + 1) if isinstance(t, int) else bass.ds(t, 1)
                    pe.reg_load(expert[u], tile_exp[0:1, at])
                if 2 in stages:
                    pe.wait_ge(q["t_h_taken"], t - 1)
                    if some(t - 3):
                        pe.wait_ge(q["t_ht_taken"], t - 3)
                    pe.transpose(s_bank[par][:, 0:P], tile_h[par][:, :], ident).then_inc(q["t_ht_ready"], 1)
                if 3 in stages:
                    e = expert_of(u - 3)
                    pe.wait_ge(q["t_ht_taken"], t - 2)
                    if some(t - 4):
                        pe.wait_ge(q["t_y_taken"], t - 4)
                    pe.matmul(o_bank[:, 1 - par, 0:D], tile_hT[1 - par][:, :],
                              w2[:, bass.ds(e, 1), :].rearrange("p e n -> p (e n)"), start=True, stop=False)
                    pe.matmul(o_bank[:, 1 - par, 0:D], ones_bf[0:3, :],
                              bias_e[:, bass.ds(e, 1), D:512].rearrange("p e n -> p (e n)"),
                              start=False, stop=True).then_inc(q["t_y_ready"], 1)

            pe.wait_ge(q["expert_in"], 64)
            pe.wait_ge(q["tiles_ready"], 1)
            pe.wait_ge(q["second_in"], 32)
            for t in range(4):
                step(t, t, 0, stages=range(t + 1))
            with pe.Fori(1, NT // 4) as j:
                for u in range(4):
                    step(4 * j + u, u, j)
            for t in range(NT, NT + 3):
                step(t, t % 4, t // 4, stages=range(t - NT + 1, 4))

        @blk.scalar
        def _(act):
            def norm_taken(i):
                act.wait_ge(q["xnT_ready"], i + 1)
                xT = bank[3][:, 0:D].rearrange("p (k n) -> p k n", k=2)
                act.activation(xnT_r[:, 0, :, :], xT, ACT.Copy)
                act.activation(xnT[:, :, :], xT, ACT.Copy).then_inc(q["xnT_taken"], 1)

            def slot(i, u, exp_of=None, head=True, tail=True):
                t = i - 1
                if exp_of is not None:
                    act.wait_ge(q["shift_ready"], exp_of + 1)
                    act.activation(r32[:, 1, :, :], r32[:, 0, :, :], ACT.Exp).then_inc(q["exp_ready"], 1)
                if head:
                    act.wait_ge(q["qk_ready"], i + 1)
                    if some(i):
                        act.wait_ge(q["rot_ready"], i)
                    act.activation(qk[:, :], bank[0][:, :], ACT.Copy).then_inc(q["qk_taken"], 1)
                    act.wait_ge(q["v_ready"], i + 1)
                    if some(i):
                        act.wait_ge(q["kv_ready"], 2 * i)
                    act.activation(val[:, :, 0:VD], bank[1][:, :].rearrange("p (h d) -> p h d", h=H), ACT.Copy)\
                        .then_inc(q["v_taken"], 1)
                if head:
                    act.wait_ge(q["qkT_ready"], i + 1)
                    qT = bank[1][:, 0:D].rearrange("p (k n) -> p k n", k=2)
                    act.activation(qkT[:, 2:4, :], bank[1][:, D:512].rearrange("p (k n) -> p k n", k=2), ACT.Copy)
                    for h in range(HH):
                        a = act.activation(q_split[:, :, h, :], qT, ACT.Copy, scale=cst[:, C_HEAD + h:C_HEAD + h + 1])
                        if h % 2:
                            a.then_inc(q["qsplit_ready"], 1)
                    act.activation(qkT[:, 0:2, :], qT, ACT.Copy).then_inc(q["qcopy_ready"], 1)
                if tail:
                    act.wait_ge(q["nT_taken"], t + 1)
                    if some(t):
                        act.wait_ge(q["wo_ready"], t)
                    act.activation(gated_r[:, 0, :, :], gated[:, :, :], ACT.Copy).then_inc(q["gated_rounded"], 1)
                if head:
                    act.wait_ge(q["gT_ready"], i + 1)
                    if some(i - 1):
                        act.wait_ge(q["nT_taken"], i - 1)
                    for m in range(4):
                        a = act.activation(gate_silu[:, u % 2, m, :], bank[3][:, m * P:(m + 1) * P], ACT.Silu,
                                           bias=bg_col[:, m:m + 1])
                    a.then_inc(q["gT_taken"], 1)
                if tail:
                    act.wait_ge(q["xn2T_ready"], t + 1)
                    if some(t):
                        act.wait_ge(q["y_ready"], t)
                    act.activation(xn2T[:, :, :], bank[2][:, 0:D].rearrange("p (k n) -> p k n", k=2), ACT.Copy)\
                        .then_inc(q["xn2T_taken"], 1)
                    act.wait_ge(q["h13_ready"], t + 1)
                    if some(t):
                        act.wait_ge(q["h3_taken"], t)
                    for m in range(2):
                        a = act.activation(sh_silu[:, m, :], bank[3][:, m * P:(m + 1) * P], ACT.Silu,
                                           bias=bs_col[:, m:m + 1])
                    a.then_inc(q["h1_taken"], 1)
                if head:
                    act.wait_ge(q["o_ready"], i + 1)
                    if some(i):
                        act.wait_ge(q["gn_ve_ready"], i)
                    act.activation(squares[:, :, :], o_bank[:, :, 0:HH * VW], ACT.Square).then_inc(q["o_squared"], 1)
                if head and not (isinstance(i, int) and i == NCH - 1):
                    norm_taken(i + 1)

            act.wait_ge(q["b_in"], 16 * B_DMAS)
            norm_taken(0)
            act.wait_ge(q["w_in"], 16 * W_DMAS)
            act.activation(wqk[:, 0, :, :], wqk_f, ACT.Copy)
            act.activation(wo[:, 0, :, :], wo_f, ACT.Copy).then_inc(q["w_rounded"], 1)
            act.wait_ge(q["setup_dve"], 1)
            act.wait_ge(q["part_out"], 48)
            slot(0, 0, tail=False)
            for i in range(1, B + 1):
                slot(i, i % B)
            with act.Fori(1, NCH // B - 1) as c:
                for u in range(1, B + 1):
                    slot(B * c + u, u % B, exp_of=c - 1 if u == 2 else None)
            for u in range(1, B + 1):
                slot(NCH - B + u, u % B, exp_of=NCH // B - 2 if u == 2 else None, head=u < B)
            act.wait_ge(q["shift_ready"], NCH // B)
            act.activation(r32[:, 1, :, :], r32[:, 0, :, :], ACT.Exp).then_inc(q["exp_ready"], 1)

            def step(t, u, turn, stages=(0, 1, 3)):
                par = u % 2
                if 0 in stages:
                    act.wait_ge(q["t_x_ready"], t + 1)
                    if some(t - 1):
                        act.wait_ge(q["t_h_ready"], t - 1)
                    act.activation(tile_xT[par][:, :, :], bank[par][:, 0:D].rearrange("p (k n) -> p k n", k=2),
                                   ACT.Copy).then_inc(q["t_x_taken"], 1)
                if 1 in stages:
                    act.wait_ge(q["t_h_ready"], t)
                    if some(t - 2):
                        act.wait_ge(q["t_h_taken"], t - 2)
                    act.activation(tile_silu[1 - par][:, :], bank[2 + 1 - par][:, 0:INTER], ACT.Silu)\
                        .then_inc(q["t_h_silu"], 1)
                if 3 in stages:
                    act.wait_ge(q["t_y_ready"], t - 2)
                    if some(turn + (u - 3) // 4):
                        act.wait_ge(y_out[(u + 1) % 4], 16 * (turn + (u - 3) // 4))
                    act.activation(tile_y[(u + 1) % 4][:, :], o_bank[:, 1 - par, 0:D], ACT.Copy)\
                        .then_inc(q["t_y_taken"], 1)

            act.wait_ge(q["tiles_ready"], 1)
            for t in range(8):
                step(t, t % 4, t // 4, stages=[s for s in (0, 1, 3) if s <= t])
            with act.Fori(2, NT // 4) as j:
                for u in range(4):
                    step(4 * j + u, u, j)
            for t in range(NT, NT + 3):
                step(t, t % 4, t // 4, stages=[s for s in (1, 3) if s > t - NT])

            out_pos = out.rearrange("b (c p) d -> c p b d", p=P)
            with act.Fori(0, S // P) as c:
                for h in range(2):
                    act.wait_ge(q["sum_done"], B * c + 4 * h + 4)
                    act.dma_start(out_pos[bass.ds(c, 1), :, 4 * h:4 * h + 4, :].rearrange("c p b d -> (c p) b d"),
                                  stream[:, bass.ds(B * c + 4 * h, 4), :]).then_inc(q["out_done"], 16)
            act.wait_ge(q["out_done"], 16 * 2 * (S // P))

        @blk.vector
        def _(dve):
            dve.wait_ge(q["brow_in"], 80)
            n = [0]

            def then(ins):
                n[0] += 1
                ins.then_inc(q["setup_step"], 1)
                dve.wait_ge(q["setup_step"], n[0])

            then(dve.tensor_copy(bpart[:, 0, :], brows))
            then(dve.tensor_tensor(bres, brows, bpart[:, 0, :], ALU.subtract))
            then(dve.tensor_copy(bpart[:, 1, :], bres))
            then(dve.tensor_tensor(brows, bres, bpart[:, 1, :], ALU.subtract))
            dve.tensor_copy(bpart[:, 2, :], brows).then_inc(q["parts_ready"], 1)
            dve.memset(fill[:, :, 0], 0)
            dve.memset(fill_spare[:, :, 0], 0)
            dve.wait_ge(q["setup_pool"], 4)
            dve.wait_ge(q["const_in"], 16)
            dve.tensor_scalar(fill[:, :, 1], fill[:, :, 1], cst[:, C_SPARE:C_SPARE + 1], None, ALU.add)\
                .then_inc(q["zeros_ready"], 1)

            def norm_stats(src, w, step_sem, ready, i):
                dve.bn_stats(stats[:, w, :], src).then_inc(step_sem, 1)
                dve.wait_ge(step_sem, alone(dve, 2 * i + 1))
                dve.bn_aggr(mean_var[:, w, :], stats[:, w, :]).then_inc(step_sem, 1)
                dve.wait_ge(step_sem, 2 * i + 2)
                dve.tensor_scalar(var_eps[:, w:w + 1], mean_var[:, w, 1:2], EPS, None, ALU.add).then_inc(ready, 1)

            def row(i):
                return stream[:, i, :] if isinstance(i, int) else \
                    stream[:, bass.ds(i, 1), :].rearrange("p c d -> p (c d)")

            def norm1(i):
                dve.wait_ge(q["rstd1_ready"], i + 1)
                if some(i):
                    dve.wait_ge(q["xnT_ready"], i)
                dve.tensor_scalar(xn[:, :], row(i), mean_var[:, 0, 0:1], rstd[:, 0:1], ALU.subtract, ALU.mult)\
                    .then_inc(q["xn_ready"], 1)

            dve.memset(half_neg[:, :], -0.5).then_inc(q["setup_step"], 1)
            dve.wait_ge(q["x_in"], 16)
            dve.wait_ge(q["setup_step"], 5)
            norm_stats(row(0), 0, q["ln1_step"], q["ve1_ready"], 0)
            norm1(0)
            n[0] = 5
            dve.wait_ge(q["const_in"], 16)
            dve.wait_ge(q["b_in"], 16 * B_DMAS)
            def centre(mean, v):
                v3 = v.rearrange("p (h d) -> p h d", h=H)
                then(dve.tensor_reduce(mean, v3, AX, ALU.add))
                then(dve.tensor_scalar(mean, mean, 1.0 / VD, None, ALU.mult))
                then(dve.tensor_tensor(v3, v3, mean.unsqueeze(2).broadcast_to(list(v3.shape)), ALU.subtract))

            centre(vmean_b[:, :], bias_f[:, 1, :])
            for k in range(3):
                pick = cst[0:3, C_ID + k:C_ID + k + 1]
                then(dve.tensor_copy(bpart3[:, 0, :], bias_f[:, :, :].rearrange("p a n -> p (a n)")))
                if k == 0:
                    then(dve.tensor_scalar(bsum, bpart3[:, 0, :], pick, None, ALU.mult))
                else:
                    then(dve.scalar_tensor_tensor(bsum, bpart3[:, 0, :], pick, bsum, ALU.mult, ALU.add))
                if k < 2:
                    then(dve.tensor_tensor(bias_f[:, :, :].rearrange("p a n -> p (a n)"),
                                           bias_f[:, :, :].rearrange("p a n -> p (a n)"), bpart3[:, 0, :],
                                           ALU.subtract))
            then(dve.tensor_copy(bias_qkv[:, :, :].rearrange("p a n -> p (a n)"), bsum))
            dve.wait_ge(q["w_in"], 16 * W_DMAS)
            for k in range(2):
                centre(vmean[:, k, :], wv_f[:, k, :])
            then(dve.tensor_copy(wv[:, 0, :, :], wv_f))
            dve.wait_ge(q["w_rounded"], 1)
            for w, whole in ((wv, wv_f), (wqk, wqk_f), (wo, wo_f)):
                then(dve.tensor_tensor(w[:, 1, :, :], whole, w[:, 0, :, :].bitcast(F32), ALU.subtract))
            dve.memset(val[:, :, VD:VW], 1.0)
            dve.memset(ones_bf[:, :], 1.0)
            dve.tensor_copy(before_bf[:, :], cst[:, C_PRE:C_PRE + P])
            dve.tensor_copy(base[:, :], cst[:, C_REG:C_REG + E]).then_inc(q["setup_dve"], 1)

            bank3v = bank[3][:, :].rearrange("p (m n) -> p m n", m=4)

            def tab_of(i, a):
                if isinstance(i, int):
                    return tab[:, (i // B) % 2, a, :]
                return tab[:, bass.ds((i // B) % 2, 1), a, :].rearrange("p c n -> p (c n)")

            R_STEPS, SLOT_STEPS = 32, 6

            def slot(i, u, route=None, head=True, tail=True):
                t = i - 1
                last = isinstance(i, int) and i == NCH - 1
                if head:
                    dve.wait_ge(q["rot_in"], 16 * (i // B) + 16)
                    if some(i):
                        dve.wait_ge(q["kv_ready"], 2 * i)
                    dve.wait_ge(q["qk_taken"], i + 1)
                    for a in range(2):
                        dve.tensor_tensor(qk_rot[:, a::2], qk[:, 1 - a::2], tab_of(i, 1)[:, a::2], ALU.mult)\
                            .then_inc(q["rot_step"], 1)
                    dve.tensor_tensor(qk_cos[:, COS_POOL:512], qk[:, COS_POOL:512], tab_of(i, 0)[:, COS_POOL:512],
                                      ALU.mult).then_inc(q["rot_step"], 1)
                    dve.wait_ge(q["rot_step"], 3 * i + 3)
                    dve.wait_ge(q["cos_ready"], i + 1)
                    dve.tensor_tensor(qk_rot[:, :], qk_rot[:, :], qk_cos[:, :], ALU.add).then_inc(q["rot_ready"], 1)
                if tail:
                    dve.wait_ge(q["gn_pow_ready"], t + 1)
                    if some(t):
                        dve.wait_ge(q["nT_ready"], t)
                    dve.tensor_tensor(normed[:, :].rearrange("p (a h d) -> p a h d", a=2, h=HH),
                                      o_bank[:, :, 0:HH * VW].rearrange("p a (h w) -> p a h w", w=VW)[:, :, :, 0:VD],
                                      gn_pow[:, :].rearrange("p (a h) -> p a h", a=2).unsqueeze(3)
                                      .broadcast_to([P, 2, HH, VD]), ALU.mult).then_inc(q["normed_ready"], 1)
                if head:
                    if not last:
                        dve.wait_ge(q["x_in"], alone(dve, 16 * ((i + 1) // B) + 16))
                        dve.bn_stats(stats[:, 0, :], row(i + 1)).then_inc(q["ln1_step"], 1)
                    if not last:
                        dve.wait_ge(q["ln1_step"], alone(dve, 2 * i + 3))
                        dve.bn_aggr(mean_var[:, 0, :], stats[:, 0, :]).then_inc(q["ln1_step"], 1)
                if route is not None and u == 1:
                    pick_experts(route, 0)
                if head and not last:
                    dve.wait_ge(q["ln1_step"], 2 * i + 4)
                    dve.tensor_scalar(var_eps[:, 0:1], mean_var[:, 0, 1:2], EPS, None, ALU.add)\
                        .then_inc(q["ve1_ready"], 1)
                if tail:
                    dve.wait_ge(q["nT_ready"], t + 1)
                    dve.wait_ge(q["gT_taken"], t + 1)
                    dve.tensor_tensor(gated[:, :, :], bank[2][:, :].rearrange("p (m n) -> p m n", m=4),
                                      gate_silu[:, 1 - u % 2, :, :], ALU.mult).then_inc(q["nT_taken"], 1)
                if head and not last:
                    norm1(i + 1)
                if head:
                    for g in range(3):
                        mask(i, g)
                if tail:
                    dve.wait_ge(q["gated_rounded"], t + 1)
                    dve.tensor_tensor(gated_r[:, 1, :, :], gated[:, :, :], gated_r[:, 0, :, :].bitcast(F32),
                                      ALU.subtract).then_inc(q["gated_left"], 1)
                if head:
                    mask(i, 3)
                if tail:
                    dve.wait_ge(q["wo_ready"], t + 1)
                    dve.tensor_tensor(row(t), bank[0][:, 0:D], row(t), ALU.add).then_inc(q["wo_taken"], 1)
                    dve.wait_ge(q["wo_taken"], alone(dve, t + 1))
                    norm_stats(row(t), 1, q["ln2_step"], q["ve2_ready"], t)
                if tail:
                    dve.wait_ge(q["rstd2_ready"], t + 1)
                    if some(t // 2):
                        dve.wait_ge(xn2_stored[1 - u % 2], 16 * (t // 2))
                    dve.tensor_scalar(xn2[:, 1 - u % 2, :], row(t), mean_var[:, 1, 0:1], rstd[:, 1:2],
                                      ALU.subtract, ALU.mult).then_inc(q["xn2_ready"], 1)
                if route is not None and 2 <= u <= 5:
                    pick_experts(route, u - 1)
                if route is not None and u == SLOTS_AT:
                    slots_of(route)
                if tail:
                    dve.wait_ge(q["h1_taken"], t + 1)
                    if some(t):
                        dve.wait_ge(q["y_ready"], t)
                    for k in range(2):
                        h = dve.scalar_tensor_tensor(sh_hT[:, k, :], bank3v[:, 2 + k, :], bs_col[:, 2 + k:3 + k],
                                                     sh_silu[:, k, :], ALU.add, ALU.mult)
                    h.then_inc(q["h3_taken"], 1)
                if head:
                    sq = squares[:, :, :].rearrange("p a (h w) -> p (a h) w", w=VW)
                    dve.wait_ge(q["o_squared"], i + 1)
                    dve.scalar_tensor_tensor(gn[:, 0, :], sq[:, :, VD], EPS, floor_of(i), ALU.mult, ALU.max)\
                        .then_inc(q["gn_step"], 1)
                    dve.tensor_reduce(gn[:, 1, :], sq[:, :, 0:VD], AX, ALU.add).then_inc(q["gn_step"], 1)
                    dve.wait_ge(q["gn_step"], 2 * i + 2)
                    if some(i):
                        dve.wait_ge(q["gn_pow_ready"], i)
                    dve.scalar_tensor_tensor(gn[:, 2, :], gn[:, 1, :], 1.0 / VD, gn[:, 0, :], ALU.mult, ALU.add)\
                        .then_inc(q["gn_ve_ready"], 1)
                    dve.wait_ge(q["state_ready"], i + B)
                    for half in range(2):
                        dve.wait_ge(q["kv_ready"], 2 * i + half + 1)
                        dve.tensor_tensor(kv_new[:, half, :], bank[half][:, 0:HH * VW], block, ALU.mult)\
                            .then_inc(q["kv_taken"], 1)
                if head and not last:
                    left_of_xnT(i + 1)
                if tail:
                    dve.wait_ge(q["y_ready"], t + 1)
                    if route is not None and u == 1:
                        dve.wait_ge(q["shift_ready"], route + 1)
                    dve.tensor_copy(lg[:, (u - 1) % B, :], bank[2][:, D:D + E])
                    y = dve.tensor_tensor(row(t), bank[2][:, 0:D], row(t), ALU.add)
                    if route is not None and u == COUNTS_AT:
                        take_counts(route)
                    else:
                        y.then_inc(q["y_taken"], 1)

            def left_of_xnT(i):
                dve.wait_ge(q["xnT_taken"], i + 1)
                dve.tensor_tensor(xnT_r[:, 1, :, :], xnT[:, :, :], xnT_r[:, 0, :, :].bitcast(F32), ALU.subtract)\
                    .then_inc(q["xnT_left"], 1)

            def floor_of(i):
                if isinstance(i, int):
                    return floor_tab[:, i // B, :]
                return floor_tab[:, bass.ds(i // B, 1), :].rearrange("p c h -> p (c h)")

            def mask(i, g):
                dve.wait_ge(q["s_ready"], 4 * i + g + 1)
                if g == 0 and some(i):
                    dve.wait_ge(q["o_ready"], i)
                dve.tensor_tensor(probs[:, g, :, :, :].rearrange("p h e s -> p (h e) s"),
                                  score_bank[g].rearrange("p (h s) -> p h s", h=4),
                                  causal.unsqueeze(1).broadcast_to([P, 4, P]), ALU.mult).then_inc(q["s_taken"], 1)

            def wide(v):
                return v.unsqueeze(2).broadcast_to([P, B, E])

            def flat(v):
                return v.rearrange("p c g -> p (c g)")

            FIRST_STEP = (0, 1, 9, 17, 24)

            def pick_experts(c, part):
                m = [FIRST_STEP[part]]

                def nxt(ins):
                    m[0] += 1
                    ins.then_inc(q["route_step"], 1)
                    dve.wait_ge(q["route_step"], R_STEPS * c + m[0])

                by_e = cst[:, C_IOM:C_IOM + E].unsqueeze(1).broadcast_to([P, B, E])
                in_groups = "p c (g e) -> p (c g) e"
                soft, score, left, left2, tmp = (r32[:, k, :, :] for k in (2, 3, 4, 5, 0))
                sg, lg4 = score.rearrange(in_groups, g=G), left.rearrange(in_groups, g=G)

                def pick_best(pick, v):
                    nxt(dve.tensor_reduce(r1[:, 3, :], v, AX, ALU.max))
                    nxt(dve.tensor_tensor(tmp, v, wide(r1[:, 3, :]), ALU.is_equal))
                    nxt(dve.tensor_tensor(tmp, tmp, by_e, ALU.mult))
                    nxt(dve.tensor_reduce(r1[:, 4, :], tmp, AX, ALU.min))
                    nxt(dve.tensor_tensor(pick[:, :, :], by_e, wide(r1[:, 4, :]), ALU.is_equal))

                if part == 0:
                    dve.wait_ge(q["y_taken"], B * c + B)
                    nxt(dve.tensor_reduce(r1[:, 0, :], lg[:, :, :], AX, ALU.max))
                    dve.tensor_tensor(r32[:, 0, :, :], lg[:, :, :], wide(r1[:, 0, :]), ALU.subtract)\
                        .then_inc(q["shift_ready"], 1)
                elif part == 1:
                    dve.wait_ge(q["exp_ready"], c + 1)
                    nxt(dve.tensor_reduce(r1[:, 1, :], r32[:, 1, :, :], AX, ALU.add))
                    nxt(dve.reciprocal(r1[:, 2, :], r1[:, 1, :]))
                    nxt(dve.tensor_tensor(soft, r32[:, 1, :, :], wide(r1[:, 2, :]), ALU.mult))
                    nxt(dve.tensor_tensor(score, soft, gb_bc[:, :].unsqueeze(1).broadcast_to([P, B, E]), ALU.add))
                    high = r16[:, 0:2, :, :].rearrange("p a c g -> p (a c g)").rearrange("p (n e) -> p n e", e=2)
                    low = r16[:, 2:4, :, :].rearrange("p a c g -> p (a c g)").rearrange("p (n e) -> p n e", e=2)
                    dve.tensor_tensor(high, sg[:, :, 0::2], sg[:, :, 1::2], ALU.max)
                    nxt(dve.tensor_tensor(low, sg[:, :, 0::2], sg[:, :, 1::2], ALU.min))
                    dve.tensor_tensor(flat(r8[:, 0, :, :]), high[:, :, 0], high[:, :, 1], ALU.max)
                    dve.tensor_tensor(flat(r8[:, 1, :, :]), high[:, :, 0], high[:, :, 1], ALU.min)
                    nxt(dve.tensor_tensor(flat(r8[:, 2, :, :]), low[:, :, 0], low[:, :, 1], ALU.max))
                    nxt(dve.tensor_tensor(r8[:, 3, :, :], r8[:, 1, :, :], r8[:, 2, :, :], ALU.max))
                    nxt(dve.tensor_tensor(r8[:, 4, :, :], r8[:, 0, :, :], r8[:, 3, :, :], ALU.add))
                elif part == 2:
                    mine = r8[:, 4, :, :].unsqueeze(3).broadcast_to([P, B, G, G])
                    other = r8[:, 4, :, :].unsqueeze(2).broadcast_to([P, B, G, G])
                    higher, same = r_cmp[:, 0, :, :, :], r_cmp[:, 1, :, :, :]
                    dve.tensor_tensor(higher, other, mine, ALU.is_gt)
                    nxt(dve.tensor_tensor(same, other, mine, ALU.is_equal))
                    nxt(dve.tensor_tensor(same, same, group_lt.unsqueeze(1).broadcast_to([P, B, G, G]), ALU.mult))
                    nxt(dve.tensor_tensor(higher, higher, same, ALU.add))
                    nxt(dve.tensor_reduce(r8[:, 5, :, :], higher, AX, ALU.add))
                    nxt(dve.tensor_scalar(r8[:, 6, :, :], r8[:, 5, :, :], float(TOPK_G), None, ALU.is_lt))
                    nxt(dve.tensor_scalar(r8[:, 7, :, :], r8[:, 6, :, :], -1.0, BIG, ALU.add, ALU.mult))
                    per_e = lambda k: flat(r8[:, k, :, :]).unsqueeze(2).broadcast_to([P, B * G, E // G])
                    nxt(dve.tensor_tensor(lg4, sg, per_e(6), ALU.mult))
                    nxt(dve.tensor_tensor(lg4, lg4, per_e(7), ALU.add))
                elif part == 3:
                    pick_best(pick1, left)
                    nxt(dve.scalar_tensor_tensor(left2, pick1[:, :, :], -BIG, left, ALU.mult, ALU.add))
                    nxt(dve.tensor_tensor(left, soft, pick1[:, :, :], ALU.mult))
                else:
                    pick_best(pick2, left2)
                    dve.tensor_tensor(picks_bf[:, :, :], pick1[:, :, :], pick2[:, :, :], ALU.add)\
                        .then_inc(q["picks_ready"], 1)
                    nxt(dve.tensor_tensor(left2, soft, pick2[:, :, :], ALU.mult))
                    w_at = all_w[:, c, :, :] if isinstance(c, int) else \
                        all_w[:, bass.ds(c, 1), :, :].rearrange("p n k c -> p (n k) c")
                    nxt(dve.tensor_reduce(w_at[:, 0, :], left, AX, ALU.add))
                    nxt(dve.tensor_reduce(w_at[:, 1, :], left2, AX, ALU.add))
                want = (FIRST_STEP + (R_STEPS,))[part + 1]
                assert m[0] == want, (part, m[0])

            def slot_next(c, k, ins):
                ins.then_inc(q["slot_step"], 1)
                dve.wait_ge(q["slot_step"], SLOT_STEPS * c + k)

            def take_counts(c):
                slot_next(c, 1, dve.tensor_tensor(
                    r32[:, 0, :, :], bank[2][:, 272:272 + B * E].rearrange("p (c e) -> p c e", c=B),
                    base[:, :].unsqueeze(1).broadcast_to([P, B, E]), ALU.add))
                dve.tensor_tensor(base[:, :], bank[2][:, 272 + B * E:272 + (B + 1) * E], base[:, :], ALU.add)\
                    .then_inc(q["y_taken"], 1)

            def slots_of(c):
                for k, pick in ((0, pick1), (1, pick2)):
                    slot_next(c, 2 + 2 * k, dve.tensor_tensor(r32[:, 1, :, :], r32[:, 0, :, :], pick[:, :, :], ALU.mult))
                    slot_next(c, 3 + 2 * k, dve.tensor_reduce(slot_f[:, k, :], r32[:, 1, :, :], AX, ALU.add))
                if some(c):
                    dve.wait_ge(q["scattered"], 32 * B * c)
                slot_next(c, 6, dve.tensor_copy(slot_i[:, :, :], slot_f[:, :, :]))
                dve.tensor_scalar(token_i[:, :, :, :], token_i[:, :, :, :], float(B * P), None, ALU.add)\
                    .then_inc(q["slots_ready"], 1)

            dve.wait_ge(q["setup_step"], n[0])
            dve.wait_ge(q["part_out"], 48)
            dve.wait_ge(q["zero_in"], 32)
            left_of_xnT(0)
            slot(0, 0, tail=False)
            for i in range(1, B + 1):
                slot(i, i % B)
            with dve.Fori(1, NCH // B - 1) as c:
                for u in range(1, B + 1):
                    slot(B * c + u, u % B, route=c - 1)
            for u in range(1, B + 1):
                slot(NCH - B + u, u % B, route=NCH // B - 2, head=u < B)
            for part in range(5):
                pick_experts(NCH // B - 1, part)
            dve.wait_ge(q["y_ready"], NCH + 1)
            take_counts(NCH // B - 1)
            slots_of(NCH // B - 1)

            n[0] = 0

            def tile_next(ins):
                n[0] += 1
                ins.then_inc(q["tile_step"], 1)
                dve.wait_ge(q["tile_step"], n[0])

            nt = n_tiles
            dve.wait_ge(q["y_taken"], NCH + 1)
            tile_next(dve.tensor_tensor(nt[:, 0, :], base[:, :], cst[:, C_REG:C_REG + E], ALU.subtract))
            tile_next(dve.tensor_scalar(nt[:, 0, :], nt[:, 0, :], float(P - 1), None, ALU.add))
            tile_next(dve.tensor_copy(n_tiles_i[:, 0, :], nt[:, 0, :]))
            tile_next(dve.tensor_scalar(n_tiles_i[:, 1, :], n_tiles_i[:, 0, :], 7, None, ALU.arith_shift_right))
            tile_next(dve.tensor_copy(nt[:, 1, :], n_tiles_i[:, 1, :]))
            tile_next(dve.memset(nt[:, 3, :], 1.0))
            tile_next(dve.tensor_tensor_scan(nt[:, 2, :], nt[:, 3, :], nt[:, 1, :], 0.0, ALU.mult, ALU.add))
            tiles = cst[0:1, C_TILE:C_TILE + NT]
            per_tile = lambda v: v.unsqueeze(1).broadcast_to([1, NT, E])
            tile_next(dve.tensor_tensor(tile_cmp, tiles.unsqueeze(2).broadcast_to([1, NT, E]),
                                        per_tile(nt[0:1, 2, :]), ALU.is_ge))
            tile_next(dve.tensor_reduce(tile_e[:, 0, :], tile_cmp, AX, ALU.add))
            tile_next(dve.tensor_tensor(tile_cmp, tile_cmp, per_tile(nt[0:1, 1, :]), ALU.mult))
            tile_next(dve.tensor_reduce(tile_e[:, 1, :], tile_cmp, AX, ALU.add))
            tile_next(dve.tensor_tensor(tile_e[:, 2, :], tiles, tile_e[:, 1, :], ALU.subtract))
            tile_next(dve.tensor_scalar(tile_e[:, 2, :], tile_e[:, 2, :], float(P), None, ALU.mult))
            tile_next(dve.scalar_tensor_tensor(tile_e[:, 2, :], tile_e[:, 0, :], float(REG), tile_e[:, 2, :],
                                               ALU.mult, ALU.add))
            tile_next(dve.tensor_copy(tile_row[:, :], tile_e[:, 2, :]))
            dve.wait_ge(q["scattered"], 32 * NCH)
            for par in range(2):
                dve.wait_ge(xn2_stored[par], 16 * (NCH // 2))
            dve.tensor_scalar(tile_exp[:, :], tile_e[:, 0, :], float(E - 1), None, ALU.min).then_inc(q["tiles_ready"], 1)

            def step(t, u, turn, stages=(0, 1, 2)):
                par = u % 2
                if 0 in stages:
                    dve.wait_ge(id_in[u], 16 * turn + 16)
                    if some(turn):
                        dve.wait_ge(y_out[u % 4], alone(dve, 16 * (2 * turn - 1 + u // 4)))
                    dve.tensor_copy(tile_dest[u][:, :], tile_id[u][:, 1:2]).then_inc(q["dest_ready"], 1)
                if 1 in stages:
                    dve.wait_ge(q["t_h_silu"], t)
                    if some(t - 2):
                        dve.wait_ge(q["t_ht_ready"], t - 2)
                    dve.tensor_tensor(tile_h[1 - par][:, :], bank[2 + 1 - par][:, INTER:D], tile_silu[1 - par][:, :],
                                      ALU.mult).then_inc(q["t_h_taken"], 1)
                if 2 in stages:
                    dve.wait_ge(q["t_ht_ready"], t - 1)
                    if some(t - 3):
                        dve.wait_ge(q["t_y_ready"], t - 3)
                    dve.tensor_copy(tile_hT[par][:, :], s_bank[par][:, 0:P]).then_inc(q["t_ht_taken"], 1)

            for t in range(8):
                step(t, t, 0, stages=[s for s in (0, 1, 2) if s <= t])
            with dve.Fori(1, NT // 8) as j:
                for u in range(8):
                    step(8 * j + u, u, j)
            for t in range(NT, NT + 2):
                step(t, t % 8, t // 8, stages=[s for s in (1, 2) if s > t - NT])

            with dve.Fori(0, NCH // 16) as j:
                for g in range(4):
                    for b in range(4):
                        c, batch = 2 * j + g // 2, 4 * (g % 2) + b
                        at = row(16 * j + 4 * g + b)
                        for k in range(2):
                            w = all_w[:, bass.ds(c, 1), k, batch:batch + 1].rearrange("p n c -> p (n c)")
                            if k == 0 and b == 0:
                                dve.wait_ge(picked_in[g], 32 * j + 32)
                            o = dve.scalar_tensor_tensor(at, picked[g][:, k, b, :], w, at, ALU.mult, ALU.add)
                            if k == 0:
                                o.then_inc(q["sum_step"], 1)
                                dve.wait_ge(q["sum_step"], 16 * j + 4 * g + b + 1)
                            else:
                                o.then_inc(q["sum_done"], 1)

        @blk.gpsimd
        def _(pool):
            for a, apart in ((0, 0), (1, B * S)):
                pool.iota(token_i[:, :, :, a], pattern=[[apart, 2], [P, B]], base=-B * P, channel_multiplier=1)\
                    .then_inc(q["setup_pool"], 1)
            pool.iota(fill[:, :, 1], pattern=[[0, per_part // P], [1, P]], base=0, channel_multiplier=0)\
                .then_inc(q["setup_pool"], 1)
            pool.iota(fill_spare[:, :, 1], pattern=[[1, E]], base=ROWS + E * P, channel_multiplier=E)\
                .then_inc(q["setup_pool"], 1)
            pool.memset(state[:, :, :, :], 0.0).then_inc(q["state_ready"], B)
            pool.wait_ge(q["state_ready"], B)

            def rstd_of(w, ready):
                pool.tensor_tensor(rstd[:, w:w + 1], var_eps[:, w:w + 1], half_neg[:, 0:1], ALU.pow).then_inc(ready, 1)

            def tab_of(i, a):
                if isinstance(i, int):
                    return tab[:, (i // B) % 2, a, :]
                return tab[:, bass.ds((i // B) % 2, 1), a, :].rearrange("p c n -> p (c n)")

            def slot(i, u, scatter_of=None, head=True, tail=True):
                t = i - 1
                last = isinstance(i, int) and i == NCH - 1
                if head:
                    pool.wait_ge(q["rot_in"], 16 * (i // B) + 16)
                    if some(i):
                        pool.wait_ge(q["rot_ready"], i)
                    pool.wait_ge(q["qk_taken"], i + 1)
                    pool.tensor_tensor(qk_cos[:, 0:COS_POOL], qk[:, 0:COS_POOL], tab_of(i, 0)[:, 0:COS_POOL], ALU.mult)\
                        .then_inc(q["cos_ready"], 1)
                if head and tail:
                    pool.wait_ge(q["kv_taken"], 2 * t + 2)
                    st = state[:, (u - 1) % B, :, :].rearrange("p a n -> p (a n)")
                    pool.tensor_tensor(st, st, kv_new[:, :, :].rearrange("p a n -> p (a n)"), ALU.add)\
                        .then_inc(q["state_ready"], 1)
                if head and not last:
                    pool.wait_ge(q["ve1_ready"], i + 2)
                    rstd_of(0, q["rstd1_ready"])
                scatters = scatter_of is not None and (u - SCATTERS_AT) % B < 2
                first = 4 * ((u - SCATTERS_AT) % B)
                if scatters:
                    scatter(scatter_of, first)
                if tail:
                    pool.wait_ge(q["ve2_ready"], t + 1)
                    rstd_of(1, q["rstd2_ready"])
                if scatters:
                    for b in range(first + 1, first + 4):
                        scatter(scatter_of, b)
                if head:
                    pool.wait_ge(q["gn_ve_ready"], i + 1)
                    if some(i):
                        pool.wait_ge(q["normed_ready"], i)
                    pool.tensor_tensor(gn_pow[:, :], gn[:, 2, :], half_neg[:, :], ALU.pow)\
                        .then_inc(q["gn_pow_ready"], 1)

            def scatter(c, b):
                pool.wait_ge(q["slots_ready"], alone(pool, c + 1))
                for k in range(2):
                    pool.indirect_dma_start(
                        out=slot_table, out_offset=bass.IndirectOffsetOnAxis(ap=slot_i[:, k, b:b + 1], axis=0),
                        in_=token_i[:, k, b, :], in_offset=None).then_inc(q["scattered"], 16)

            pool.wait_ge(q["ve1_ready"], 1)
            rstd_of(0, q["rstd1_ready"])
            slot(0, 0, tail=False)
            for i in range(1, B + 1):
                slot(i, i % B)
            pool.wait_ge(q["zero_in"], 32)
            with pool.Fori(1, NCH // B - 1) as c:
                for u in range(1, B + 1):
                    slot(B * c + u, u % B, scatter_of=c - 1)
            for u in range(1, B + 1):
                slot(NCH - B + u, u % B, scatter_of=NCH // B - 2, head=u < B)
            for b in range(B):
                scatter(NCH // B - 1, b)

            def gather(t, u, turn):
                pool.wait_ge(id_in[u], alone(pool, 16 * turn + 16))
                if some(t - 3):
                    pool.wait_ge(q["t_x_ready"], alone(pool, t - 3))
                pool.indirect_dma_start(
                    out=tile_x[u % 4][:, :], out_offset=None, in_=xn2_rows,
                    in_offset=bass.IndirectOffsetOnAxis(ap=tile_id[u][:, 0:1], axis=0)).then_inc(row_in[u % 4], 16)

            def store(t, u):
                pool.wait_ge(q["t_y_taken"], alone(pool, t + 1))
                pool.wait_ge(q["dest_ready"], alone(pool, t + 1))
                pool.indirect_dma_start(
                    out=y_rows, out_offset=bass.IndirectOffsetOnAxis(ap=tile_dest[u][:, 0:1], axis=0),
                    in_=tile_y[u % 4][:, :], in_offset=None).then_inc(y_out[u % 4], 16)

            pool.wait_ge(q["tiles_ready"], 1)
            for t in range(8):
                gather(t, t, 0)
                if t >= 7:
                    store(t - 7, t - 7)
            with pool.Fori(1, NT // 8) as j:
                for u in range(8):
                    gather(8 * j + u, u, j)
                    store(8 * j + u - 7, (u + 1) % 8)
            for t in range(NT - 7, NT):
                store(t, t % 8)


_INS = ["L0_attn_x", "L0_attn_Wq", "L0_attn_bq", "L0_attn_Wk", "L0_attn_bk", "L0_attn_Wv", "L0_attn_bv", "L0_attn_Wg",
        "L0_attn_bg", "L0_attn_Wo", "L0_attn_bo", "L0_ffn_gate_w", "L0_ffn_gate_b", "L0_ffn_We1", "L0_ffn_be1",
        "L0_ffn_We2", "L0_ffn_be2", "L0_ffn_We3", "L0_ffn_be3", "L0_ffn_ws1", "L0_ffn_bs1", "L0_ffn_ws2",
        "L0_ffn_bs2", "L0_ffn_ws3", "L0_ffn_bs3"]


def kernel(**inputs):
    import numpy as _np
    import concourse.bacc as _bacc
    from concourse import mybir as _mybir
    from concourse.bass_utils import run_bass_kernel_spmd as _run

    nc = _bacc.Bacc("TRN2", target_bir_lowering=False, num_devices=1)
    arrays, args = {}, []

    def give(name, a):
        arrays[name] = a
        args.append(nc.dram_tensor(name, a.shape, _mybir.dt.from_np(a.dtype), kind="ExternalInput").ap())

    for name in _INS:
        give(f"in_{name}_dram", _np.ascontiguousarray(inputs[name]))
    for name, a in zip(("rotary", "floor", "const"), constants()):
        give(f"table_{name}_dram", a)
    out = nc.dram_tensor("out_0_dram", (B, S, D), F32, kind="ExternalOutput").ap()
    build(nc, *args, out)
    r = _run(nc, [arrays], core_ids=[0])
    return r.results[0]["out_0_dram"]
```
